# Optimizing a Trainium2 kernel written in Bass

```python
import numpy as np
import jax
import jax.numpy as jnp

def _softmax(x, axis=-1):
    return jax.nn.softmax(x, axis=axis)

def _gelu(x):
    return jax.nn.gelu(x, approximate=True)

def _silu(x):
    return jax.nn.silu(x)

def _sigmoid(x):
    return jax.nn.sigmoid(x)

def _layernorm(x, axis=-1, eps=1e-05):
    m = jnp.mean(x, axis=axis, keepdims=True)
    v = jnp.var(x, axis=axis, keepdims=True)
    return (x - m) / jnp.sqrt(v + eps)

def _scatter_add(tgt, idx, src, axis=0):
    return tgt.at[idx].add(src)

def _segment_sum(src, seg, n):
    return jax.ops.segment_sum(src, seg, n)
kernel_name = 'mk_decoder_preln_d4_seqx_r8_a1d446'

def setup_inputs(seed: int=0):
    np.random.seed(seed)
    _w = jnp.asarray

    def _rec_inputs():
        import jax
        import jax.numpy as jnp
        _rk = jax.random.key(seed)
        x = 7.22e-05 + 1 * jax.random.normal(jax.random.fold_in(_rk, 1), (8, 256, 128), jnp.float32)
        _lenS = 256 - jax.random.randint(jax.random.fold_in(_rk, 7), (8,), 0, max(1, 256 // 4) + 1, jnp.int32)
        _lenS2 = 256 - jax.random.randint(jax.random.fold_in(_rk, 8), (8,), 0, max(1, 256 // 4) + 1, jnp.int32)
        _ctx_1024P = jax.random.normal(jax.random.fold_in(_rk, 11), (8, 16, 128), jnp.float32)
        _ctx_1024c = jax.random.dirichlet(jax.random.fold_in(_rk, 511), 0.3 * jnp.ones((16,), jnp.float32), (8, 256))
        _ctx_1024t = jnp.einsum('bsk,bkd->bsd', _ctx_1024c, _ctx_1024P)
        _ctx_1024t = _ctx_1024t * jax.lax.rsqrt(jnp.mean(jnp.square(_ctx_1024t)) + 1e-12) * 0.953939
        ctx_1024 = 4.13588e-05 + 0.999923 * (_ctx_1024t + 0.3 * jax.random.normal(jax.random.fold_in(_rk, 611), (8, 256, 128), jnp.float32))
        _validS = jnp.arange(256)[None, :] < _lenS[:, None]
        _validS2 = jnp.arange(256)[None, :] < _lenS2[:, None]
        _causal = jnp.tril(jnp.ones((256, 256), dtype=bool))
        mask_BxS_ik0 = jnp.where(jnp.broadcast_to(_validS[:, :], (8, 256)), 0, 1).astype(jnp.int32)
        mask_Bx1xSxS2_ff0 = jnp.where(jnp.ones((8, 1, 256, 256), dtype=bool), 0.0, -1000000000.0).astype(jnp.float32)
        return (x, ctx_1024, mask_BxS_ik0, mask_Bx1xSxS2_ff0)
    x, ctx_1024, mask_BxS_ik0, mask_Bx1xSxS2_ff0 = _rec_inputs()

    def _L0_attn_setup():
        import jax, jax.numpy as jnp
        import numpy as np
        import math
        D_MODEL = 128
        N_HEADS = 16
        D_K = D_MODEL // N_HEADS
        D_FF = 512
        ROPE_THETA = 10000.0
        EPS = 1e-05

        def _rms_norm(x, w):
            rms = jnp.sqrt(EPS + jnp.mean(x * x, axis=-1, keepdims=True))
            return x / rms * w

        def _rope_tables(seq_len):
            pos = jnp.arange(seq_len, dtype=jnp.float32)
            k = jnp.arange(D_K) // 2
            angles = pos[:, None] / jnp.power(ROPE_THETA, 2.0 * k.astype(jnp.float32) / D_K)
            cos = jnp.cos(angles)
            sin = jnp.sin(angles)
            idx = jnp.arange(D_K)
            even = idx % 2 == 0
            sin = sin * jnp.where(even, -1.0, 1.0)
            pair_swaps = idx + jnp.where(even, 1, -1)
            return (cos, sin, pair_swaps)

        def _apply_rope(t, cos, sin, pair_swaps):
            return t * cos + t[..., pair_swaps] * sin
        key = jax.random.key(seed)
        ks = jax.random.split(key, 10)
        B, S = (4, 256)
        s = 0.02
        return {'x': jax.random.normal(ks[0], (B, S, D_MODEL), dtype=jnp.float32), 'wq': jax.random.normal(ks[1], (D_MODEL, D_MODEL), dtype=jnp.float32) * s, 'wk': jax.random.normal(ks[2], (D_MODEL, D_MODEL), dtype=jnp.float32) * s, 'wv': jax.random.normal(ks[3], (D_MODEL, D_MODEL), dtype=jnp.float32) * s, 'wo': jax.random.normal(ks[4], (D_MODEL, D_MODEL), dtype=jnp.float32) * s, 'norm1_w': jnp.ones((D_MODEL,), dtype=jnp.float32), 'norm2_w': jnp.ones((D_MODEL,), dtype=jnp.float32), 'w1': jax.random.normal(ks[5], (D_FF, D_MODEL), dtype=jnp.float32) * s, 'w2': jax.random.normal(ks[6], (D_MODEL, D_FF), dtype=jnp.float32) * s, 'w3': jax.random.normal(ks[7], (D_FF, D_MODEL), dtype=jnp.float32) * s}
    _L0_attn_all = _L0_attn_setup()
    _L0_attn_in = {k: v for k, v in _L0_attn_all.items() if k in ('wq', 'wk', 'wv', 'wo', 'norm1_w', 'norm2_w', 'w1', 'w2', 'w3')}
    del _L0_attn_all

    def _L0_xattn_setup():
        import jax, jax.numpy as jnp
        import numpy as np
        D_MODEL = 128
        N_HEAD = 16

        def _split_heads(x, n_head):
            B, S, D = x.shape
            return x.reshape(B, S, n_head, D // n_head).transpose(0, 2, 1, 3)
        key = jax.random.key(seed)
        ks = jax.random.split(key, 12)
        B, S, D = (4, 256, D_MODEL)
        scale = 1.0 / np.sqrt(D)
        inp = {'Q': jax.random.normal(ks[0], (B, S, D), jnp.float32), 'K': jax.random.normal(ks[1], (B, S, D), jnp.float32), 'V': jax.random.normal(ks[2], (B, S, D), jnp.float32), 'Wq': jax.random.normal(ks[3], (D, D), jnp.float32) * scale, 'bq': jax.random.normal(ks[4], (D,), jnp.float32) * scale, 'Wk': jax.random.normal(ks[5], (D, D), jnp.float32) * scale, 'bk': jax.random.normal(ks[6], (D,), jnp.float32) * scale, 'Wv': jax.random.normal(ks[7], (D, D), jnp.float32) * scale, 'bv': jax.random.normal(ks[8], (D,), jnp.float32) * scale, 'Wo': jax.random.normal(ks[9], (D, D), jnp.float32) * scale, 'bo': jax.random.normal(ks[10], (D,), jnp.float32) * scale}
        return inp
    _L0_xattn_all = _L0_xattn_setup()
    _L0_xattn_in = {k: v for k, v in _L0_xattn_all.items() if k in ('Wq', 'bq', 'Wk', 'bk', 'Wv', 'bv', 'Wo', 'bo')}
    del _L0_xattn_all

    def _L0_ffn_setup():
        import jax, jax.numpy as jnp
        import numpy as np
        B, T, D, E, FF, K = (4, 128, 128, 8, 256, 2)
        SINKHORN_ITERS = 3

        def _sinkhorn(log_alpha, iters=SINKHORN_ITERS):
            for _ in range(iters):
                log_alpha = log_alpha - jax.nn.logsumexp(log_alpha, axis=-1, keepdims=True)
                log_alpha = log_alpha - jax.nn.logsumexp(log_alpha, axis=-2, keepdims=True)
            gates = jnp.exp(log_alpha)
            return gates / (jnp.sum(gates, axis=-1, keepdims=True) + 1e-08)
        key = jax.random.key(seed)
        ks = jax.random.split(key, 7)
        scale = 0.02
        return {'x': jax.random.normal(ks[0], (B, T, D), dtype=jnp.float32), 'router_w': jax.random.normal(ks[1], (E, D), dtype=jnp.float32) * scale, 'router_b': jnp.zeros((E,), dtype=jnp.float32), 'temperature': jnp.ones((1,), dtype=jnp.float32) * 0.5, 'wg': jax.random.normal(ks[2], (E, D, FF), dtype=jnp.float32) * scale, 'wp': jax.random.normal(ks[3], (E, D, FF), dtype=jnp.float32) * scale, 'wo': jax.random.normal(ks[4], (E, FF, D), dtype=jnp.float32) * scale}
    _L0_ffn_all = _L0_ffn_setup()
    _L0_ffn_in = {k: v for k, v in _L0_ffn_all.items() if k in ('router_w', 'router_b', 'temperature', 'wg', 'wp', 'wo')}
    del _L0_ffn_all

    def _L1_attn_setup():
        import jax, jax.numpy as jnp
        import numpy as np
        B, N, C, H = (4, 512, 128, 16)
        EPS = 1e-06
        key = jax.random.key(seed)
        k1, k2, k3 = jax.random.split(key, 3)
        x = jax.random.normal(k1, (B, N, C), dtype=jnp.float32)
        qkv_w = jax.random.normal(k2, (3 * C, C), dtype=jnp.float32) * 0.02
        qkv_b = jnp.zeros((3 * C,), dtype=jnp.float32)
        proj_w = jax.random.normal(k3, (C, C), dtype=jnp.float32) * 0.02
        proj_b = jnp.zeros((C,), dtype=jnp.float32)
        return {'x': x, 'qkv_w': qkv_w, 'qkv_b': qkv_b, 'proj_w': proj_w, 'proj_b': proj_b}
    _L1_attn_all = _L1_attn_setup()
    _L1_attn_in = {k: v for k, v in _L1_attn_all.items() if k in ('qkv_w', 'qkv_b', 'proj_w', 'proj_b')}
    del _L1_attn_all

    def _L1_xattn_setup():
        import jax, jax.numpy as jnp
        import numpy as np
        B, S, P, D, H = (2, 512, 128, 128, 16)
        key = jax.random.key(seed)
        ks = jax.random.split(key, 8)
        init = 0.02
        queries = jax.random.normal(ks[0], (B, S, D), dtype=jnp.float32)
        patch_representations = jax.random.normal(ks[1], (B, P, D), dtype=jnp.float32)
        patch_boundaries = jax.random.randint(ks[2], (B, S), 0, 2, dtype=jnp.int32)
        wq = jax.random.normal(ks[3], (D, D), dtype=jnp.float32) * init
        wk = jax.random.normal(ks[4], (D, D), dtype=jnp.float32) * init
        wv = jax.random.normal(ks[5], (D, D), dtype=jnp.float32) * init
        wo = jax.random.normal(ks[6], (D, D), dtype=jnp.float32) * init
        bq = jnp.zeros((D,), jnp.float32)
        bk = jnp.zeros((D,), jnp.float32)
        bv = jnp.zeros((D,), jnp.float32)
        bo = jnp.zeros((D,), jnp.float32)
        return {'queries': queries, 'patch_representations': patch_representations, 'patch_boundaries': patch_boundaries, 'wq': wq, 'wk': wk, 'wv': wv, 'wo': wo, 'bq': bq, 'bk': bk, 'bv': bv, 'bo': bo}
    _L1_xattn_all = _L1_xattn_setup()
    _L1_xattn_in = {k: v for k, v in _L1_xattn_all.items() if k in ('wq', 'wk', 'wv', 'wo', 'bq', 'bk', 'bv', 'bo')}
    del _L1_xattn_all

    def _L1_ffn_setup():
        import jax, jax.numpy as jnp
        import numpy as np
        HIDDEN = 128
        INNER = 512

        def _weight_quant(w):
            scale = 1.0 / jnp.clip(jnp.mean(jnp.abs(w)), 1e-05)
            wq = jnp.clip(jnp.round(w * scale), -1.0, 1.0) / scale
            return w + jax.lax.stop_gradient(wq - w)

        def _act_quant(x):
            scale = 127.0 / jnp.clip(jnp.max(jnp.abs(x), axis=-1, keepdims=True), 1e-05)
            xq = jnp.clip(jnp.round(x * scale), -128.0, 127.0) / scale
            return x + jax.lax.stop_gradient(xq - x)

        def _bitlinear(x, w):
            return jnp.einsum('bsi,oi->bso', _act_quant(x), _weight_quant(w))
        key = jax.random.key(seed)
        k0, k1, k2, k3 = jax.random.split(key, 4)
        x = jax.random.normal(k0, (4, 256, HIDDEN), dtype=jnp.float32)
        w_gate = jax.random.normal(k1, (INNER, HIDDEN), dtype=jnp.float32) / np.sqrt(HIDDEN)
        w_up = jax.random.normal(k2, (INNER, HIDDEN), dtype=jnp.float32) / np.sqrt(HIDDEN)
        w_down = jax.random.normal(k3, (HIDDEN, INNER), dtype=jnp.float32) / np.sqrt(INNER)
        return {'x': x, 'w_gate': w_gate, 'w_up': w_up, 'w_down': w_down}
    _L1_ffn_all = _L1_ffn_setup()
    _L1_ffn_in = {k: v for k, v in _L1_ffn_all.items() if k in ('w_gate', 'w_up', 'w_down')}
    del _L1_ffn_all

    def _L2_attn_setup():
        import jax, jax.numpy as jnp
        import numpy as np
        DIM = 128
        NUM_HEAD = 16
        DIM_HEAD = DIM // NUM_HEAD
        RMS_EPS = 1.1920929e-07
        EPS_LIN = 1e-06
        THETA = 10000.0

        def rmsnorm(x, g, eps=RMS_EPS):
            return x * jax.lax.rsqrt(jnp.mean(x * x, axis=-1, keepdims=True) + eps) * g

        def rope_cos_sin(seq_len, dim_head, dtype=jnp.float32):
            inv_freq = 1.0 / THETA ** (jnp.arange(0, dim_head, 2, dtype=dtype) / dim_head)
            t = jnp.arange(seq_len, dtype=dtype)
            freqs = jnp.outer(t, inv_freq)
            return (jnp.cos(freqs), jnp.sin(freqs))

        def apply_rope(t, cos, sin):
            tr = t[..., 0::2]
            ti = t[..., 1::2]
            out_r = tr * cos - ti * sin
            out_i = tr * sin + ti * cos
            return jnp.stack([out_r, out_i], axis=-1).reshape(t.shape)
        key = jax.random.key(seed)
        ks = jax.random.split(key, 5)
        B, L = (4, 512)
        x = jax.random.normal(ks[0], (B, L, DIM), dtype=jnp.float32)
        Wqkv = jax.random.normal(ks[1], (3 * DIM, DIM), dtype=jnp.float32) * 0.02
        bqkv = jax.random.normal(ks[2], (3 * DIM,), dtype=jnp.float32) * 0.02
        gq = jnp.ones((DIM,), dtype=jnp.float32)
        gk = jnp.ones((DIM,), dtype=jnp.float32)
        Wout = jax.random.normal(ks[3], (DIM, DIM), dtype=jnp.float32) * 0.02
        bout = jax.random.normal(ks[4], (DIM,), dtype=jnp.float32) * 0.02
        gout = jnp.ones((DIM,), dtype=jnp.float32)
        return {'x': x, 'Wqkv': Wqkv, 'bqkv': bqkv, 'gq': gq, 'gk': gk, 'Wout': Wout, 'bout': bout, 'gout': gout}
    _L2_attn_all = _L2_attn_setup()
    _L2_attn_in = {k: v for k, v in _L2_attn_all.items() if k in ('Wqkv', 'bqkv', 'gq', 'gk', 'Wout', 'bout', 'gout')}
    del _L2_attn_all

    def _L2_xattn_setup():
        import jax, jax.numpy as jnp
        import numpy as np
        BS, LX, LY, D, H, DK = (2, 256, 256, 128, 16, 64)
        key = jax.random.key(seed)
        ks = jax.random.split(key, 12)
        s = 1.0 / np.sqrt(D)
        return {'x': jax.random.normal(ks[0], (BS, LX, D), jnp.float32), 'y': jax.random.normal(ks[1], (BS, LY, D), jnp.float32), 'mask': jnp.zeros((BS, 1, LX, LY), jnp.float32), 'Wq': jax.random.normal(ks[2], (D, H * DK), jnp.float32) * s, 'bq': jnp.zeros((H * DK,), jnp.float32), 'Wk': jax.random.normal(ks[3], (D, H * DK), jnp.float32) * s, 'bk': jnp.zeros((H * DK,), jnp.float32), 'Wv': jax.random.normal(ks[4], (D, H * DK), jnp.float32) * s, 'bv': jnp.zeros((H * DK,), jnp.float32), 'Wo': jax.random.normal(ks[5], (H * DK, D), jnp.float32) * s, 'bo': jnp.zeros((D,), jnp.float32)}
    _L2_xattn_all = _L2_xattn_setup()
    _L2_xattn_in = {k: v for k, v in _L2_xattn_all.items() if k in ('Wq', 'bq', 'Wk', 'bk', 'Wv', 'bv', 'Wo', 'bo')}
    del _L2_xattn_all

    def _L2_ffn_setup():
        import jax, jax.numpy as jnp
        import numpy as np
        B, S, H = (2, 128, 128)
        DFF = 256
        E = 8
        TOPK = 2

        def _expert_ffn(x, w1, b1, w2, b2, wg, bg, w3, b3):
            x1 = jnp.einsum('bsh,hf->bsf', x, w1) + b1
            x2 = jnp.einsum('bsh,hf->bsf', x, w2) + b2
            z = x1 * x2
            s = jax.nn.silu(jnp.einsum('bsf,fg->bsg', z, wg) + bg)
            return jnp.einsum('bsg,gh->bsh', s, w3) + b3
        key = jax.random.key(seed)
        ks = jax.random.split(key, 12)
        sc = 0.02
        return {'x': jax.random.normal(ks[0], (B, S, H), jnp.float32), 'gate_w': jax.random.normal(ks[1], (H, E), jnp.float32) * sc, 'gate_b': jnp.zeros((E,), jnp.float32), 'w1': jax.random.normal(ks[2], (E, H, DFF), jnp.float32) * sc, 'b1': jnp.zeros((E, DFF), jnp.float32), 'w2': jax.random.normal(ks[3], (E, H, DFF), jnp.float32) * sc, 'b2': jnp.zeros((E, DFF), jnp.float32), 'wg': jax.random.normal(ks[4], (E, DFF, DFF), jnp.float32) * sc, 'bg': jnp.zeros((E, DFF), jnp.float32), 'w3': jax.random.normal(ks[5], (E, DFF, H), jnp.float32) * sc, 'b3': jnp.zeros((E, H), jnp.float32)}
    _L2_ffn_all = _L2_ffn_setup()
    _L2_ffn_in = {k: v for k, v in _L2_ffn_all.items() if k in ('gate_w', 'gate_b', 'w1', 'b1', 'w2', 'b2', 'wg', 'bg', 'w3', 'b3')}
    del _L2_ffn_all

    def _L3_attn_setup():
        import jax, jax.numpy as jnp
        import numpy as np
        B, N, C, H, BS = (4, 512, 128, 16, 64)
        E = C // H
        EPS = 0.001
        key = jax.random.key(seed)
        k0, k1, k2, k3 = jax.random.split(key, 4)
        x = jax.random.normal(k0, (B, N, C), jnp.float32)
        qkv_w = jax.random.normal(k1, (3 * C, C), jnp.float32) * 0.02
        proj_w = jax.random.normal(k2, (C, C), jnp.float32) * 0.02
        proj_b = jax.random.normal(k3, (C,), jnp.float32) * 0.02
        return {'x': x, 'qkv_w': qkv_w, 'proj_w': proj_w, 'proj_b': proj_b}
    _L3_attn_all = _L3_attn_setup()
    _L3_attn_in = {k: v for k, v in _L3_attn_all.items() if k in ('qkv_w', 'proj_w', 'proj_b')}
    del _L3_attn_all

    def _L3_xattn_setup():
        import jax, jax.numpy as jnp
        import numpy as np
        EMBED_DIM = 128
        NUM_HEADS = 16
        HEAD_DIM = EMBED_DIM // NUM_HEADS

        def _split_heads(x, B, S):
            return x.reshape(B, S, NUM_HEADS, HEAD_DIM).transpose(0, 2, 1, 3)
        key = jax.random.key(seed)
        ks = jax.random.split(key, 11)
        B, S, D = (2, 256, EMBED_DIM)
        scale = 1.0 / np.sqrt(D)
        inp = {'query': jax.random.normal(ks[0], (B, S, D), jnp.float32), 'key': jax.random.normal(ks[1], (B, S, D), jnp.float32), 'value': jax.random.normal(ks[2], (B, S, D), jnp.float32), 'Wq': jax.random.normal(ks[3], (D, D), jnp.float32) * scale, 'bq': jnp.zeros((D,), jnp.float32), 'Wk': jax.random.normal(ks[4], (D, D), jnp.float32) * scale, 'bk': jnp.zeros((D,), jnp.float32), 'Wv': jax.random.normal(ks[5], (D, D), jnp.float32) * scale, 'bv': jnp.zeros((D,), jnp.float32), 'Wo': jax.random.normal(ks[6], (D, D), jnp.float32) * scale, 'bo': jnp.zeros((D,), jnp.float32)}
        return inp
    _L3_xattn_all = _L3_xattn_setup()
    _L3_xattn_in = {k: v for k, v in _L3_xattn_all.items() if k in ('Wq', 'bq', 'Wk', 'bk', 'Wv', 'bv', 'Wo', 'bo')}
    del _L3_xattn_all

    def _L3_ffn_setup():
        import jax, jax.numpy as jnp
        import numpy as np
        EPS = 1e-08

        def _ste(x, q):
            return x + jax.lax.stop_gradient(q - x)

        def quant_act_uint8(x):
            s = jax.lax.stop_gradient(jnp.maximum(jnp.max(x), EPS)) / 255.0
            q = jnp.clip(jnp.round(x / s), 0.0, 255.0) * s
            return (_ste(x, q), s)

        def quant_weight_int8_perchannel(w):
            s = jax.lax.stop_gradient(jnp.maximum(jnp.max(jnp.abs(w), axis=1, keepdims=True), EPS)) / 127.0
            q = jnp.clip(jnp.round(w / s), -128.0, 127.0) * s
            return (_ste(w, q), s[:, 0])

        def quant_bias_int32(b, s_in, s_w):
            s = jax.lax.stop_gradient(s_in * s_w)
            q = jnp.round(b / s) * s
            return _ste(b, q)

        def quant_linear(x, w, b):
            xq, s_in = quant_act_uint8(x)
            wq, s_w = quant_weight_int8_perchannel(w)
            bq = quant_bias_int32(b, s_in, s_w)
            return jnp.einsum('btd,fd->btf', xq, wq) + bq
        key = jax.random.key(seed)
        k1, k2, k3, k4, k5 = jax.random.split(key, 5)
        B, S, D, F = (4, 256, 128, 512)
        return {'x': jax.random.normal(k1, (B, S, D), dtype=jnp.float32), 'w1': jax.random.normal(k2, (F, D), dtype=jnp.float32) * (1.0 / np.sqrt(D)), 'b1': jax.random.normal(k3, (F,), dtype=jnp.float32) * 0.01, 'w2': jax.random.normal(k4, (D, F), dtype=jnp.float32) * (1.0 / np.sqrt(F)), 'b2': jax.random.normal(k5, (D,), dtype=jnp.float32) * 0.01}
    _L3_ffn_all = _L3_ffn_setup()
    _L3_ffn_in = {k: v for k, v in _L3_ffn_all.items() if k in ('w1', 'b1', 'w2', 'b2')}
    del _L3_ffn_all
    return {'x': x, 'ctx_1024': ctx_1024, 'mask_BxS_ik0': mask_BxS_ik0, 'mask_Bx1xSxS2_ff0': mask_Bx1xSxS2_ff0, 'L0_attn_wq': _L0_attn_in['wq'], 'L0_attn_wk': _L0_attn_in['wk'], 'L0_attn_wv': _L0_attn_in['wv'], 'L0_attn_wo': _L0_attn_in['wo'], 'L0_attn_norm1_w': _L0_attn_in['norm1_w'], 'L0_attn_norm2_w': _L0_attn_in['norm2_w'], 'L0_attn_w1': _L0_attn_in['w1'], 'L0_attn_w2': _L0_attn_in['w2'], 'L0_attn_w3': _L0_attn_in['w3'], 'L0_xattn_Wq': _L0_xattn_in['Wq'], 'L0_xattn_bq': _L0_xattn_in['bq'], 'L0_xattn_Wk': _L0_xattn_in['Wk'], 'L0_xattn_bk': _L0_xattn_in['bk'], 'L0_xattn_Wv': _L0_xattn_in['Wv'], 'L0_xattn_bv': _L0_xattn_in['bv'], 'L0_xattn_Wo': _L0_xattn_in['Wo'], 'L0_xattn_bo': _L0_xattn_in['bo'], 'L0_ffn_router_w': _L0_ffn_in['router_w'], 'L0_ffn_router_b': _L0_ffn_in['router_b'], 'L0_ffn_temperature': _L0_ffn_in['temperature'], 'L0_ffn_wg': _L0_ffn_in['wg'], 'L0_ffn_wp': _L0_ffn_in['wp'], 'L0_ffn_wo': _L0_ffn_in['wo'], 'L1_attn_qkv_w': _L1_attn_in['qkv_w'], 'L1_attn_qkv_b': _L1_attn_in['qkv_b'], 'L1_attn_proj_w': _L1_attn_in['proj_w'], 'L1_attn_proj_b': _L1_attn_in['proj_b'], 'L1_xattn_wq': _L1_xattn_in['wq'], 'L1_xattn_wk': _L1_xattn_in['wk'], 'L1_xattn_wv': _L1_xattn_in['wv'], 'L1_xattn_wo': _L1_xattn_in['wo'], 'L1_xattn_bq': _L1_xattn_in['bq'], 'L1_xattn_bk': _L1_xattn_in['bk'], 'L1_xattn_bv': _L1_xattn_in['bv'], 'L1_xattn_bo': _L1_xattn_in['bo'], 'L1_ffn_w_gate': _L1_ffn_in['w_gate'], 'L1_ffn_w_up': _L1_ffn_in['w_up'], 'L1_ffn_w_down': _L1_ffn_in['w_down'], 'L2_attn_Wqkv': _L2_attn_in['Wqkv'], 'L2_attn_bqkv': _L2_attn_in['bqkv'], 'L2_attn_gq': _L2_attn_in['gq'], 'L2_attn_gk': _L2_attn_in['gk'], 'L2_attn_Wout': _L2_attn_in['Wout'], 'L2_attn_bout': _L2_attn_in['bout'], 'L2_attn_gout': _L2_attn_in['gout'], 'L2_xattn_Wq': _L2_xattn_in['Wq'], 'L2_xattn_bq': _L2_xattn_in['bq'], 'L2_xattn_Wk': _L2_xattn_in['Wk'], 'L2_xattn_bk': _L2_xattn_in['bk'], 'L2_xattn_Wv': _L2_xattn_in['Wv'], 'L2_xattn_bv': _L2_xattn_in['bv'], 'L2_xattn_Wo': _L2_xattn_in['Wo'], 'L2_xattn_bo': _L2_xattn_in['bo'], 'L2_ffn_gate_w': _L2_ffn_in['gate_w'], 'L2_ffn_gate_b': _L2_ffn_in['gate_b'], 'L2_ffn_w1': _L2_ffn_in['w1'], 'L2_ffn_b1': _L2_ffn_in['b1'], 'L2_ffn_w2': _L2_ffn_in['w2'], 'L2_ffn_b2': _L2_ffn_in['b2'], 'L2_ffn_wg': _L2_ffn_in['wg'], 'L2_ffn_bg': _L2_ffn_in['bg'], 'L2_ffn_w3': _L2_ffn_in['w3'], 'L2_ffn_b3': _L2_ffn_in['b3'], 'L3_attn_qkv_w': _L3_attn_in['qkv_w'], 'L3_attn_proj_w': _L3_attn_in['proj_w'], 'L3_attn_proj_b': _L3_attn_in['proj_b'], 'L3_xattn_Wq': _L3_xattn_in['Wq'], 'L3_xattn_bq': _L3_xattn_in['bq'], 'L3_xattn_Wk': _L3_xattn_in['Wk'], 'L3_xattn_bk': _L3_xattn_in['bk'], 'L3_xattn_Wv': _L3_xattn_in['Wv'], 'L3_xattn_bv': _L3_xattn_in['bv'], 'L3_xattn_Wo': _L3_xattn_in['Wo'], 'L3_xattn_bo': _L3_xattn_in['bo'], 'L3_ffn_w1': _L3_ffn_in['w1'], 'L3_ffn_b1': _L3_ffn_in['b1'], 'L3_ffn_w2': _L3_ffn_in['w2'], 'L3_ffn_b2': _L3_ffn_in['b2']}

def reference(x, ctx_1024, mask_BxS_ik0, mask_Bx1xSxS2_ff0, L0_attn_wq, L0_attn_wk, L0_attn_wv, L0_attn_wo, L0_attn_norm1_w, L0_attn_norm2_w, L0_attn_w1, L0_attn_w2, L0_attn_w3, L0_xattn_Wq, L0_xattn_bq, L0_xattn_Wk, L0_xattn_bk, L0_xattn_Wv, L0_xattn_bv, L0_xattn_Wo, L0_xattn_bo, L0_ffn_router_w, L0_ffn_router_b, L0_ffn_temperature, L0_ffn_wg, L0_ffn_wp, L0_ffn_wo, L1_attn_qkv_w, L1_attn_qkv_b, L1_attn_proj_w, L1_attn_proj_b, L1_xattn_wq, L1_xattn_wk, L1_xattn_wv, L1_xattn_wo, L1_xattn_bq, L1_xattn_bk, L1_xattn_bv, L1_xattn_bo, L1_ffn_w_gate, L1_ffn_w_up, L1_ffn_w_down, L2_attn_Wqkv, L2_attn_bqkv, L2_attn_gq, L2_attn_gk, L2_attn_Wout, L2_attn_bout, L2_attn_gout, L2_xattn_Wq, L2_xattn_bq, L2_xattn_Wk, L2_xattn_bk, L2_xattn_Wv, L2_xattn_bv, L2_xattn_Wo, L2_xattn_bo, L2_ffn_gate_w, L2_ffn_gate_b, L2_ffn_w1, L2_ffn_b1, L2_ffn_w2, L2_ffn_b2, L2_ffn_wg, L2_ffn_bg, L2_ffn_w3, L2_ffn_b3, L3_attn_qkv_w, L3_attn_proj_w, L3_attn_proj_b, L3_xattn_Wq, L3_xattn_bq, L3_xattn_Wk, L3_xattn_bk, L3_xattn_Wv, L3_xattn_bv, L3_xattn_Wo, L3_xattn_bo, L3_ffn_w1, L3_ffn_b1, L3_ffn_w2, L3_ffn_b2):
    import jax
    import jax.numpy as jnp

    def _L0_attn_ref(x, wq, wk, wv, wo, norm1_w, norm2_w, w1, w2, w3):
        import jax, jax.numpy as jnp
        import numpy as np
        import math
        D_MODEL = 128
        N_HEADS = 16
        D_K = D_MODEL // N_HEADS
        D_FF = 512
        ROPE_THETA = 10000.0
        EPS = 1e-05

        def _rms_norm(x, w):
            rms = jnp.sqrt(EPS + jnp.mean(x * x, axis=-1, keepdims=True))
            return x / rms * w

        def _rope_tables(seq_len):
            pos = jnp.arange(seq_len, dtype=jnp.float32)
            k = jnp.arange(D_K) // 2
            angles = pos[:, None] / jnp.power(ROPE_THETA, 2.0 * k.astype(jnp.float32) / D_K)
            cos = jnp.cos(angles)
            sin = jnp.sin(angles)
            idx = jnp.arange(D_K)
            even = idx % 2 == 0
            sin = sin * jnp.where(even, -1.0, 1.0)
            pair_swaps = idx + jnp.where(even, 1, -1)
            return (cos, sin, pair_swaps)

        def _apply_rope(t, cos, sin, pair_swaps):
            return t * cos + t[..., pair_swaps] * sin
        B, S, _ = x.shape
        h = _rms_norm(x, norm1_w)
        q = h @ wq.T
        k = h @ wk.T
        v = h @ wv.T

        def split_heads(t):
            return t.reshape(B, S, N_HEADS, D_K).transpose(0, 2, 1, 3)
        q, k, v = (split_heads(q), split_heads(k), split_heads(v))
        cos, sin, pair_swaps = _rope_tables(S)
        q = _apply_rope(q, cos, sin, pair_swaps)
        k = _apply_rope(k, cos, sin, pair_swaps)
        scores = jnp.einsum('bhqd,bhkd->bhqk', q, k) / math.sqrt(D_K)
        causal = jnp.tril(jnp.ones((S, S), dtype=bool))
        scores = jnp.where(causal, scores, -jnp.inf)
        probs = jax.nn.softmax(scores, axis=-1)
        ctx = jnp.einsum('bhqk,bhkd->bhqd', probs, v)
        ctx = ctx.transpose(0, 2, 1, 3).reshape(B, S, D_MODEL)
        attn_out = ctx @ wo.T
        y = x + attn_out
        h2 = _rms_norm(y, norm2_w)
        p1 = h2 @ w1.T
        p1 = p1 * jax.nn.sigmoid(p1)
        ff = p1 * (h2 @ w3.T) @ w2.T
        return y + ff

    def _L0_xattn_ref(Q, K, V, Wq, bq, Wk, bk, Wv, bv, Wo, bo):
        import jax, jax.numpy as jnp
        import numpy as np
        D_MODEL = 128
        N_HEAD = 16

        def _split_heads(x, n_head):
            B, S, D = x.shape
            return x.reshape(B, S, n_head, D // n_head).transpose(0, 2, 1, 3)
        q = _split_heads(Q @ Wq.T + bq, N_HEAD)
        k = _split_heads(K @ Wk.T + bk, N_HEAD)
        v = _split_heads(V @ Wv.T + bv, N_HEAD)
        d_k = k.shape[-1]
        score = jnp.einsum('bhqd,bhkd->bhqk', q, k) / jnp.sqrt(jnp.float32(d_k))
        attn = jax.nn.softmax(score, axis=-1)
        out = jnp.einsum('bhqk,bhkd->bhqd', attn, v)
        B, H, S, dh = out.shape
        out = out.transpose(0, 2, 1, 3).reshape(B, S, H * dh)
        return out @ Wo.T + bo

    def _L0_ffn_ref(x, router_w, router_b, temperature, wg, wp, wo):
        import jax, jax.numpy as jnp
        import numpy as np
        B, T, D, E, FF, K = (4, 128, 128, 8, 256, 2)
        SINKHORN_ITERS = 3

        def _sinkhorn(log_alpha, iters=SINKHORN_ITERS):
            for _ in range(iters):
                log_alpha = log_alpha - jax.nn.logsumexp(log_alpha, axis=-1, keepdims=True)
                log_alpha = log_alpha - jax.nn.logsumexp(log_alpha, axis=-2, keepdims=True)
            gates = jnp.exp(log_alpha)
            return gates / (jnp.sum(gates, axis=-1, keepdims=True) + 1e-08)
        temp = jnp.maximum(temperature, 0.1)
        scores = (jnp.einsum('btd,ed->bte', x, router_w) + router_b) / temp
        gates = _sinkhorn(scores)
        topk_vals, topk_idx = jax.lax.top_k(gates, K)
        topk_gates = topk_vals / (jnp.sum(topk_vals, axis=-1, keepdims=True) + 1e-08)
        g = jax.nn.relu(jnp.einsum('btd,edf->btef', x, wg))
        p = jnp.einsum('btd,edf->btef', x, wp)
        all_out = jnp.einsum('btef,efd->bted', g * p, wo)
        gathered = jnp.take_along_axis(all_out, topk_idx[..., None], axis=2)
        expert_out = jnp.sum(gathered * topk_gates[..., None], axis=2)
        return x + expert_out

    def _L1_attn_ref(x, qkv_w, qkv_b, proj_w, proj_b):
        import jax, jax.numpy as jnp
        import numpy as np
        B, N, C, H = (4, 512, 128, 16)
        EPS = 1e-06
        b, n, c = x.shape
        d = c // H
        qkv = x @ qkv_w.T + qkv_b
        qkv = qkv.reshape(b, n, 3, H, d).transpose(2, 0, 3, 1, 4)
        q, k, v = (qkv[0], qkv[1], qkv[2])
        q = jax.nn.sigmoid(q)
        k = jax.nn.sigmoid(k)
        k_sum = k.sum(axis=2)
        sink_incoming = 1.0 / jnp.sum((q + EPS) * (k_sum[:, :, None, :] + EPS), axis=-1)
        q_sum = q.sum(axis=2)
        source_outgoing = 1.0 / jnp.sum((k + EPS) * (q_sum[:, :, None, :] + EPS), axis=-1)
        k_so_sum = (k * source_outgoing[..., None]).sum(axis=2, keepdims=True)
        conserved_sink = jnp.sum((q + EPS) * (k_so_sum + EPS), axis=-1) + EPS
        q_si_sum = (q * sink_incoming[..., None]).sum(axis=2, keepdims=True)
        conserved_source = jnp.sum((k + EPS) * (q_si_sum + EPS), axis=-1) + EPS
        conserved_source = jnp.clip(conserved_source, -1.0, 1.0)
        ratio = float(n) / float(n)
        sink_allocation = jax.nn.sigmoid(conserved_sink * ratio)
        source_competition = jax.nn.softmax(conserved_source, axis=-1) * float(n)
        q_norm = q * sink_incoming[..., None]
        v_comp = v * source_competition[..., None]
        kv = jnp.einsum('bhnd,bhnm->bhdm', k, v_comp)
        out = jnp.einsum('bhnd,bhdm->bhnm', q_norm, kv)
        out = out * sink_allocation[..., None]
        out = out.transpose(0, 2, 1, 3).reshape(b, n, c)
        out = out @ proj_w.T + proj_b
        return out

    def _L1_xattn_ref(queries, patch_representations, patch_boundaries, wq, wk, wv, wo, bq, bk, bv, bo):
        import jax, jax.numpy as jnp
        import numpy as np
        B, S, P, D, H = (2, 512, 128, 128, 16)
        b, s, d = queries.shape
        p = patch_representations.shape[1]
        h = H
        dh = d // h
        scale = 1.0 / jnp.sqrt(jnp.asarray(dh, queries.dtype))
        q = (queries @ wq.T + bq).reshape(b, s, h, dh)
        k = (patch_representations @ wk.T + bk).reshape(b, p, h, dh)
        v = (patch_representations @ wv.T + bv).reshape(b, p, h, dh)
        scores = jnp.einsum('bqhd,bkhd->bhqk', q, k) * scale
        patch_idx = jnp.cumsum(patch_boundaries, axis=1)
        mask = jnp.arange(p)[None, None, :] > patch_idx[:, :, None]
        scores = jnp.where(mask[:, None, :, :], jnp.finfo(scores.dtype).min, scores)
        attn = jax.nn.softmax(scores, axis=-1)
        out = jnp.einsum('bhqk,bkhd->bqhd', attn, v).reshape(b, s, d)
        return out @ wo.T + bo

    def _L1_ffn_ref(x, w_gate, w_up, w_down):
        import jax, jax.numpy as jnp
        import numpy as np
        HIDDEN = 128
        INNER = 512

        def _weight_quant(w):
            scale = 1.0 / jnp.clip(jnp.mean(jnp.abs(w)), 1e-05)
            wq = jnp.clip(jnp.round(w * scale), -1.0, 1.0) / scale
            return w + jax.lax.stop_gradient(wq - w)

        def _act_quant(x):
            scale = 127.0 / jnp.clip(jnp.max(jnp.abs(x), axis=-1, keepdims=True), 1e-05)
            xq = jnp.clip(jnp.round(x * scale), -128.0, 127.0) / scale
            return x + jax.lax.stop_gradient(xq - x)

        def _bitlinear(x, w):
            return jnp.einsum('bsi,oi->bso', _act_quant(x), _weight_quant(w))
        gate = jax.nn.silu(_bitlinear(x, w_gate))
        up = _bitlinear(x, w_up)
        return _bitlinear(gate * up, w_down)

    def _L2_attn_ref(x, Wqkv, bqkv, gq, gk, Wout, bout, gout):
        import jax, jax.numpy as jnp
        import numpy as np
        DIM = 128
        NUM_HEAD = 16
        DIM_HEAD = DIM // NUM_HEAD
        RMS_EPS = 1.1920929e-07
        EPS_LIN = 1e-06
        THETA = 10000.0

        def rmsnorm(x, g, eps=RMS_EPS):
            return x * jax.lax.rsqrt(jnp.mean(x * x, axis=-1, keepdims=True) + eps) * g

        def rope_cos_sin(seq_len, dim_head, dtype=jnp.float32):
            inv_freq = 1.0 / THETA ** (jnp.arange(0, dim_head, 2, dtype=dtype) / dim_head)
            t = jnp.arange(seq_len, dtype=dtype)
            freqs = jnp.outer(t, inv_freq)
            return (jnp.cos(freqs), jnp.sin(freqs))

        def apply_rope(t, cos, sin):
            tr = t[..., 0::2]
            ti = t[..., 1::2]
            out_r = tr * cos - ti * sin
            out_i = tr * sin + ti * cos
            return jnp.stack([out_r, out_i], axis=-1).reshape(t.shape)
        B, L, D = x.shape
        qkv = x @ Wqkv.T + bqkv
        q, k, v = jnp.split(qkv, 3, axis=-1)
        q = rmsnorm(q, gq)
        k = rmsnorm(k, gk)
        split = lambda t: t.reshape(B, L, NUM_HEAD, DIM_HEAD).transpose(0, 2, 1, 3)
        q, k, v = (split(q), split(k), split(v))
        cos, sin = rope_cos_sin(L, DIM_HEAD)
        cos = cos[None, None]
        sin = sin[None, None]
        q = apply_rope(q, cos, sin)
        k = apply_rope(k, cos, sin)
        qf = jax.nn.relu(q)
        kf = jax.nn.relu(k)
        vpad = jnp.concatenate([v, jnp.ones_like(v[..., :1])], axis=-1)
        vk = jnp.einsum('bhlp,bhld->bhpd', vpad, kf)
        res = jnp.einsum('bhpd,bhld->bhlp', vk, qf)
        attn = res[..., :-1] / (res[..., -1:] + EPS_LIN)
        attn = attn.transpose(0, 2, 1, 3).reshape(B, L, D)
        out = rmsnorm(attn @ Wout.T + bout, gout)
        return out

    def _L2_xattn_ref(x, y, mask, Wq, bq, Wk, bk, Wv, bv, Wo, bo):
        import jax, jax.numpy as jnp
        import numpy as np
        BS, LX, LY, D, H, DK = (2, 256, 256, 128, 16, 64)
        bs, lx, _ = x.shape
        ly = y.shape[1]
        norm = DK ** 0.5
        q = (x @ Wq + bq).reshape(bs, lx, H, DK)
        k = (y @ Wk + bk).reshape(bs, ly, H, DK)
        v = (y @ Wv + bv).reshape(bs, ly, H, DK)
        scores = jnp.einsum('bxhd,byhd->bhxy', q, k) / norm + mask
        attn = jax.nn.softmax(scores, axis=-1)
        out = jnp.einsum('bhxy,byhd->bxhd', attn, v).reshape(bs, lx, H * DK)
        return out @ Wo + bo

    def _L2_ffn_ref(x, gate_w, gate_b, w1, b1, w2, b2, wg, bg, w3, b3):
        import jax, jax.numpy as jnp
        import numpy as np
        B, S, H = (2, 128, 128)
        DFF = 256
        E = 8
        TOPK = 2

        def _expert_ffn(x, w1, b1, w2, b2, wg, bg, w3, b3):
            x1 = jnp.einsum('bsh,hf->bsf', x, w1) + b1
            x2 = jnp.einsum('bsh,hf->bsf', x, w2) + b2
            z = x1 * x2
            s = jax.nn.silu(jnp.einsum('bsf,fg->bsg', z, wg) + bg)
            return jnp.einsum('bsg,gh->bsh', s, w3) + b3
        logits = jnp.einsum('bsh,he->bse', x, gate_w) + gate_b
        topv, topi = jax.lax.top_k(logits, TOPK)
        probs = jax.nn.softmax(topv, axis=-1)
        out = jnp.zeros_like(x)
        for e in range(E):
            we = jnp.sum(probs * (topi == e), axis=-1)
            y = _expert_ffn(x, w1[e], b1[e], w2[e], b2[e], wg[e], bg[e], w3[e], b3[e])
            out = out + we[..., None] * y
        return out

    def _L3_attn_ref(x, qkv_w, proj_w, proj_b):
        import jax, jax.numpy as jnp
        import numpy as np
        B, N, C, H, BS = (4, 512, 128, 16, 64)
        E = C // H
        EPS = 0.001
        b, n, c = x.shape
        h, e, bs = (H, E, BS)
        u = n // bs
        qkv = (x @ qkv_w.T).reshape(b, n, 3, h, e).transpose(2, 0, 3, 1, 4)
        q, k, v = (qkv[0], qkv[1], qkv[2])
        q = jax.nn.softmax(q, axis=-1) * e ** (-0.5)
        k = jnp.exp(k)
        b_q = q.reshape(b, h, u, bs, e)
        b_k = k.reshape(b, h, u, bs, e)
        b_v = v.reshape(b, h, u, bs, e)
        b_k_cumsum = jnp.cumsum(b_k.sum(axis=-2), axis=-2)
        context = jnp.einsum('bhund,bhune->bhude', b_k, b_v)
        context = jnp.cumsum(context, axis=2)
        context = jnp.concatenate([jnp.zeros_like(context[:, :, :1]), context[:, :, :-1]], axis=2)
        b_k_cumsum = jnp.concatenate([jnp.zeros_like(b_k_cumsum[:, :, :1]), b_k_cumsum[:, :, :-1]], axis=2)
        D_inv = 1.0 / jnp.maximum(jnp.einsum('bhud,bhund->bhun', b_k_cumsum, b_q), EPS)
        attn = jnp.einsum('bhund,bhude,bhun->bhune', b_q, context, D_inv)
        out = attn.reshape(b, h, n, e).transpose(0, 2, 1, 3).reshape(b, n, c)
        return out @ proj_w.T + proj_b

    def _L3_xattn_ref(query, key, value, Wq, bq, Wk, bk, Wv, bv, Wo, bo):
        import jax, jax.numpy as jnp
        import numpy as np
        EMBED_DIM = 128
        NUM_HEADS = 16
        HEAD_DIM = EMBED_DIM // NUM_HEADS

        def _split_heads(x, B, S):
            return x.reshape(B, S, NUM_HEADS, HEAD_DIM).transpose(0, 2, 1, 3)
        B, S, D = query.shape
        q = _split_heads(query @ Wq + bq, B, S)
        k = _split_heads(key @ Wk + bk, B, S)
        v = _split_heads(value @ Wv + bv, B, S)
        score = jnp.einsum('bhqd,bhkd->bhqk', q, k) / np.sqrt(HEAD_DIM)
        weights = jax.nn.softmax(score, axis=-1)
        attn = jnp.einsum('bhqk,bhkd->bhqd', weights, v)
        out = attn.transpose(0, 2, 1, 3).reshape(B, S, D)
        return out @ Wo + bo

    def _L3_ffn_ref(x, w1, b1, w2, b2):
        import jax, jax.numpy as jnp
        import numpy as np
        EPS = 1e-08

        def _ste(x, q):
            return x + jax.lax.stop_gradient(q - x)

        def quant_act_uint8(x):
            s = jax.lax.stop_gradient(jnp.maximum(jnp.max(x), EPS)) / 255.0
            q = jnp.clip(jnp.round(x / s), 0.0, 255.0) * s
            return (_ste(x, q), s)

        def quant_weight_int8_perchannel(w):
            s = jax.lax.stop_gradient(jnp.maximum(jnp.max(jnp.abs(w), axis=1, keepdims=True), EPS)) / 127.0
            q = jnp.clip(jnp.round(w / s), -128.0, 127.0) * s
            return (_ste(w, q), s[:, 0])

        def quant_bias_int32(b, s_in, s_w):
            s = jax.lax.stop_gradient(s_in * s_w)
            q = jnp.round(b / s) * s
            return _ste(b, q)

        def quant_linear(x, w, b):
            xq, s_in = quant_act_uint8(x)
            wq, s_w = quant_weight_int8_perchannel(w)
            bq = quant_bias_int32(b, s_in, s_w)
            return jnp.einsum('btd,fd->btf', xq, wq) + bq
        h = jax.nn.relu(quant_linear(x, w1, b1))
        return quant_linear(h, w2, b2)
    x = x + _L0_attn_ref(_layernorm(x, axis=-1), L0_attn_wq, L0_attn_wk, L0_attn_wv, L0_attn_wo, L0_attn_norm1_w, L0_attn_norm2_w, L0_attn_w1, L0_attn_w2, L0_attn_w3)
    x = x + _L0_xattn_ref(_layernorm(x, axis=-1), ctx_1024, ctx_1024, L0_xattn_Wq, L0_xattn_bq, L0_xattn_Wk, L0_xattn_bk, L0_xattn_Wv, L0_xattn_bv, L0_xattn_Wo, L0_xattn_bo)
    x = x + _L0_ffn_ref(_layernorm(x, axis=-1), L0_ffn_router_w, L0_ffn_router_b, L0_ffn_temperature, L0_ffn_wg, L0_ffn_wp, L0_ffn_wo)
    x = x + _L1_attn_ref(_layernorm(x, axis=-1), L1_attn_qkv_w, L1_attn_qkv_b, L1_attn_proj_w, L1_attn_proj_b)
    x = x + _L1_xattn_ref(_layernorm(x, axis=-1), ctx_1024, mask_BxS_ik0, L1_xattn_wq, L1_xattn_wk, L1_xattn_wv, L1_xattn_wo, L1_xattn_bq, L1_xattn_bk, L1_xattn_bv, L1_xattn_bo)
    x = x + _L1_ffn_ref(_layernorm(x, axis=-1), L1_ffn_w_gate, L1_ffn_w_up, L1_ffn_w_down)
    x = x + _L2_attn_ref(_layernorm(x, axis=-1), L2_attn_Wqkv, L2_attn_bqkv, L2_attn_gq, L2_attn_gk, L2_attn_Wout, L2_attn_bout, L2_attn_gout)
    x = x + _L2_xattn_ref(_layernorm(x, axis=-1), ctx_1024, mask_Bx1xSxS2_ff0, L2_xattn_Wq, L2_xattn_bq, L2_xattn_Wk, L2_xattn_bk, L2_xattn_Wv, L2_xattn_bv, L2_xattn_Wo, L2_xattn_bo)
    x = x + _L2_ffn_ref(_layernorm(x, axis=-1), L2_ffn_gate_w, L2_ffn_gate_b, L2_ffn_w1, L2_ffn_b1, L2_ffn_w2, L2_ffn_b2, L2_ffn_wg, L2_ffn_bg, L2_ffn_w3, L2_ffn_b3)
    x = x + _L3_attn_ref(_layernorm(x, axis=-1), L3_attn_qkv_w, L3_attn_proj_w, L3_attn_proj_b)
    x = x + _L3_xattn_ref(_layernorm(x, axis=-1), ctx_1024, ctx_1024, L3_xattn_Wq, L3_xattn_bq, L3_xattn_Wk, L3_xattn_bk, L3_xattn_Wv, L3_xattn_bv, L3_xattn_Wo, L3_xattn_bo)
    x = x + _L3_ffn_ref(_layernorm(x, axis=-1), L3_ffn_w1, L3_ffn_b1, L3_ffn_w2, L3_ffn_b2)
    return x

_drawn_inputs = setup_inputs


def setup_inputs(seed=0):
    import zlib

    import numpy as np

    out = dict(_drawn_inputs(seed))
    spreads = {'L0_attn_norm1_w': (1.0, 0.6),
     'L0_attn_norm2_w': (1.0, 0.6),
     'L0_ffn_router_b': (0.0, 0.8),
     'L1_attn_qkv_b': (0.0, 0.8),
     'L1_attn_proj_b': (0.0, 0.289),
     'L1_xattn_bq': (0.0, 2.0),
     'L1_xattn_bk': (0.0, 2.0),
     'L1_xattn_bv': (0.0, 0.8),
     'L1_xattn_bo': (0.0, 0.36),
     'L2_attn_gq': (1.0, 0.6),
     'L2_attn_gk': (1.0, 0.6),
     'L2_attn_gout': (1.0, 0.2),
     'L2_xattn_bq': (0.0, 0.441),
     'L2_xattn_bk': (0.0, 2.0),
     'L2_xattn_bv': (0.0, 0.1),
     'L2_xattn_bo': (0.0, 0.273),
     'L2_ffn_gate_b': (0.0, 0.545),
     'L2_ffn_b1': (0.0, 0.8),
     'L2_ffn_b2': (0.0, 0.8),
     'L2_ffn_bg': (0.0, 0.8),
     'L2_ffn_b3': (0.0, 2.0),
     'L3_xattn_bq': (0.0, 2.0),
     'L3_xattn_bk': (0.0, 2.0),
     'L3_xattn_bv': (0.0, 2.0),
     'L3_xattn_bo': (0.0, 1.801)}
    factors = {'L0_attn_wq': 8.0,
     'L0_attn_wk': 8.0,
     'L0_attn_wv': 8.0,
     'L0_attn_wo': 8.0,
     'L0_attn_w1': 8.0,
     'L0_attn_w2': 8.0,
     'L0_attn_w3': 8.0,
     'L0_xattn_bq': 5.346,
     'L0_xattn_bk': 64.0,
     'L0_ffn_router_w': 8.0,
     'L0_ffn_wg': 8.0,
     'L0_ffn_wp': 8.0,
     'L0_ffn_wo': 8.0,
     'L1_attn_qkv_w': 8.0,
     'L1_attn_proj_w': 8.0,
     'L1_xattn_wq': 26.128,
     'L1_xattn_wk': 25.171,
     'L1_xattn_wv': 3.684,
     'L1_xattn_wo': 3.396,
     'L2_ffn_gate_w': 3.806,
     'L2_ffn_w1': 8.0,
     'L2_ffn_w2': 8.0,
     'L2_ffn_wg': 8.0,
     'L2_ffn_w3': 8.0,
     'L3_attn_qkv_w': 8.0,
     'L3_attn_proj_w': 8.0,
     'L3_attn_proj_b': 63.294,
     'L3_ffn_b1': 64.0,
     'L3_ffn_b2': 64.0,
     'L3_xattn_Wq': 5.711,
     'L3_xattn_Wk': 4.726,
     'L3_ffn_w1': 3.157,
     'L3_ffn_w2': 2.722}
    for name, (base, spread) in spreads.items():
        noise = np.random.default_rng([zlib.crc32(name.encode()), seed]).standard_normal(out[name].shape)
        drawn = base * np.exp(spread * noise) if base else spread * noise
        out[name] = jnp.asarray(drawn.astype(out[name].dtype))
    for name, factor in factors.items():
        out[name] = (out[name] * factor).astype(out[name].dtype)
    return out
```

```python
from contextlib import ExitStack, contextmanager

import numpy as np

import concourse.bass as bass
from concourse import mybir

P = 128
SEQS, SEQ, D = 8, 256, 128
TILES = SEQS * SEQ // P
PT = 4
PAIR = PT * P
PAIRS = TILES // PT
HEADS, HD = 16, 8
GROUPS = 4
AUG = 8
NEG = -1.0e30
LN_EPS = 1e-5

ALU = mybir.AluOpType
ACT = mybir.ActivationFunctionType
AX = mybir.AxisListType
F32 = mybir.dt.float32
BF16 = mybir.dt.bfloat16
I32 = mybir.dt.int32

SUBLAYERS = ["L0_attn", "L0_xattn", "L0_ffn", "L1_attn", "L1_xattn", "L1_ffn",
             "L2_attn", "L2_xattn", "L2_ffn", "L3_attn", "L3_xattn", "L3_ffn"]


class Link:

    def __init__(self, eng, sem):
        self.eng, self.sem, self.n = eng, sem, 0

    def tick(self, ins):
        self.n += 1
        ins.then_inc(self.sem, 1)

    def settle(self):
        self.eng.wait_ge(self.sem, self.n)

    def __call__(self, ins):
        self.tick(ins)
        self.settle()


class Core:

    def __init__(self, nc, ctx, layout, ks):
        self.nc, self.layout, self.ks = nc, layout, ks
        sb = lambda name, shape, dt=F32: ctx.enter_context(nc.sbuf_tensor(name, shape, dt))
        self.x = sb("x", [P, TILES * D])
        self.ctxT = sb("ctxT", [P, TILES * P])
        self.const = sb("const", [P, layout["const"]["_width"]])
        self.identb = sb("identb", [P, P], BF16)
        widths = [[layout[SUBLAYERS[k]]["_width"] for k in ks[r::2]] or [1] for r in range(2)]
        self.regions = [sb(f"weights_{r}", [P, max(widths[r])]) for r in range(2)]
        self.stats = sb("stats", [P, PT, 6])
        self.mv = sb("mv", [P, PT, 2])
        self.rstd = sb("rstd", [P, PT])
        self.nwt = [sb("newton_a", [P, 64]), sb("newton_v", [P, 64])]
        self.ps = ctx.enter_context(nc.psum_tensor("ps", [P, 8, 512], F32))
        self.loaded = ctx.enter_context(nc.semaphore("loaded"))
        self.stored = ctx.enter_context(nc.semaphore("stored"))
        self.weights_loaded = [ctx.enter_context(nc.semaphore(f"weights_loaded_{n}")) for n in SUBLAYERS]
        self.sems, self.ctx = {}, ctx
        self.ident = self.c("ident")

    def c(self, name):
        o, n = self.layout["const"][name]
        return self.const[:, o:o + n]

    def sem(self, name):
        if name not in self.sems:
            self.sems[name] = self.ctx.enter_context(self.nc.semaphore(name))
        return self.sems[name]

    def region(self, k):
        return self.regions[self.ks.index(k) % 2]

    def weights(self, k):
        region, lay = self.region(k), self.layout[SUBLAYERS[k]]
        return lambda name: region[:, lay[name][0]:lay[name][0] + lay[name][1]]

    def xt(self, i, t, n=1):
        return self.x[:, bass.ds(i * PAIR + t * D, n * D)]

    @contextmanager
    def turn(self):
        with self.nc.Block() as block:
            yield block
        nums = [s.num for s in self.sems.values()]
        if nums:
            self.nc.sync.sem_clear(range(min(nums), max(nums) + 1))
            self.nc.all_engine_barrier()


def bcast(ap, axis, shape):
    return ap.unsqueeze(axis).to_broadcast(shape)


def load_weights(C, eng, k, packed):
    w = C.layout[SUBLAYERS[k]]["_width"]
    h = w // 2
    for a, b in ((0, h), (h, w)):
        eng.dma_start(C.region(k)[:, a:b], packed[SUBLAYERS[k]][:, a:b]).then_inc(C.weights_loaded[k], 16)


def start_sublayer(C, k, ks, packed, setup=None):
    nc = C.nc
    with C.turn() as block:
        @block.sync
        def _(sp):
            at = ks.index(k)
            if at + 1 < len(ks):
                load_weights(C, sp, ks[at + 1], packed)

        @block.vector
        def _(v):
            v.wait_ge(C.weights_loaded[k], 32)
            if setup:
                setup(v, Link(v, C.sem("vector_step")))


def rsqrt(v, L, C, out, var, eps):
    n = out.shape[1]
    a, vv = C.nwt[0][:, 0:n], C.nwt[1][:, 0:n]
    L(v.tensor_scalar(vv, var, eps, None, ALU.add))
    L(v.tensor_scalar(out.bitcast(I32), vv.bitcast(I32), -0.5, 1597463007.0, ALU.mult, ALU.add))
    for _ in range(4):
        L(v.scalar_tensor_tensor(a, out, -0.5, out, ALU.mult, ALU.mult))
        L(v.tensor_tensor(a, a, vv, ALU.mult))
        L(v.scalar_tensor_tensor(out, a, 1.5, out, ALU.add, ALU.mult))


def moments(v, L, C, tiles):
    for t, ap in enumerate(tiles):
        L.tick(v.bn_stats(C.stats[:, t, :], ap))
    L.settle()
    for t in range(len(tiles)):
        L.tick(v.bn_aggr(C.mv[:, t, :], C.stats[:, t, :]))
    L.settle()


def norm_pair(v, L, C, i, xn, ready):
    moments(v, L, C, [C.xt(i, t) for t in range(PT)])
    rsqrt(v, L, C, C.rstd[:, :], C.mv[:, :, 1], LN_EPS)
    for t in range(PT):
        v.tensor_scalar(xn[:, t, :], C.xt(i, t), C.mv[:, t, 0:1], C.rstd[:, t:t + 1],
                        ALU.subtract, ALU.mult).then_inc(ready, 1)


def turn_tiles(pe, C, bank, src, ready, done):
    for t in range(PT):
        pe.wait_ge(ready, t + 1)
        ins = pe.transpose(C.ps[:, bank, t * P:(t + 1) * P], src[:, t, :], C.ident)
    ins.then_inc(done, 1)


def attend8(C, k, ks, packed, *, cross, rope=False, causal=False, boundary=None, inner=None):
    nc, w = C.nc, C.weights(k)
    with ExitStack() as ctx:
        sb = lambda name, shape, dt=F32: ctx.enter_context(nc.sbuf_tensor(f"{SUBLAYERS[k]}_{name}", shape, dt))
        xn = sb("xn", [P, PT, D])
        hn = sb("hn", [P, PT, D]) if rope else xn
        hT = sb("hT", [P, PAIR])
        kvT = sb("kvT", [P, PAIR]) if cross else hT
        q = sb("q", [P, GROUPS, PAIR])
        kk = sb("k", [P, GROUPS, PAIR])
        V = sb("v", [P, PT, HEADS, HD + 1])
        maxs = sb("maxs", [P, 2, 2, GROUPS, P])
        probs = sb("probs", [P, 2, 4, 2, SEQ])
        sums = sb("sums", [P, 2, HEADS])
        att = sb("att", [P, 2, HEADS, HD])
        attT = sb("attT", [P, 2 * P])
        rotc = sb("rotc", [P, 2, PAIR]) if rope else None
        rots = sb("rots", [P, 2, PAIR]) if rope else None
        maskT = None
        if causal:
            maskT = sb("maskT", [P, 1, P], BF16)
        if boundary is not None:
            maskT = sb("maskT", [P, 4, SEQ], BF16)
            bnd = sb("bnd", [P, PAIR], I32)
            bndf = sb("bndf", [P, PAIR])
            idx = sb("idx", [P, PAIR])
        ps = C.ps

        def setup(v, L):
            L(v.memset(V[:, :, :, HD:HD + 1], 1.0))
            L(v.memset(maxs[:], 0.0))
            if causal:
                L(v.tensor_copy(maskT[:, 0, :], C.c("causalT")))

        start_sublayer(C, k, ks, packed, setup)
        slots = [(s // GROUPS, s % GROUPS) for s in range(2 * GROUPS)]
        S = C.sem
        with nc.Fori(0, PAIRS) as i, C.turn() as block:

            @block.sync
            def _(sp):
                if boundary is not None:
                    sp.dma_start(bnd[:, :], boundary[0:1, bass.ds(i * PAIR, PAIR)].to_broadcast([P, PAIR]))\
                      .then_inc(S("boundary_loaded"), 16)

            @block.gpsimd
            def _(g):
                if cross:
                    g.tensor_copy(kvT[:, :], C.ctxT[:, bass.ds(i * PAIR, PAIR)]).then_inc(S("context_ready"), 1)

            @block.vector
            def _(v):
                L = Link(v, S("vector_step"))
                if rope:
                    moments(v, L, C, [C.xt(i, t) for t in range(PT)])
                    rsqrt(v, L, C, C.rstd[:, :], C.mv[:, :, 1], LN_EPS)
                    for t in range(PT):
                        L.tick(v.tensor_scalar(xn[:, t, :], C.xt(i, t), C.mv[:, t, 0:1], C.rstd[:, t:t + 1],
                                               ALU.subtract, ALU.mult))
                    L.settle()
                    moments(v, L, C, [xn[:, t, :] for t in range(PT)])
                    L(v.tensor_tensor(C.mv[:, :, 0], C.mv[:, :, 0], C.mv[:, :, 0], ALU.mult))
                    L(v.tensor_tensor(C.mv[:, :, 1], C.mv[:, :, 1], C.mv[:, :, 0], ALU.add))
                    rsqrt(v, L, C, C.rstd[:, :], C.mv[:, :, 1], 1e-5)
                    for t in range(PT):
                        v.tensor_scalar(hn[:, t, :], xn[:, t, :], C.rstd[:, t:t + 1], None, ALU.mult)\
                         .then_inc(S("xn_ready"), 1)
                else:
                    norm_pair(v, L, C, i, xn, S("xn_ready"))
                if boundary is not None:
                    v.wait_ge(S("boundary_loaded"), 16)
                    L(v.tensor_copy(bndf[:, :], bnd[:, :]))
                    for b in range(2):
                        cols = slice(b * SEQ, (b + 1) * SEQ)
                        L.tick(v.tensor_tensor_scan(idx[:, cols], bndf[:, cols], C.c("zeros"), 0.0, ALU.add, ALU.add))
                    L.settle()
                    for b in range(2):
                        for kt in range(2):
                            ins = v.tensor_scalar(maskT[:, 2 * b + kt, :], idx[:, b * SEQ:(b + 1) * SEQ],
                                                  C.c("position")[:, kt:kt + 1], NEG, ALU.is_lt, ALU.mult)
                    ins.then_inc(S("mask_ready"), 1)
                if rope:
                    for n in range(2 * GROUPS):
                        dst, g = (q, kk)[n // GROUPS], n % GROUPS
                        v.wait_ge(S("proj_ready"), n + 1)
                        b0 = 2 + 2 * (n % 2)
                        L.tick(v.tensor_tensor(rotc[:, n % 2, :], ps[:, b0, :], C.c("cosF"), ALU.mult))
                        L.tick(v.tensor_tensor(rots[:, n % 2, :], ps[:, b0 + 1, :], C.c("sinF"), ALU.mult))
                        L.settle()
                        aug = C.c("aug") if dst is kk else 0.0
                        v.scalar_tensor_tensor(dst[:, g, :], rotc[:, n % 2, :], aug, rots[:, n % 2, :],
                                               ALU.add, ALU.add).then_inc(S("qk_ready"), 1)
                else:
                    for g in range(GROUPS):
                        v.wait_ge(S("k_proj"), g + 1)
                        v.tensor_scalar(kk[:, g, :], ps[:, 4 + g, :], w("bk")[:, g:g + 1], None, ALU.add)\
                         .then_inc(S("k_ready"), 1)
                v.wait_ge(S("v_proj"), 1)
                src = ps[:, 0, :].rearrange("p (t h d) -> p t h d", t=PT, d=HD)
                if rope:
                    v.tensor_copy(V[:, :, :, 0:HD], src).then_inc(S("v_ready"), 1)
                else:
                    bv = w("bv").rearrange("p (h d) -> p h d", d=HD)
                    v.tensor_tensor(V[:, :, :, 0:HD], src, bcast(bv, 1, [P, PT, HEADS, HD]), ALU.add)\
                     .then_inc(S("v_ready"), 1)

                def add_max(s):
                    b, g = slots[s]
                    v.wait_ge(S("maxT_ready"), s + 1)
                    cols = slice(b * SEQ, (b + 1) * SEQ)
                    v.tensor_tensor(q[:, g, cols], q[:, g, cols], ps[:, 6 + g % 2, SEQ:2 * SEQ], ALU.add)\
                     .then_inc(S("max_in_q"), 1)

                def normalise(b):
                    v.wait_ge(S("pv_ready"), GROUPS * (b + 1))
                    src = ps[:, 4:6, SEQ:SEQ + HEADS * (HD + 1)].rearrange("p t (h e) -> p t h e", e=HD + 1)
                    L(v.reciprocal(sums[:, :, :], src[:, :, :, HD]))
                    v.tensor_tensor(att[:, :, :, :], src[:, :, :, 0:HD],
                                    bcast(sums[:, :, :], 3, [P, 2, HEADS, HD]), ALU.mult)\
                     .then_inc(S("att_ready"), 1)

                def residual(b):
                    v.wait_ge(S("out_ready"), b + 1)
                    o = ps[:, 7, 0:2 * P]
                    xs = C.xt(i, 2 * b, 2)
                    if inner is not None:
                        y = inner[:, bass.ds(i * PAIR + 2 * b * D, 2 * D)]
                        L(v.tensor_tensor(y, xn[:, 2 * b:2 * b + 2, :].rearrange("p t d -> p (t d)"), o, ALU.add))
                        L(v.tensor_tensor(xs, xs, y, ALU.add))
                    else:
                        bo = bcast(w("bo"), 1, [P, 2, D])
                        tmp = att[:, :, :, :].rearrange("p t h d -> p t (h d)")
                        L(v.tensor_tensor(tmp, o.rearrange("p (t d) -> p t d", t=2), bo, ALU.add))
                        L(v.tensor_tensor(xs, xs, tmp.rearrange("p t d -> p (t d)"), ALU.add))

                for s in range(len(slots) + 1):
                    if s >= 1:
                        add_max(s - 1)
                    if s == GROUPS + 2:
                        normalise(0)
                    if s < len(slots):
                        b, g = slots[s]
                        for qt in range(2):
                            v.wait_ge(S("m_ready"), 2 * s + qt + 1)
                            nk = P if causal and qt == 0 else SEQ
                            out = maxs[:, b, qt, g, :].rearrange("p (j r) -> p j r", r=32)[:, :, AUG]
                            v.tensor_reduce(out, ps[:, 4:8, 0:nk], AX.X, ALU.max, negate=True)\
                             .then_inc(S("m_used"), 1)
                residual(0)
                normalise(1)
                residual(1)

            @block.scalar
            def _(a):
                a.wait_ge(S("hT_ps"), 1)
                if rope:
                    a.activation(hT[:, :], ps[:, 0, :], ACT.Copy, scale=w("norm1")).then_inc(S("hT_ready"), 1)
                else:
                    a.activation(hT[:, :], ps[:, 0, :], ACT.Copy).then_inc(S("hT_ready"), 1)
                    for g in range(GROUPS):
                        a.wait_ge(S("q_proj"), g + 1)
                        a.activation(q[:, g, :], ps[:, g, :], ACT.Identity, bias=w("bq")[:, g:g + 1])\
                         .then_inc(S("q_ready"), 1)

                def exps(s):
                    a.wait_ge(S("p_ready"), s + 1)
                    if s >= 2:
                        a.wait_ge(S("pv_ready"), s - 1)
                    if causal:
                        a.activation(probs[:, s % 2, :, 0, :], ps[:, 0:4, 0:SEQ], ACT.Exp, scale=HD ** -0.5)
                        a.activation(probs[:, s % 2, :, 1, P:SEQ], ps[:, 0:4, SEQ + P:2 * SEQ], ACT.Exp,
                                     scale=HD ** -0.5).then_inc(S("probs_ready"), 1)
                    else:
                        a.activation(probs[:, s % 2, :, :, :].rearrange("p j t n -> p j (t n)"),
                                     ps[:, 0:4, :], ACT.Exp, scale=HD ** -0.5).then_inc(S("probs_ready"), 1)

                def turned_att(b):
                    a.wait_ge(S("attT_ps"), b + 1)
                    if b == 1:
                        a.wait_ge(S("out_ready"), 1)
                    a.activation(attT[:, :], ps[:, 6, 0:2 * P], ACT.Copy).then_inc(S("attT_ready"), 1)

                for s in range(len(slots)):
                    exps(s)
                turned_att(0)
                turned_att(1)

            @block.tensor
            def _(pe):
                turn_tiles(pe, C, 0, hn, S("xn_ready"), S("hT_ps"))
                pe.wait_ge(S("hT_ready"), 1)
                if rope:
                    for n in range(2 * GROUPS):
                        ab, g = ("wq", "wk")[n // GROUPS], n % GROUPS
                        if n >= 2:
                            pe.wait_ge(S("qk_ready"), n - 1)
                        b0 = 2 + 2 * (n % 2)
                        pe.matmul(ps[:, b0, :], w(ab)[:, g * P:(g + 1) * P], hT[:, :], start=True, stop=True)
                        pe.matmul(ps[:, b0 + 1, :], w(ab + "_swapped")[:, g * P:(g + 1) * P], hT[:, :],
                                  start=True, stop=True).then_inc(S("proj_ready"), 1)
                else:
                    for g in range(GROUPS):
                        pe.matmul(ps[:, g, :], w("wq")[:, g * P:(g + 1) * P], hT[:, :], start=True, stop=True)\
                          .then_inc(S("q_proj"), 1)
                    pe.wait_ge(S("context_ready"), 1)
                    for g in range(GROUPS):
                        pe.matmul(ps[:, 4 + g, :], w("wk")[:, g * P:(g + 1) * P], kvT[:, :], start=True, stop=True)\
                          .then_inc(S("k_proj"), 1)
                    pe.wait_ge(S("q_ready"), 1)
                for t in range(PT):
                    mm = pe.matmul(ps[:, 0, t * P:(t + 1) * P], kvT[:, t * P:(t + 1) * P], w("wv"),
                                   start=True, stop=True)
                mm.then_inc(S("v_proj"), 1)
                if rope:
                    pe.wait_ge(S("qk_ready"), 2 * GROUPS)
                else:
                    pe.wait_ge(S("q_ready"), GROUPS)
                    pe.wait_ge(S("k_ready"), GROUPS)
                if boundary is not None:
                    pe.wait_ge(S("mask_ready"), 1)

                def max_scores(s, qt):
                    b, g = slots[s]
                    if qt:
                        pe.wait_ge(S("m_used"), 2 * s + 1)
                    elif s:
                        pe.wait_ge(S("max_in_q"), s)
                    if qt == 0 and s == GROUPS + 2:
                        pe.wait_ge(S("att_ready"), 1)
                    nk = P if causal and qt == 0 else SEQ
                    q0 = b * SEQ + qt * P
                    masked = boundary is not None or causal
                    if masked:
                        for j in range(4):
                            if causal:
                                pe.matmul(ps[:, 4 + j, nk - P:nk], maskT[:, 0, :], C.identb[:, :], start=True, stop=False,
                                          skip_group_check=True)
                            else:
                                for kt in range(2):
                                    pe.matmul(ps[:, 4 + j, kt * P:(kt + 1) * P],
                                              maskT[:, 2 * b + kt, qt * P:(qt + 1) * P], C.identb[:, :],
                                              start=kt == 0, stop=False, skip_group_check=True)
                    for j in range(4):
                        r = slice(32 * j, 32 * j + 32)
                        parts = [(0, nk)] if not (causal and qt) else [(0, P), (P, SEQ)]
                        for c0, c1 in parts:
                            mm = pe.matmul(ps[:, 4 + j, c0:c1], q[r, g, q0:q0 + P],
                                           kk[r, g, b * SEQ + c0:b * SEQ + c1], start=not masked, stop=True,
                                           skip_group_check=masked)
                    mm.then_inc(S("m_ready"), 1)

                def turn_max(s):
                    b, g = slots[s]
                    pe.wait_ge(S("m_used"), 2 * s + 2)
                    if s >= 2:
                        pe.wait_ge(S("max_in_q"), s - 1)
                    for qt in range(2):
                        mm = pe.transpose(ps[:, 6 + g % 2, SEQ + qt * P:SEQ + (qt + 1) * P], maxs[:, b, qt, g, :], C.ident)
                    mm.then_inc(S("maxT_ready"), 1)

                def prob_scores(s):
                    b, g = slots[s]
                    pe.wait_ge(S("max_in_q"), s + 1)
                    if s >= 1:
                        pe.wait_ge(S("probs_ready"), s)
                    masked = boundary is not None or causal
                    for kt in range(2):
                        k0 = b * SEQ + kt * P
                        if masked:
                            for j in range(4):
                                if causal:
                                    pe.matmul(ps[:, j, kt * (SEQ + P):kt * (SEQ + P) + P], C.identb[:, :], maskT[:, 0, :],
                                              start=kt == 0, stop=False, skip_group_check=True)
                                else:
                                    pe.matmul(ps[:, j, kt * SEQ:(kt + 1) * SEQ], C.identb[:, :], maskT[:, 2 * b + kt, :],
                                              start=kt == 0, stop=False, skip_group_check=True)
                        for j in range(4):
                            r = slice(32 * j, 32 * j + 32)
                            parts = [(0, SEQ)] if not causal else ([(0, P), (P, SEQ)] if kt == 0 else [(P, SEQ)])
                            for c0, c1 in parts:
                                mm = pe.matmul(ps[:, j, kt * SEQ + c0:kt * SEQ + c1], kk[r, g, k0:k0 + P],
                                               q[r, g, b * SEQ + c0:b * SEQ + c1],
                                               start=(not masked), stop=True, skip_group_check=True)
                    mm.then_inc(S("p_ready"), 1)

                def weigh_values(s):
                    b, g = slots[s]
                    pe.wait_ge(S("probs_ready"), s + 1)
                    if s == 0:
                        pe.wait_ge(S("v_ready"), 1)
                    for qt in range(2):
                        for j in range(4):
                            h = 4 * g + j
                            kts = range(1 if causal and qt == 0 else 2)
                            for kt in kts:
                                mm = pe.matmul(ps[:, 4 + qt, SEQ + h * (HD + 1):SEQ + (h + 1) * (HD + 1)],
                                               probs[:, s % 2, j, kt, qt * P:(qt + 1) * P], V[:, 2 * b + kt, h, :],
                                               start=kt == 0, stop=kt == kts[-1], skip_group_check=True)
                    mm.then_inc(S("pv_ready"), 1)

                def turn_att(b):
                    pe.wait_ge(S("att_ready"), b + 1)
                    for t in range(2):
                        mm = pe.transpose(ps[:, 6, t * P:(t + 1) * P],
                                          att[:, t, :, :].rearrange("p h d -> p (h d)"), C.ident)
                    mm.then_inc(S("attT_ps"), 1)

                def project_out(b):
                    pe.wait_ge(S("attT_ready"), b + 1)
                    for t in range(2):
                        mm = pe.matmul(ps[:, 7, t * P:(t + 1) * P], attT[:, t * P:(t + 1) * P], w("wo"),
                                       start=True, stop=True)
                    mm.then_inc(S("out_ready"), 1)

                n = len(slots)
                pe.wait_ge(S("v_ready"), 1)
                for s in range(n + 3):
                    if 2 <= s < n + 2:
                        prob_scores(s - 2)
                    if 1 <= s <= n:
                        turn_max(s - 1)
                    if s >= 3:
                        weigh_values(s - 3)
                    if s < n:
                        max_scores(s, 0)
                        max_scores(s, 1)
                turn_att(0)
                project_out(0)
                turn_att(1)
                project_out(1)


def swiglu(C, k, y):
    nc, w, S, ps = C.nc, C.weights(k), C.sem, C.ps
    FT = 4
    with ExitStack() as ctx:
        sb = lambda name, shape, dt=F32: ctx.enter_context(nc.sbuf_tensor(f"swiglu_{name}", shape, dt))
        hn = sb("hn", [P, PT, D])
        hT = sb("hT", [P, PAIR])
        gate = sb("gate", [P, 2, PAIR])
        gated = sb("gated", [P, FT, PAIR])
        with nc.Fori(0, PAIRS) as i, C.turn() as block:

            @block.vector
            def _(v):
                L = Link(v, S("vector_step"))
                yt = [y[:, bass.ds(i * PAIR + t * D, D)] for t in range(PT)]
                moments(v, L, C, yt)
                L(v.tensor_tensor(C.mv[:, :, 0], C.mv[:, :, 0], C.mv[:, :, 0], ALU.mult))
                L(v.tensor_tensor(C.mv[:, :, 1], C.mv[:, :, 1], C.mv[:, :, 0], ALU.add))
                rsqrt(v, L, C, C.rstd[:, :], C.mv[:, :, 1], 1e-5)
                for t in range(PT):
                    v.tensor_scalar(hn[:, t, :], yt[t], C.rstd[:, t:t + 1], None, ALU.mult).then_inc(S("xn_ready"), 1)
                for m in range(FT):
                    v.wait_ge(S("gate_ready"), m + 1)
                    v.tensor_tensor(gated[:, m, :], gate[:, m % 2, :], ps[:, 3 + m % 2, :], ALU.mult)\
                     .then_inc(S("gated_ready"), 1)
                v.wait_ge(S("down_ready"), 1)
                L(v.tensor_tensor(C.xt(i, 0, PT), C.xt(i, 0, PT), ps[:, 5, :], ALU.add))

            @block.scalar
            def _(a):
                a.wait_ge(S("hT_ps"), 1)
                a.activation(hT[:, :], ps[:, 0, :], ACT.Copy, scale=w("norm2")).then_inc(S("hT_ready"), 1)
                for m in range(FT):
                    a.wait_ge(S("up_ready"), m + 1)
                    if m >= 2:
                        a.wait_ge(S("gated_ready"), m - 1)
                    a.activation(gate[:, m % 2, :], ps[:, 1 + m % 2, :], ACT.Silu).then_inc(S("gate_ready"), 1)

            @block.tensor
            def _(pe):
                turn_tiles(pe, C, 0, hn, S("xn_ready"), S("hT_ps"))
                pe.wait_ge(S("hT_ready"), 1)
                for m in range(FT):
                    if m >= 2:
                        pe.wait_ge(S("gated_ready"), m - 1)
                    pe.matmul(ps[:, 1 + m % 2, :], w("w1")[:, m * P:(m + 1) * P], hT[:, :], start=True, stop=True)
                    pe.matmul(ps[:, 3 + m % 2, :], w("w3")[:, m * P:(m + 1) * P], hT[:, :], start=True, stop=True)\
                      .then_inc(S("up_ready"), 1)
                pe.wait_ge(S("gated_ready"), FT)
                for t in range(PT):
                    for m in range(FT):
                        mm = pe.matmul(ps[:, 5, t * P:(t + 1) * P], gated[:, m, t * P:(t + 1) * P],
                                       w("w2")[:, m * D:(m + 1) * D], start=m == 0, stop=m == FT - 1)
                mm.then_inc(S("down_ready"), 1)


def choose_two(v, L, C, g, sel, top, n, tmp):
    m, c, cm = tmp
    first = bcast(C.c("first"), 1, [P, n, 8])
    for s in range(2):
        src = g if s == 0 else m
        L(v.tensor_reduce(top[:, s, :], src, AX.X, ALU.max))
        L(v.tensor_tensor(c, src, bcast(top[:, s, :], 2, [P, n, 8]), ALU.is_equal))
        L(v.tensor_tensor(c, c, first, ALU.mult))
        L(v.tensor_reduce(cm, c, AX.X, ALU.max))
        L(v.tensor_tensor(sel[:, s, :, :], c, bcast(cm, 2, [P, n, 8]), ALU.is_equal))
        if s == 0:
            L(v.scalar_tensor_tensor(m, sel[:, 0, :, :], -3.0e38, g, ALU.mult, ALU.add))


def sinkhorn_moe(C, k, ks, packed):
    nc, w, S, ps = C.nc, C.weights(k), C.sem, C.ps
    E, FT, ROUNDS = 8, 2, 3
    with ExitStack() as ctx:
        sb = lambda name, shape, dt=F32: ctx.enter_context(nc.sbuf_tensor(f"moe0_{name}", shape, dt))
        xn = sb("xn", [P, PT, D])
        hT = sb("hT", [P, PAIR])
        la = sb("la", [P, TILES, E])
        ex = sb("ex", [P, TILES, E])
        st = sb("st", [P, 4, TILES])
        packed_la = sb("packed_la", [P, 2, SEQS * E])
        laT = sb("laT", [SEQS * E, 2 * P])
        exT = sb("exT", [SEQS * E, 2 * P])
        stT = sb("stT", [SEQS * E, 4])
        sel = sb("sel", [P, 2, TILES, E])
        top = sb("top", [P, 2, TILES])
        cw = sb("cw", [P, TILES, E])
        cwp = sb("cwp", [P, PT, E])
        g_sb = sb("g_sb", [P, 2, FT, PAIR])
        h_sb = sb("h_sb", [P, 2, FT, PAIR])
        acc = sb("acc", [P, PAIR])
        tmp = (sb("tm", [P, TILES, E]), sb("tc", [P, TILES, E]), sb("tcm", [P, TILES]))
        itemp = sb("itemp", [P, 1])

        def setup(v, L):
            L(v.tensor_scalar(itemp[:, :], w("temperature"), 0.1, None, ALU.max))
            L(v.reciprocal(itemp[:, :], itemp[:, :]))

        start_sublayer(C, k, ks, packed, setup)

        with nc.Fori(0, PAIRS) as i, C.turn() as block:

            @block.vector
            def _(v):
                L = Link(v, S("vector_step"))
                norm_pair(v, L, C, i, xn, S("xn_ready"))
                v.wait_ge(S("logits_ready"), 1)
                lg = la[:, bass.ds(i * PT, PT), :]
                L(v.tensor_tensor(lg, ps[:, 1, 0:PT * E].rearrange("p (t e) -> p t e", e=E),
                                  bcast(w("router_b"), 1, [P, PT, E]), ALU.add))
                L(v.tensor_scalar(lg, lg, itemp[:, 0:1], None, ALU.mult))

            @block.scalar
            def _(a):
                a.wait_ge(S("hT_ps"), 1)
                a.activation(hT[:, :], ps[:, 0, :], ACT.Copy).then_inc(S("hT_ready"), 1)

            @block.tensor
            def _(pe):
                turn_tiles(pe, C, 0, xn, S("xn_ready"), S("hT_ps"))
                pe.wait_ge(S("hT_ready"), 1)
                for t in range(PT):
                    mm = pe.matmul(ps[:, 1, t * E:(t + 1) * E], hT[:, t * P:(t + 1) * P], w("router"),
                                   start=True, stop=True)
                mm.then_inc(S("logits_ready"), 1)

        with C.turn() as block:

            @block.vector
            def _(v):
                L = Link(v, S("vector_step"))
                mx, sm = st[:, 0, :], st[:, 1, :]
                back = ps[:, 2, 0:2 * SEQS * E].rearrange("p (t b e) -> p b t e", t=2, e=E)
                la4 = la[:, :, :].rearrange("p (b t) e -> p b t e", t=2)
                for r in range(ROUNDS):
                    if r:
                        v.wait_ge(S("turned_back"), r)
                        L(v.tensor_copy(la4, back))
                    L(v.tensor_reduce(mx, la[:, :, :], AX.X, ALU.max))
                    v.tensor_tensor(la[:, :, :], la[:, :, :], bcast(mx, 2, [P, TILES, E]), ALU.subtract)\
                     .then_inc(S("shifted"), 1)
                    v.wait_ge(S("expd"), r + 1)
                    v.tensor_reduce(sm, ex[:, :, :], AX.X, ALU.add).then_inc(S("summed"), 1)
                    v.wait_ge(S("logd"), r + 1)
                    v.tensor_tensor(packed_la[:, :, :].rearrange("p t (b e) -> p b t e", e=E), la4,
                                    bcast(st[:, 3, :].rearrange("p (b t) -> p b t", t=2), 3, [P, SEQS, 2, E]),
                                    ALU.subtract).then_inc(S("rows_done"), 1)
                    v.wait_ge(S("turned"), r + 1)
                    L(v.tensor_copy(laT[:, :], ps[0:SEQS * E, 3, 0:2 * P]))
                    v.tensor_reduce(stT[:, 0:1], laT[:, :], AX.X, ALU.max, negate=True).then_inc(S("max_done"), 1)
                    v.wait_ge(S("lse_done"), r + 1)
                    v.wait_ge(S("max_done"), r + 1)
                    L(v.tensor_tensor(stT[:, 3:4], stT[:, 0:1], stT[:, 2:3], ALU.subtract))
                    v.tensor_scalar(laT[:, :], laT[:, :], stT[:, 3:4], None, ALU.add).then_inc(S("cols_done"), 1)
                v.wait_ge(S("gates"), 1)
                L(v.tensor_reduce(sm, ex[:, :, :], AX.X, ALU.add))
                L(v.tensor_scalar(sm, sm, 1e-8, None, ALU.add))
                L(v.reciprocal(sm, sm))
                L(v.tensor_tensor(ex[:, :, :], ex[:, :, :], bcast(sm, 2, [P, TILES, E]), ALU.mult))
                choose_two(v, L, C, ex[:, :, :], sel, top, TILES, (tmp[0][:, :, :], tmp[1][:, :, :], tmp[2][:, :]))
                L(v.tensor_tensor(sm, top[:, 0, :], top[:, 1, :], ALU.add))
                L(v.tensor_scalar(sm, sm, 1e-8, None, ALU.add))
                L(v.reciprocal(sm, sm))
                L(v.tensor_tensor(cw[:, :, :], sel[:, 0, :, :], sel[:, 1, :, :], ALU.add))
                L(v.tensor_tensor(cw[:, :, :], cw[:, :, :], ex[:, :, :], ALU.mult))
                L(v.tensor_tensor(cw[:, :, :], cw[:, :, :], bcast(sm, 2, [P, TILES, E]), ALU.mult))

            @block.scalar
            def _(a):
                for r in range(ROUNDS):
                    a.wait_ge(S("shifted"), r + 1)
                    a.activation(ex[:, :, :], la[:, :, :], ACT.Exp).then_inc(S("expd"), 1)
                    a.wait_ge(S("summed"), r + 1)
                    a.activation(st[:, 3, :], st[:, 1, :], ACT.Ln).then_inc(S("logd"), 1)
                    a.wait_ge(S("max_done"), r + 1)
                    a.activation(exT[:, :], laT[:, :], ACT.Exp, bias=stT[:, 0:1],
                                 accum_out=stT[:, 1:2]).then_inc(S("scalar_step"), 1)
                    a.wait_ge(S("scalar_step"), r + 1)
                    a.activation(stT[:, 2:3], stT[:, 1:2], ACT.Ln).then_inc(S("lse_done"), 1)
                a.wait_ge(S("turned_back"), ROUNDS)
                a.activation(ex[:, :, :].rearrange("p (b t) e -> p b t e", t=2),
                             ps[:, 2, 0:2 * SEQS * E].rearrange("p (t b e) -> p b t e", t=2, e=E),
                             ACT.Exp).then_inc(S("gates"), 1)

            @block.tensor
            def _(pe):
                n = SEQS * E
                for r in range(ROUNDS):
                    pe.wait_ge(S("rows_done"), r + 1)
                    for tt in range(2):
                        mm = pe.transpose(ps[0:n, 3, tt * P:(tt + 1) * P], packed_la[:, tt, :], C.ident)
                    mm.then_inc(S("turned"), 1)
                    pe.wait_ge(S("cols_done"), r + 1)
                    for tt in range(2):
                        mm = pe.transpose(ps[:, 2, tt * n:(tt + 1) * n], laT[:, tt * P:(tt + 1) * P],
                                          C.ident[0:n, 0:n])
                    mm.then_inc(S("turned_back"), 1)

        with nc.Fori(0, PAIRS) as i, C.turn() as block:

            @block.vector
            def _(v):
                L = Link(v, S("vector_step"))
                L.tick(v.tensor_copy(cwp[:, :, :], cw[:, bass.ds(i * PT, PT), :]))
                norm_pair(v, L, C, i, xn, S("xn_ready"))
                L.settle()
                accs = [acc[:, t * P:(t + 1) * P] for t in range(PT)]

                def down(e):
                    v.wait_ge(S("down_ready"), e + 1)
                    for t in range(PT):
                        ins = v.scalar_tensor_tensor(accs[t], ps[:, 5 + e % 2, t * P:(t + 1) * P], cwp[:, t, e:e + 1],
                                                     xn[:, t, :] if e == 0 else accs[t], ALU.mult, ALU.add)
                        L.tick(ins) if t < PT - 1 else ins.then_inc(S("combined"), 1)
                    v.wait_ge(S("combined"), e + 1)

                v.wait_ge(S("xn_ready"), PT)
                for e in range(E):
                    for f in range(FT):
                        v.wait_ge(S("g_ready"), FT * e + f + 1)
                        if e >= 2 and f == 0:
                            v.wait_ge(S("down_ready"), e - 1)
                        v.tensor_tensor(h_sb[:, e % 2, f, :], g_sb[:, e % 2, f, :], ps[:, 3 + f, :], ALU.mult)\
                         .then_inc(S("h_ready"), 1)
                    if e:
                        down(e - 1)
                down(E - 1)
                L(v.tensor_tensor(C.xt(i, 0, PT), C.xt(i, 0, PT), acc[:, :], ALU.add))

            @block.scalar
            def _(a):
                a.wait_ge(S("hT_ps"), 1)
                a.activation(hT[:, :], ps[:, 0, :], ACT.Copy).then_inc(S("hT_ready"), 1)
                for e in range(E):
                    for f in range(FT):
                        a.wait_ge(S("up_ready"), FT * e + f + 1)
                        if e >= 2:
                            a.wait_ge(S("h_ready"), FT * (e - 2) + f + 1)
                        a.activation(g_sb[:, e % 2, f, :], ps[:, 1 + f, :], ACT.Relu).then_inc(S("g_ready"), 1)

            @block.tensor
            def _(pe):
                turn_tiles(pe, C, 0, xn, S("xn_ready"), S("hT_ps"))
                pe.wait_ge(S("hT_ready"), 1)

                def down(e):
                    pe.wait_ge(S("h_ready"), FT * (e + 1))
                    if e >= 2:
                        pe.wait_ge(S("combined"), e - 1)
                    for t in range(PT):
                        for f in range(FT):
                            mm = pe.matmul(ps[:, 5 + e % 2, t * P:(t + 1) * P], h_sb[:, e % 2, f, t * P:(t + 1) * P],
                                           w("wo")[:, (e * FT + f) * D:(e * FT + f + 1) * D],
                                           start=f == 0, stop=f == FT - 1)
                    mm.then_inc(S("down_ready"), 1)

                for e in range(E):
                    for f in range(FT):
                        if e:
                            pe.wait_ge(S("h_ready"), FT * (e - 1) + f + 1)
                        col = slice((e * FT + f) * P, (e * FT + f + 1) * P)
                        pe.matmul(ps[:, 1 + f, :], w("wg")[:, col], hT[:, :], start=True, stop=True)
                        pe.matmul(ps[:, 3 + f, :], w("wp")[:, col], hT[:, :], start=True, stop=True)\
                          .then_inc(S("up_ready"), 1)
                    if e:
                        down(e - 1)
                down(E - 1)


def top2_moe(C, k, ks, packed):
    nc, w, S, ps = C.nc, C.weights(k), C.sem, C.ps
    E, FT = 8, 2
    with ExitStack() as ctx:
        sb = lambda name, shape, dt=F32: ctx.enter_context(nc.sbuf_tensor(f"moe2_{name}", shape, dt))
        xn = sb("xn", [P, PT, D])
        hT = sb("hT", [P, PAIR])
        lg = sb("lg", [P, PT, E])
        sel = sb("sel", [P, 2, PT, E])
        top = sb("top", [P, 2, PT])
        pr = sb("pr", [P, 2, PT])
        cw = sb("cw", [P, PT, E])
        cwT = sb("cwT", [E, PAIR])
        one = sb("one", [P, PT])
        a_sb = sb("a_sb", [P, 2, PAIR])
        z_sb = sb("z_sb", [P, FT, PAIR])
        s_sb = sb("s_sb", [P, 2, FT, PAIR])
        acc = sb("acc", [P, PAIR])
        tmp = (sb("tm", [P, PT, E]), sb("tc", [P, PT, E]), sb("tcm", [P, PT]))
        start_sublayer(C, k, ks, packed)
        with nc.Fori(0, PAIRS) as i, C.turn() as block:

            @block.vector
            def _(v):
                L = Link(v, S("vector_step"))
                norm_pair(v, L, C, i, xn, S("xn_ready"))
                v.wait_ge(S("logits_ready"), 1)
                L(v.tensor_tensor(lg[:, :, :], ps[:, 7, 0:PT * E].rearrange("p (t e) -> p t e", e=E),
                                  bcast(w("gate_b"), 1, [P, PT, E]), ALU.add))
                choose_two(v, L, C, lg[:, :, :], sel, top, PT, (tmp[0][:, :, :], tmp[1][:, :, :], tmp[2][:, :]))
                v.tensor_tensor(pr[:, 1, :], top[:, 1, :], top[:, 0, :], ALU.subtract).then_inc(S("gap_ready"), 1)
                v.wait_ge(S("gap_exp"), 1)
                L(v.tensor_scalar(one[:, :], pr[:, 0, :], 1.0, None, ALU.add))
                L(v.reciprocal(one[:, :], one[:, :]))
                L(v.tensor_tensor(pr[:, 1, :], pr[:, 0, :], one[:, :], ALU.mult))
                L(v.tensor_tensor(cw[:, :, :], sel[:, 0, :, :], bcast(one[:, :], 2, [P, PT, E]), ALU.mult))
                L(v.tensor_tensor(tmp[0][:, :, :], sel[:, 1, :, :], bcast(pr[:, 1, :], 2, [P, PT, E]), ALU.mult))
                v.tensor_tensor(cw[:, :, :], cw[:, :, :], tmp[0][:, :, :], ALU.add).then_inc(S("weights_ready"), 1)
                v.wait_ge(S("weights_ready"), 1)
                v.wait_ge(S("cwT_ps"), 1)
                v.tensor_copy(cwT[:, :], ps[0:E, 7, :]).then_inc(S("cwT_ready"), 1)
                v.wait_ge(S("bias_ready"), 1)
                v.tensor_copy(acc[:, :], ps[:, 7, :]).then_inc(S("acc_ready"), 1)
                v.wait_ge(S("acc_ready"), 1)
                accs = [acc[:, t * P:(t + 1) * P] for t in range(PT)]

                def down(e):
                    v.wait_ge(S("down_ready"), e + 1)
                    for t in range(PT):
                        ins = v.scalar_tensor_tensor(accs[t], ps[:, 7, t * P:(t + 1) * P], cw[:, t, e:e + 1],
                                                     accs[t], ALU.mult, ALU.add)
                        L.tick(ins) if t < PT - 1 else ins.then_inc(S("combined"), 1)
                    v.wait_ge(S("combined"), e + 1)

                for e in range(E):
                    for f in range(FT):
                        v.wait_ge(S("a_ready"), FT * e + f + 1)
                        if e:
                            v.wait_ge(S("mid_ready"), FT * e)
                        v.scalar_tensor_tensor(z_sb[:, f, :], ps[:, 3 + f, :], w("b2")[:, e * FT + f:e * FT + f + 1],
                                               a_sb[:, f, :], ALU.add, ALU.mult).then_inc(S("z_ready"), 1)
                    if e:
                        down(e - 1)
                down(E - 1)
                L(v.tensor_tensor(C.xt(i, 0, PT), C.xt(i, 0, PT), acc[:, :], ALU.add))

            @block.scalar
            def _(a):
                a.wait_ge(S("hT_ps"), 1)
                a.activation(hT[:, :], ps[:, 0, :], ACT.Copy).then_inc(S("hT_ready"), 1)
                a.wait_ge(S("gap_ready"), 1)
                a.activation(pr[:, 0, :], pr[:, 1, :], ACT.Exp).then_inc(S("gap_exp"), 1)
                for e in range(E):
                    for f in range(FT):
                        a.wait_ge(S("up_ready"), FT * e + f + 1)
                        if e:
                            a.wait_ge(S("z_ready"), FT * (e - 1) + f + 1)
                        a.activation(a_sb[:, f, :], ps[:, 1 + f, :], ACT.Identity,
                                     bias=w("b1")[:, e * FT + f:e * FT + f + 1]).then_inc(S("a_ready"), 1)
                    for f in range(FT):
                        a.wait_ge(S("mid_ready"), FT * e + f + 1)
                        if e >= 2:
                            a.wait_ge(S("down_ready"), e - 1)
                        a.activation(s_sb[:, e % 2, f, :], ps[:, 5 + f, :], ACT.Silu,
                                     bias=w("bg")[:, e * FT + f:e * FT + f + 1]).then_inc(S("s_ready"), 1)

            @block.tensor
            def _(pe):
                turn_tiles(pe, C, 0, xn, S("xn_ready"), S("hT_ps"))
                pe.wait_ge(S("hT_ready"), 1)
                for t in range(PT):
                    mm = pe.matmul(ps[:, 7, t * E:(t + 1) * E], hT[:, t * P:(t + 1) * P], w("gate"),
                                   start=True, stop=True)
                mm.then_inc(S("logits_ready"), 1)

                def up(e):
                    for f in range(FT):
                        if e:
                            pe.wait_ge(S("z_ready"), FT * (e - 1) + f + 1)
                        col = slice((e * FT + f) * P, (e * FT + f + 1) * P)
                        pe.matmul(ps[:, 1 + f, :], w("w1")[:, col], hT[:, :], start=True, stop=True)
                        pe.matmul(ps[:, 3 + f, :], w("w2")[:, col], hT[:, :], start=True, stop=True)\
                          .then_inc(S("up_ready"), 1)

                def mid(e):
                    pe.wait_ge(S("z_ready"), FT * (e + 1))
                    for m in range(FT):
                        if e:
                            pe.wait_ge(S("s_ready"), FT * (e - 1) + m + 1)
                        for f in range(FT):
                            c0 = (e * FT + f) * FT * P + m * P
                            mm = pe.matmul(ps[:, 5 + m, :], w("wg")[:, c0:c0 + P], z_sb[:, f, :],
                                           start=f == 0, stop=f == FT - 1)
                        mm.then_inc(S("mid_ready"), 1)

                def down(e):
                    pe.wait_ge(S("s_ready"), FT * (e + 1))
                    if e:
                        pe.wait_ge(S("combined"), e)
                    else:
                        pe.wait_ge(S("acc_ready"), 1)
                    for t in range(PT):
                        for f in range(FT):
                            mm = pe.matmul(ps[:, 7, t * P:(t + 1) * P], s_sb[:, e % 2, f, t * P:(t + 1) * P],
                                           w("w3")[:, (e * FT + f) * D:(e * FT + f + 1) * D],
                                           start=f == 0, stop=f == FT - 1)
                    mm.then_inc(S("down_ready"), 1)

                up(0)
                pe.wait_ge(S("weights_ready"), 1)
                for t in range(PT):
                    mm = pe.transpose(ps[0:E, 7, t * P:(t + 1) * P], cw[:, t, :], C.ident)
                mm.then_inc(S("cwT_ps"), 1)
                pe.wait_ge(S("cwT_ready"), 1)
                for t in range(PT):
                    mm = pe.matmul(ps[:, 7, t * P:(t + 1) * P], cwT[:, t * P:(t + 1) * P], w("b3")[0:E, :],
                                   start=True, stop=True)
                mm.then_inc(S("bias_ready"), 1)
                for e in range(E):
                    mid(e)
                    if e + 1 < E:
                        up(e + 1)
                    down(e)


def heads4(ap):
    return ap.rearrange("p t (h d) -> p t h d", d=HD)


def project_tokens(pe, C, first_bank, hT, wt, n, done):
    for t in range(PT):
        pe.matmul(C.ps[:, first_bank + t, 0:n], hT[:, t * P:(t + 1) * P], wt, start=True, stop=True)\
          .then_inc(done, 1)


def flow_attention(C, k, ks, packed):
    nc, w, S, ps = C.nc, C.weights(k), C.sem, C.ps
    EPS = 1e-6
    with ExitStack() as ctx:
        sb = lambda name, shape, dt=F32: ctx.enter_context(nc.sbuf_tensor(f"flow_{name}", shape, dt))
        xn = sb("xn", [P, PT, D])
        hT = sb("hT", [P, PAIR])
        pre = sb("pre", [P, PT, 3 * D])
        qk = sb("qk", [P, PT, 2 * D])
        qke = sb("qke", [P, PT, 2 * D])
        tot = sb("tot", [P, 2, 2 * D])
        prod = sb("prod", [P, PT, 2 * D])
        flow = sb("flow", [P, PT, 2 * HEADS])
        scaled = sb("scaled", [P, PT, 2 * D])
        cons = sb("cons", [P, PT, 2 * HEADS])
        comp = sb("comp", [P, PT, HEADS])
        csum = sb("csum", [P, 2, HEADS])
        alloc = sb("alloc", [P, PT, HEADS])
        vc = sb("vc", [P, PT, D])
        qT = sb("qT", [P, PAIR])
        kv = sb("kv", [P, 2, D])
        att = sb("att", [P, PT, D])
        attT = sb("attT", [P, PAIR])
        start_sublayer(C, k, ks, packed)
        by2 = lambda ap: ap.rearrange("p (b t) n -> p b t n", t=2)
        with nc.Fori(0, PAIRS) as i, C.turn() as block:

            @block.vector
            def _(v):
                L = Link(v, S("vector_step"))
                norm_pair(v, L, C, i, xn, S("xn_ready"))
                for t in range(PT):
                    v.wait_ge(S("qkv_ready"), t + 1)
                    v.tensor_tensor(pre[:, t, :], ps[:, t, 0:3 * D], w("qkv_b"), ALU.add).then_inc(S("biased"), 1)
                v.wait_ge(S("biased"), PT)
                v.wait_ge(S("sigmoid"), 1)
                L(v.tensor_scalar(qke[:, :, :], qk[:, :, :], EPS, None, ALU.add))

                def against_totals(n, out):
                    v.wait_ge(S("totals"), n)
                    L(v.tensor_scalar(tot[:, :, :], ps[:, 4:6, 0:2 * D], EPS, None, ALU.add))
                    for b in range(2):
                        for s in range(2):
                            L.tick(v.tensor_tensor(prod[:, 2 * b:2 * b + 2, s * D:(s + 1) * D],
                                                   qke[:, 2 * b:2 * b + 2, s * D:(s + 1) * D],
                                                   bcast(tot[:, b, (1 - s) * D:(2 - s) * D], 1, [P, 2, D]), ALU.mult))
                    L.settle()
                    L(v.tensor_reduce(out, prod[:, :, :].rearrange("p t (h d) -> p t h d", d=HD), AX.X, ALU.add))

                against_totals(1, flow[:, :, :])
                L(v.reciprocal(flow[:, :, :], flow[:, :, :]))
                v.tensor_tensor(heads4(scaled[:, :, :]), heads4(qk[:, :, :]),
                                bcast(flow[:, :, :], 3, [P, PT, 2 * HEADS, HD]), ALU.mult).then_inc(S("scaled_ready"), 1)
                v.wait_ge(S("scaled_ready"), 1)
                against_totals(2, cons[:, :, :])
                L(v.tensor_scalar(cons[:, :, :], cons[:, :, :], EPS, None, ALU.add))
                v.tensor_scalar(cons[:, :, HEADS:2 * HEADS], cons[:, :, HEADS:2 * HEADS], -1.0, 1.0,
                                ALU.max, ALU.min).then_inc(S("conserved"), 1)
                v.wait_ge(S("comp_sum"), 1)
                L(v.reciprocal(csum[:, :, :], ps[:, 6, 0:2 * HEADS].rearrange("p (b h) -> p b h", b=2)))
                L(v.tensor_scalar(csum[:, :, :], csum[:, :, :], float(SEQ), None, ALU.mult))
                for b in range(2):
                    L.tick(v.tensor_tensor(comp[:, 2 * b:2 * b + 2, :], comp[:, 2 * b:2 * b + 2, :],
                                           bcast(csum[:, b, :], 1, [P, 2, HEADS]), ALU.mult))
                L.settle()
                v.tensor_tensor(heads4(vc[:, :, :]), heads4(pre[:, :, 2 * D:3 * D]),
                                bcast(comp[:, :, :], 3, [P, PT, HEADS, HD]), ALU.mult).then_inc(S("vc_ready"), 1)
                for b in range(2):
                    v.wait_ge(S("kv_ps"), b + 1)
                    v.tensor_tensor(kv[:, b, :], ps[:, 2 + b, 0:D], C.c("block"), ALU.mult).then_inc(S("kv_ready"), 1)
                v.wait_ge(S("att_ps"), 1)
                v.wait_ge(S("alloc_ready"), 1)
                v.tensor_tensor(heads4(att[:, :, :]), heads4(ps[:, 4, :].rearrange("p (t d) -> p t d", d=D)),
                                bcast(alloc[:, :, :], 3, [P, PT, HEADS, HD]), ALU.mult).then_inc(S("att_ready"), 1)
                add_projection(v, L, C, i, w, S, 6)

            @block.scalar
            def _(a):
                a.wait_ge(S("hT_ps"), 1)
                a.activation(hT[:, :], ps[:, 7, :], ACT.Copy).then_inc(S("hT_ready"), 1)
                a.wait_ge(S("biased"), PT)
                a.activation(qk[:, :, :], pre[:, :, 0:2 * D], ACT.Sigmoid).then_inc(S("sigmoid"), 1)
                a.wait_ge(S("conserved"), 1)
                a.activation(alloc[:, :, :], cons[:, :, 0:HEADS], ACT.Sigmoid).then_inc(S("alloc_ready"), 1)
                a.activation(comp[:, :, :], cons[:, :, HEADS:2 * HEADS], ACT.Exp).then_inc(S("comp_ready"), 1)
                a.wait_ge(S("qT_ps"), 1)
                a.activation(qT[:, :], ps[:, 7, :], ACT.Copy).then_inc(S("qT_ready"), 1)
                a.wait_ge(S("attT_ps"), 1)
                a.activation(attT[:, :], ps[:, 5, :], ACT.Copy).then_inc(S("attT_ready"), 1)

            @block.tensor
            def _(pe):
                ones = C.c("ones")
                turn_tiles(pe, C, 7, xn, S("xn_ready"), S("hT_ps"))
                pe.wait_ge(S("hT_ready"), 1)
                project_tokens(pe, C, 0, hT, w("qkv"), 3 * D, S("qkv_ready"))

                def totals(src):
                    for b in range(2):
                        for t in range(2):
                            mm = pe.matmul(ps[:, 4 + b, 0:2 * D], ones, src[:, 2 * b + t, :], start=t == 0, stop=t == 1)
                    mm.then_inc(S("totals"), 1)

                pe.wait_ge(S("sigmoid"), 1)
                totals(qk)
                pe.wait_ge(S("scaled_ready"), 1)
                totals(scaled)
                for t in range(PT):
                    mm = pe.transpose(ps[:, 7, t * P:(t + 1) * P], scaled[:, t, 0:D], C.ident)
                mm.then_inc(S("qT_ps"), 1)
                pe.wait_ge(S("comp_ready"), 1)
                for b in range(2):
                    for t in range(2):
                        mm = pe.matmul(ps[:, 6, b * HEADS:(b + 1) * HEADS], ones, comp[:, 2 * b + t, :],
                                       start=t == 0, stop=t == 1)
                mm.then_inc(S("comp_sum"), 1)
                pe.wait_ge(S("vc_ready"), 1)
                for b in range(2):
                    for t in range(2):
                        mm = pe.matmul(ps[:, 2 + b, 0:D], qk[:, 2 * b + t, D:2 * D], vc[:, 2 * b + t, :],
                                       start=t == 0, stop=t == 1)
                    mm.then_inc(S("kv_ps"), 1)
                pe.wait_ge(S("qT_ready"), 1)
                pe.wait_ge(S("kv_ready"), 2)
                for t in range(PT):
                    mm = pe.matmul(ps[:, 4, t * P:(t + 1) * P], qT[:, t * P:(t + 1) * P], kv[:, t // 2, :],
                                   start=True, stop=True)
                mm.then_inc(S("att_ps"), 1)
                turn_and_project(pe, C, w, S, att, attT, 5, 6)


def turn_and_project(pe, C, w, S, att, attT, turn_bank, out_bank):
    pe.wait_ge(S("att_ready"), 1)
    for t in range(PT):
        mm = pe.transpose(C.ps[:, turn_bank, t * P:(t + 1) * P], att[:, t, :], C.ident)
    mm.then_inc(S("attT_ps"), 1)
    pe.wait_ge(S("attT_ready"), 1)
    for t in range(PT):
        mm = pe.matmul(C.ps[:, out_bank, t * P:(t + 1) * P], attT[:, t * P:(t + 1) * P], w("proj"),
                       start=True, stop=True)
    mm.then_inc(S("out_ready"), 1)


def add_projection(v, L, C, i, w, S, bank):
    v.wait_ge(S("out_ready"), 1)
    xs = C.xt(i, 0, PT)
    L(v.tensor_tensor(xs, xs, C.ps[:, bank, :], ALU.add))
    L(v.tensor_tensor(xs.rearrange("p (t d) -> p t d", d=D), xs.rearrange("p (t d) -> p t d", d=D),
                      bcast(w("proj_b"), 1, [P, PT, D]), ALU.add))


def relu_attention(C, k, ks, packed):
    nc, w, S, ps = C.nc, C.weights(k), C.sem, C.ps
    RMS_EPS, LIN_EPS = 1.1920929e-07, 1e-6
    N = D + HEADS
    with ExitStack() as ctx:
        sb = lambda name, shape, dt=F32: ctx.enter_context(nc.sbuf_tensor(f"lin_{name}", shape, dt))
        xn = sb("xn", [P, PT, D])
        hT = sb("hT", [P, PAIR])
        pre = sb("pre", [P, PT, 3 * D + 1])
        qk = sb("qk", [P, 2, PT, D])
        rot = sb("rot", [P, 2, PT, D])
        qT = sb("qT", [P, PAIR])
        kv = sb("kv", [P, 2, N])
        den = sb("den", [P, PT, HEADS])
        att = sb("att", [P, PT, D])
        attT = sb("attT", [P, PAIR])
        o = sb("o", [P, PT, D])

        def setup(v, L):
            L(v.memset(pre[:, :, 3 * D:3 * D + 1], 1.0))

        start_sublayer(C, k, ks, packed, setup)
        pairs = lambda ap: ap.rearrange("p t (c two) -> p t c two", two=2)

        def mean_square(v, L):
            L(v.tensor_tensor(C.mv[:, :, 0], C.mv[:, :, 0], C.mv[:, :, 0], ALU.mult))
            L(v.tensor_tensor(C.mv[:, :, 1], C.mv[:, :, 1], C.mv[:, :, 0], ALU.add))

        with nc.Fori(0, PAIRS) as i, C.turn() as block:

            @block.vector
            def _(v):
                L = Link(v, S("vector_step"))
                norm_pair(v, L, C, i, xn, S("xn_ready"))
                for t in range(PT):
                    v.wait_ge(S("qkv_ready"), t + 1)
                    L.tick(v.tensor_tensor(pre[:, t, 0:3 * D], ps[:, t, 0:3 * D], w("qkv_b"), ALU.add))
                L.settle()
                for s, gain in enumerate(("gq", "gk")):
                    moments(v, L, C, [pre[:, t, s * D:(s + 1) * D] for t in range(PT)])
                    mean_square(v, L)
                    rsqrt(v, L, C, C.rstd[:, :], C.mv[:, :, 1], RMS_EPS)
                    for t in range(PT):
                        L.tick(v.scalar_tensor_tensor(qk[:, s, t, :], pre[:, t, s * D:(s + 1) * D],
                                                      C.rstd[:, t:t + 1], w(gain), ALU.mult, ALU.mult))
                    L.settle()
                    cosT = C.c("cosT").rearrange("p (t d) -> p t d", t=2)
                    sinT = pairs(C.c("sinT").rearrange("p (t d) -> p t d", t=2))
                    for b in range(2):
                        tl = slice(2 * b, 2 * b + 2)
                        a2, r2 = pairs(qk[:, s, tl, :]), pairs(rot[:, s, tl, :])
                        for e in range(2):
                            L.tick(v.tensor_tensor(r2[:, :, :, e], a2[:, :, :, 1 - e], sinT[:, :, :, e], ALU.mult))
                    L.settle()
                    for b in range(2):
                        tl = slice(2 * b, 2 * b + 2)
                        L.tick(v.tensor_tensor(qk[:, s, tl, :], qk[:, s, tl, :], cosT, ALU.mult))
                    L.settle()
                    L(v.tensor_tensor(qk[:, s, :, :], qk[:, s, :, :], rot[:, s, :, :], ALU.add))
                    v.tensor_scalar(qk[:, s, :, :], qk[:, s, :, :], 0.0, None, ALU.max).then_inc(S("qk_ready"), 1)
                for b in range(2):
                    v.wait_ge(S("kv_ps"), b + 1)
                    L.tick(v.tensor_tensor(kv[:, b, 0:D], ps[:, 4 + b, 0:D], C.c("block"), ALU.mult))
                    v.tensor_scalar(kv[:, b, D:N], C.c("heads"), ps[:, 4 + b, D:D + 1], None, ALU.mult)\
                     .then_inc(S("kv_ready"), 1)
                for h in range(2):
                    v.wait_ge(S("att_ps"), h + 1)
                    src = ps[:, 6 + h, 0:2 * N].rearrange("p (t n) -> p t n", n=N)
                    tl = slice(2 * h, 2 * h + 2)
                    L(v.tensor_scalar(den[:, tl, :], src[:, :, D:N], LIN_EPS, None, ALU.add))
                    L(v.reciprocal(den[:, tl, :], den[:, tl, :]))
                    ins = v.tensor_tensor(heads4(att[:, tl, :]), heads4(src[:, :, 0:D]),
                                          bcast(den[:, tl, :], 3, [P, 2, HEADS, HD]), ALU.mult)
                    ins.then_inc(S("att_ready" if h else "att_half"), 1)
                v.wait_ge(S("out_ready"), 1)
                L(v.tensor_tensor(o[:, :, :], ps[:, 1, :].rearrange("p (t d) -> p t d", d=D),
                                  bcast(w("proj_b"), 1, [P, PT, D]), ALU.add))
                moments(v, L, C, [o[:, t, :] for t in range(PT)])
                mean_square(v, L)
                rsqrt(v, L, C, C.rstd[:, :], C.mv[:, :, 1], RMS_EPS)
                for t in range(PT):
                    L.tick(v.scalar_tensor_tensor(o[:, t, :], o[:, t, :], C.rstd[:, t:t + 1], w("gout"),
                                                  ALU.mult, ALU.mult))
                L.settle()
                xs = C.xt(i, 0, PT)
                L(v.tensor_tensor(xs, xs, o[:, :, :].rearrange("p t d -> p (t d)"), ALU.add))

            @block.scalar
            def _(a):
                a.wait_ge(S("hT_ps"), 1)
                a.activation(hT[:, :], ps[:, 7, :], ACT.Copy).then_inc(S("hT_ready"), 1)
                a.wait_ge(S("qT_ps"), 1)
                a.activation(qT[:, :], ps[:, 7, :], ACT.Copy).then_inc(S("qT_ready"), 1)
                a.wait_ge(S("attT_ps"), 1)
                a.activation(attT[:, :], ps[:, 0, :], ACT.Copy).then_inc(S("attT_ready"), 1)

            @block.tensor
            def _(pe):
                turn_tiles(pe, C, 7, xn, S("xn_ready"), S("hT_ps"))
                pe.wait_ge(S("hT_ready"), 1)
                project_tokens(pe, C, 0, hT, w("qkv"), 3 * D, S("qkv_ready"))
                pe.wait_ge(S("qk_ready"), 1)
                for t in range(PT):
                    mm = pe.transpose(ps[:, 7, t * P:(t + 1) * P], qk[:, 0, t, :], C.ident)
                mm.then_inc(S("qT_ps"), 1)
                pe.wait_ge(S("qk_ready"), 2)
                for b in range(2):
                    for t in range(2):
                        mm = pe.matmul(ps[:, 4 + b, 0:D + 1], qk[:, 1, 2 * b + t, :], pre[:, 2 * b + t, 2 * D:3 * D + 1],
                                       start=t == 0, stop=t == 1)
                    mm.then_inc(S("kv_ps"), 1)
                pe.wait_ge(S("qT_ready"), 1)
                for t in range(PT):
                    pe.wait_ge(S("kv_ready"), t // 2 + 1)
                    mm = pe.matmul(ps[:, 6 + t // 2, (t % 2) * N:(t % 2 + 1) * N], qT[:, t * P:(t + 1) * P],
                                   kv[:, t // 2, :], start=True, stop=True)
                    if t % 2:
                        mm.then_inc(S("att_ps"), 1)
                turn_and_project(pe, C, w, S, att, attT, 0, 1)


def block_attention(C, k, ks, packed):
    nc, w, S, ps = C.nc, C.weights(k), C.sem, C.ps
    EPS, B = 1e-3, 64
    N = D + HEADS
    with ExitStack() as ctx:
        sb = lambda name, shape, dt=F32: ctx.enter_context(nc.sbuf_tensor(f"blocks_{name}", shape, dt))
        xn = sb("xn", [P, PT, D])
        hT = sb("hT", [P, PAIR])
        qx = sb("qx", [P, PT, D])
        kx = sb("kx", [P, PT, D])
        vv = sb("vv", [P, PT, D + 1])
        mx = sb("mx", [P, PT, HEADS])
        qT = sb("qT", [P, PAIR])
        kv = sb("kv", [P, 2, 3, N])
        den = sb("den", [P, PT, HEADS])
        att = sb("att", [P, PT, D])
        attT = sb("attT", [P, PAIR])

        def setup(v, L):
            L(v.memset(vv[:, :, D:D + 1], 1.0))

        start_sublayer(C, k, ks, packed, setup)
        with nc.Fori(0, PAIRS) as i, C.turn() as block:

            @block.vector
            def _(v):
                L = Link(v, S("vector_step"))
                norm_pair(v, L, C, i, xn, S("xn_ready"))
                bc = lambda ap: bcast(ap, 3, [P, PT, HEADS, HD])
                v.wait_ge(S("qkv_ready"), PT)
                for t in range(PT):
                    L.tick(v.tensor_reduce(mx[:, t, :], ps[:, t, 0:D].rearrange("p (h d) -> p h d", d=HD), AX.X, ALU.max))
                    L.tick(v.tensor_copy(vv[:, t, 0:D], ps[:, t, 2 * D:3 * D]))
                L.settle()
                for t in range(PT):
                    L.tick(v.tensor_tensor(qx[:, t, :].rearrange("p (h d) -> p h d", d=HD),
                                           ps[:, t, 0:D].rearrange("p (h d) -> p h d", d=HD),
                                           bcast(mx[:, t, :], 2, [P, HEADS, HD]), ALU.subtract))
                L.settle()
                v.tensor_copy(kx[:, :, :], ps[:, 0:PT, D:2 * D]).then_inc(S("logits_ready"), 1)
                v.wait_ge(S("exp_ready"), 1)
                L(v.tensor_reduce(mx[:, :, :], heads4(qx[:, :, :]), AX.X, ALU.add))
                L(v.reciprocal(mx[:, :, :], mx[:, :, :]))
                L(v.tensor_scalar(mx[:, :, :], mx[:, :, :], HD ** -0.5, None, ALU.mult))
                v.tensor_tensor(heads4(qx[:, :, :]), heads4(qx[:, :, :]), bc(mx[:, :, :]), ALU.mult)\
                 .then_inc(S("q_ready"), 1)
                for b in range(2):
                    v.wait_ge(S("kv_ps"), b + 1)
                    for u in range(3):
                        src = ps[:, 4 + b, u * (D + 1):(u + 1) * (D + 1)]
                        L.tick(v.tensor_tensor(kv[:, b, u, 0:D], src[:, 0:D], C.c("block"), ALU.mult))
                        ins = v.tensor_scalar(kv[:, b, u, D:N], C.c("heads"), src[:, D:D + 1], None, ALU.mult)
                        L.tick(ins) if u < 2 else ins.then_inc(S("kv_ready"), 1)
                for b in range(2):
                    L.tick(v.memset(att[0:B, 2 * b, :], 0.0))
                L.settle()
                for b in range(2):
                    v.wait_ge(S("att_ps"), b + 1)
                    for t, p0 in ((0, B), (1, 0)):
                        src = ps[p0:P, 6 + b, t * N:(t + 1) * N]
                        L(v.tensor_scalar(den[p0:P, 2 * b + t, :], src[:, D:N], EPS, None, ALU.max))
                        L(v.reciprocal(den[p0:P, 2 * b + t, :], den[p0:P, 2 * b + t, :]))
                        ins = v.tensor_tensor(att[p0:P, 2 * b + t, :].rearrange("p (h d) -> p h d", d=HD),
                                              src[:, 0:D].rearrange("p (h d) -> p h d", d=HD),
                                              bcast(den[p0:P, 2 * b + t, :], 2, [P - p0, HEADS, HD]), ALU.mult)
                        L.tick(ins) if (b, t) != (1, 1) else ins.then_inc(S("att_ready"), 1)
                L.settle()
                add_projection(v, L, C, i, w, S, 1)

            @block.scalar
            def _(a):
                a.wait_ge(S("hT_ps"), 1)
                a.activation(hT[:, :], ps[:, 7, :], ACT.Copy).then_inc(S("hT_ready"), 1)
                a.wait_ge(S("logits_ready"), 1)
                a.activation(qx[:, :, :], qx[:, :, :], ACT.Exp)
                a.activation(kx[:, :, :], kx[:, :, :], ACT.Exp).then_inc(S("exp_ready"), 1)
                a.wait_ge(S("qT_ps"), 1)
                a.activation(qT[:, :], ps[:, 7, :], ACT.Copy).then_inc(S("qT_ready"), 1)
                a.wait_ge(S("attT_ps"), 1)
                a.activation(attT[:, :], ps[:, 0, :], ACT.Copy).then_inc(S("attT_ready"), 1)

            @block.tensor
            def _(pe):
                turn_tiles(pe, C, 7, xn, S("xn_ready"), S("hT_ps"))
                pe.wait_ge(S("hT_ready"), 1)
                project_tokens(pe, C, 0, hT, w("qkv"), 3 * D, S("qkv_ready"))
                pe.wait_ge(S("exp_ready"), 1)
                for b in range(2):
                    for u, parts in enumerate(([(0, B)], [(0, P)], [(0, P), (1, B)])):
                        for n, (t, rows_) in enumerate(parts):
                            mm = pe.matmul(ps[:, 4 + b, u * (D + 1):(u + 1) * (D + 1)], kx[0:rows_, 2 * b + t, :],
                                           vv[0:rows_, 2 * b + t, :], start=n == 0, stop=n == len(parts) - 1)
                    mm.then_inc(S("kv_ps"), 1)
                pe.wait_ge(S("q_ready"), 1)
                for t in range(PT):
                    mm = pe.transpose(ps[:, 7, t * P:(t + 1) * P], qx[:, t, :], C.ident)
                mm.then_inc(S("qT_ps"), 1)
                pe.wait_ge(S("qT_ready"), 1)
                for b in range(2):
                    pe.wait_ge(S("kv_ready"), b + 1)
                    for u in range(1, 4):
                        t, p0 = u // 2, (u % 2) * B
                        mm = pe.matmul(ps[p0:p0 + B, 6 + b, t * N:(t + 1) * N],
                                       qT[:, 2 * b * P + u * B:2 * b * P + (u + 1) * B], kv[:, b, u - 1, :],
                                       start=True, stop=True)
                    mm.then_inc(S("att_ps"), 1)
                turn_and_project(pe, C, w, S, att, attT, 0, 1)


ROUND = 1.5 * 2.0 ** 23


def bit_ffn(C, k, ks, packed):
    nc, w, S, ps = C.nc, C.weights(k), C.sem, C.ps
    F, FT = 4 * D, 4
    with ExitStack() as ctx:
        sb = lambda name, shape, dt=F32: ctx.enter_context(nc.sbuf_tensor(f"bit_{name}", shape, dt))
        wq = {n: sb("q_" + n, [P, F], BF16) for n in ("gate", "up", "down")}
        wabs = sb("wabs", [P, 4])
        wscale = sb("wscale", [P, 4])
        winv = sb("winv", [P, 4])
        wt = sb("wt", [P, F])
        xn = sb("xn", [P, PT, D])
        amax = sb("amax", [P, PT])
        asc = sb("asc", [P, PT])
        gsc = sb("gsc", [P, PT])
        usc = sb("usc", [P, PT])
        dsc = sb("dsc", [P, PT])
        hmax = sb("hmax", [P, PT])
        hsc = sb("hsc", [P, PT])
        xr = sb("xr", [P, PT, D])
        xq = sb("xq", [P, PT, D], BF16)
        xqT = sb("xqT", [P, PAIR], BF16)
        gate = sb("gate", [P, 2, F])
        h = sb("h", [P, 2, F])
        hr = sb("hr", [P, 2, F])
        hq = sb("hq", [P, 2, F], BF16)
        hqT = sb("hqT", [P, 2, F], BF16)
        psb = lambda bank: ps[:, bank, 0:F // 2].bitcast(BF16)
        start_sublayer(C, k, ks, packed)
        names = ("gate", "up", "down")
        with C.turn() as block:

            @block.vector
            def _(v):
                L = Link(v, S("vector_step"))
                L(v.memset(wabs[:, 3:4], 0.0))
                for n, name in enumerate(names):
                    L.tick(v.tensor_reduce(wabs[:, n:n + 1], w(name), AX.X, ALU.add, apply_absolute_value=True))
                L.settle()
                v.tensor_copy(wscale[:, :], wabs[:, :]).then_inc(S("row_sums"), 1)
                v.wait_ge(S("sums"), 1)
                L(v.tensor_scalar(wscale[:, :], ps[:, 0, 0:4], 1.0 / (F * D), 1e-5, ALU.mult, ALU.max))
                L(v.reciprocal(winv[:, :], wscale[:, :]))
                for n, name in enumerate(names):
                    L(v.tensor_scalar(wt[:, :], w(name), winv[:, n:n + 1], ROUND, ALU.mult, ALU.add))
                    L(v.tensor_scalar(wt[:, :], wt[:, :], -ROUND, None, ALU.add))
                    L(v.tensor_scalar(wq[name][:, :], wt[:, :], -1.0, 1.0, ALU.max, ALU.min))

            @block.tensor
            def _(pe):
                pe.wait_ge(S("row_sums"), 1)
                pe.matmul(ps[:, 0, 0:4], C.c("ones"), wscale[:, :], start=True, stop=True).then_inc(S("sums"), 1)

        with nc.Fori(0, PAIRS) as i, C.turn() as block:

            @block.vector
            def _(v):
                L = Link(v, S("vector_step"))
                norm_pair(v, L, C, i, xn, S("xn_ready"))
                v.wait_ge(S("xn_ready"), PT)
                L(v.tensor_reduce(amax[:, :], xn[:, :, :], AX.X, ALU.max, apply_absolute_value=True))
                L(v.tensor_scalar(amax[:, :], amax[:, :], 1e-5, None, ALU.max))
                L(v.reciprocal(asc[:, :], amax[:, :]))
                L(v.tensor_scalar(asc[:, :], asc[:, :], 127.0, None, ALU.mult))
                for t in range(PT):
                    L.tick(v.tensor_scalar(xr[:, t, :], xn[:, t, :], asc[:, t:t + 1], ROUND, ALU.mult, ALU.add))
                L.settle()
                L(v.tensor_scalar(xr[:, :, :], xr[:, :, :], -ROUND, None, ALU.add))
                v.tensor_scalar(xq[:, :, :], xr[:, :, :], -128.0, 127.0, ALU.max, ALU.min).then_inc(S("xq_ready"), 1)
                L(v.tensor_scalar(amax[:, :], amax[:, :], 1.0 / 127.0, None, ALU.mult))
                L(v.tensor_scalar(usc[:, :], amax[:, :], wscale[:, 1:2], None, ALU.mult))
                v.tensor_scalar(gsc[:, :], amax[:, :], wscale[:, 0:1], None, ALU.mult).then_inc(S("scales_ready"), 1)
                for t in range(PT):
                    hb, rb = h[:, t % 2, :], hr[:, t % 2, :]
                    v.wait_ge(S("gate_ready"), t + 1)
                    L(v.scalar_tensor_tensor(hb, ps[:, 3 + t % 2, :], usc[:, t:t + 1], gate[:, t % 2, :], ALU.mult, ALU.mult))
                    L(v.tensor_reduce(hmax[:, t:t + 1], hb, AX.X, ALU.max, apply_absolute_value=True))
                    L(v.tensor_scalar(hmax[:, t:t + 1], hmax[:, t:t + 1], 1e-5, None, ALU.max))
                    L(v.reciprocal(hsc[:, t:t + 1], hmax[:, t:t + 1]))
                    L(v.tensor_scalar(hsc[:, t:t + 1], hsc[:, t:t + 1], 127.0, None, ALU.mult))
                    L(v.tensor_scalar(rb, hb, hsc[:, t:t + 1], ROUND, ALU.mult, ALU.add))
                    L(v.tensor_scalar(rb, rb, -ROUND, None, ALU.add))
                    if t >= 2:
                        v.wait_ge(S("hqT_ps"), t - 1)
                    v.tensor_scalar(hq[:, t % 2, :], rb, -128.0, 127.0, ALU.max, ALU.min).then_inc(S("hq_ready"), 1)
                L(v.tensor_scalar(dsc[:, :], hmax[:, :], 1.0 / 127.0, wscale[:, 2:3], ALU.mult, ALU.mult))
                v.wait_ge(S("down_ready"), PT)
                for t in range(PT):
                    xs = C.xt(i, t)
                    L.tick(v.scalar_tensor_tensor(xs, ps[:, 7, t * P:(t + 1) * P], dsc[:, t:t + 1], xs, ALU.mult, ALU.add))
                L.settle()

            def turned(a, t):
                a.wait_ge(S("hqT_ps"), t + 1)
                if t >= 2:
                    a.wait_ge(S("down_ready"), t - 1)
                a.activation(hqT[:, t % 2, :], psb(5 + t % 2), ACT.Copy).then_inc(S("hqT_ready"), 1)

            @block.scalar
            def _(a):
                a.wait_ge(S("xqT_ps"), 1)
                a.activation(xqT[:, :], psb(0), ACT.Copy).then_inc(S("xqT_ready"), 1)
                a.wait_ge(S("scales_ready"), 1)
                for t in range(PT):
                    a.wait_ge(S("up_ready"), t + 1)
                    if t >= 2:
                        a.wait_ge(S("hq_ready"), t - 1)
                    a.activation(gate[:, t % 2, :], ps[:, 1 + t % 2, :], ACT.Silu, scale=gsc[:, t:t + 1])\
                     .then_inc(S("gate_ready"), 1)
                    if t >= 1:
                        turned(a, t - 1)
                turned(a, PT - 1)

            @block.tensor
            def _(pe):
                pe.wait_ge(S("xq_ready"), 1)
                for t in range(PT):
                    mm = pe.transpose(psb(0)[:, t * P:(t + 1) * P], xq[:, t, :], C.identb[:, :])
                mm.then_inc(S("xqT_ps"), 1)
                pe.wait_ge(S("xqT_ready"), 1)

                def up(t):
                    if t >= 2:
                        pe.wait_ge(S("hq_ready"), t - 1)
                    pe.matmul(ps[:, 1 + t % 2, :], xqT[:, t * P:(t + 1) * P], wq["gate"][:, :], start=True, stop=True)
                    pe.matmul(ps[:, 3 + t % 2, :], xqT[:, t * P:(t + 1) * P], wq["up"][:, :], start=True, stop=True)\
                      .then_inc(S("up_ready"), 1)

                up(0)
                for t in range(PT):
                    if t + 1 < PT:
                        up(t + 1)
                    pe.wait_ge(S("hq_ready"), t + 1)
                    if t >= 2:
                        pe.wait_ge(S("hqT_ready"), t - 1)
                    for m in range(FT):
                        mm = pe.transpose(psb(5 + t % 2)[:, m * P:(m + 1) * P], hq[:, t % 2, m * P:(m + 1) * P], C.identb[:, :])
                    mm.then_inc(S("hqT_ps"), 1)
                    pe.wait_ge(S("hqT_ready"), t + 1)
                    for m in range(FT):
                        mm = pe.matmul(ps[:, 7, t * P:(t + 1) * P], hqT[:, t % 2, m * P:(m + 1) * P],
                                       wq["down"][:, m * D:(m + 1) * D], start=m == 0, stop=m == FT - 1)
                    mm.then_inc(S("down_ready"), 1)


def int8_ffn(C, k, ks, packed):
    nc, w, S, ps = C.nc, C.weights(k), C.sem, C.ps
    F, FT, EPS = 4 * D, 4, 1e-8
    with ExitStack() as ctx:
        sb = lambda name, shape, dt=F32: ctx.enter_context(nc.sbuf_tensor(f"int8_{name}", shape, dt))
        wr = sb("wr", [P, F])
        w1b = sb("w1b", [P, F], BF16)
        w2b = sb("w2b", [P, F], BF16)
        w1T = sb("w1T", [P, F], BF16)
        w2T = sb("w2T", [P, F], BF16)
        ws = sb("ws", [P, 2 * FT])
        wi = sb("wi", [P, 2 * FT])
        xn = sb("xn", [P, PT, D])
        xT = sb("xT", [P, TILES * P])
        xqT = sb("xqT", [P, PAIR], BF16)
        rnd = sb("rnd", [P, PAIR])
        hT = sb("hT", [P, FT, TILES * P])
        hmaxs = sb("hmaxs", [P, TILES])
        hqT = sb("hqT", [P, FT, PAIR], BF16)
        rnd2 = sb("rnd2", [P, FT, PAIR])
        m1 = sb("m1", [P, 1])
        mall = sb("mall", [P, 1])
        s1 = sb("s1", [P, 1])
        s1i = sb("s1i", [P, 1])
        su = sb("su", [P, FT])
        sui = sb("sui", [P, FT])
        bq = sb("bq", [P, FT])
        y = sb("y", [P, PAIR])
        psb = lambda bank: ps[:, bank, 0:F // 2].bitcast(BF16)

        def setup(v, L):
            L(v.memset(hmaxs[:, :], 0.0))
            for n in range(FT):
                L.tick(v.tensor_reduce(ws[:, n:n + 1], w("w1")[:, n * P:(n + 1) * P], AX.X, ALU.max, apply_absolute_value=True))
            L.tick(v.tensor_reduce(ws[:, FT:FT + 1], w("w2"), AX.X, ALU.max, apply_absolute_value=True))
            L.settle()
            n5 = FT + 1
            L(v.tensor_scalar(ws[:, 0:n5], ws[:, 0:n5], EPS, 1.0 / 127.0, ALU.max, ALU.mult))
            L(v.reciprocal(wi[:, 0:n5], ws[:, 0:n5]))
            for n in range(FT):
                L.tick(v.tensor_scalar(wr[:, n * P:(n + 1) * P], w("w1")[:, n * P:(n + 1) * P], wi[:, n:n + 1], ROUND,
                                       ALU.mult, ALU.add))
            L.settle()
            L(v.tensor_scalar(wr[:, :], wr[:, :], -ROUND, None, ALU.add))
            L(v.tensor_scalar(w1b[:, :], wr[:, :], -128.0, 127.0, ALU.max, ALU.min))
            L(v.tensor_scalar(wr[:, :], w("w2"), wi[:, FT:FT + 1], ROUND, ALU.mult, ALU.add))
            L(v.tensor_scalar(wr[:, :], wr[:, :], -ROUND, None, ALU.add))
            L(v.tensor_scalar(w2b[:, :], wr[:, :], -128.0, 127.0, ALU.max, ALU.min))

        def scale_and_bias(v, L, wcols, bias, n):
            L(v.tensor_scalar(s1[:, :], mall[:, :], EPS, 1.0 / 255.0, ALU.max, ALU.mult))
            L(v.reciprocal(s1i[:, :], s1[:, :]))
            L(v.tensor_scalar(su[:, 0:n], wcols, s1[:, 0:1], None, ALU.mult))
            L(v.reciprocal(sui[:, 0:n], su[:, 0:n]))
            L(v.tensor_tensor(bq[:, 0:n], bias, sui[:, 0:n], ALU.mult))
            L(v.tensor_scalar(bq[:, 0:n], bq[:, 0:n], ROUND, None, ALU.add))
            L(v.tensor_scalar(bq[:, 0:n], bq[:, 0:n], -ROUND, None, ALU.add))
            L(v.tensor_tensor(bq[:, 0:n], bq[:, 0:n], su[:, 0:n], ALU.mult))

        start_sublayer(C, k, ks, packed, setup)

        with C.turn() as block:

            @block.tensor
            def _(pe):
                for bank, src in ((0, w1b), (1, w2b)):
                    for n in range(FT):
                        mm = pe.transpose(psb(bank)[:, n * P:(n + 1) * P], src[:, n * P:(n + 1) * P], C.identb[:, :])
                    mm.then_inc(S("weights_turned"), 1)

            @block.scalar
            def _(a):
                for bank, dst in ((0, w1T), (1, w2T)):
                    a.wait_ge(S("weights_turned"), bank + 1)
                    a.activation(dst[:, :], psb(bank), ACT.Copy).then_inc(S("weights_copied"), 1)

        with nc.Fori(0, PAIRS) as i, C.turn() as block:

            @block.vector
            def _(v):
                norm_pair(v, Link(v, S("vector_step")), C, i, xn, S("xn_ready"))

            @block.scalar
            def _(a):
                a.wait_ge(S("hT_ps"), 1)
                a.activation(xT[:, bass.ds(i * PAIR, PAIR)], ps[:, 0, :], ACT.Copy).then_inc(S("hT_ready"), 1)

            @block.tensor
            def _(pe):
                turn_tiles(pe, C, 0, xn, S("xn_ready"), S("hT_ps"))

        def whole_max(block, src, wcols, bias, n):
            @block.vector
            def _(v):
                L = Link(v, S("vector_step"))
                v.tensor_reduce(m1[:, :], src, AX.X, ALU.max).then_inc(S("row_max"), 1)
                v.wait_ge(S("all_max"), 1)
                scale_and_bias(v, L, wcols, bias, n)

            @block.gpsimd
            def _(g):
                g.wait_ge(S("row_max"), 1)
                g.partition_all_reduce(mall[:, :], m1[:, :], P, bass.bass_isa.ReduceOp.max).then_inc(S("all_max"), 1)

        with C.turn() as block:
            whole_max(block, xT[:, :], ws[:, 0:FT], w("b1"), FT)

        with nc.Fori(0, PAIRS) as i, C.turn() as block:

            @block.vector
            def _(v):
                L = Link(v, S("vector_step"))
                L(v.tensor_scalar(rnd[:, :], xT[:, bass.ds(i * PAIR, PAIR)], s1i[:, 0:1], ROUND, ALU.mult, ALU.add))
                L(v.tensor_scalar(rnd[:, :], rnd[:, :], -ROUND, None, ALU.add))
                v.tensor_scalar(xqT[:, :], rnd[:, :], 0.0, 255.0, ALU.max, ALU.min).then_inc(S("xq_ready"), 1)
                for m in range(FT):
                    v.wait_ge(S("h_ready"), m + 1)
                    L.tick(v.tensor_reduce(hmaxs[:, bass.ds(i * FT + m, 1)],
                                           hT[:, m, bass.ds(i * PAIR, PAIR)], AX.X, ALU.max))
                L.settle()

            @block.scalar
            def _(a):
                for m in range(FT):
                    a.wait_ge(S("up_ready"), m + 1)
                    a.activation(hT[:, m, bass.ds(i * PAIR, PAIR)], ps[:, m, :], ACT.Relu, bias=bq[:, m:m + 1],
                                 scale=su[:, m:m + 1]).then_inc(S("h_ready"), 1)

            @block.tensor
            def _(pe):
                pe.wait_ge(S("xq_ready"), 1)
                for m in range(FT):
                    pe.matmul(ps[:, m, :], w1T[:, m * P:(m + 1) * P], xqT[:, :], start=True, stop=True)\
                      .then_inc(S("up_ready"), 1)

        with C.turn() as block:
            whole_max(block, hmaxs[:, :], ws[:, FT:FT + 1], w("b2"), 1)

        with nc.Fori(0, PAIRS) as i, C.turn() as block:

            @block.vector
            def _(v):
                L = Link(v, S("vector_step"))
                for m in range(FT):
                    L.tick(v.tensor_scalar(rnd2[:, m, :], hT[:, m, bass.ds(i * PAIR, PAIR)], s1i[:, 0:1], ROUND,
                                           ALU.mult, ALU.add))
                L.settle()
                for m in range(FT):
                    L.tick(v.tensor_scalar(rnd2[:, m, :], rnd2[:, m, :], -ROUND, None, ALU.add))
                L.settle()
                for m in range(FT):
                    v.tensor_scalar(hqT[:, m, :], rnd2[:, m, :], 0.0, 255.0, ALU.max, ALU.min).then_inc(S("hq_ready"), 1)
                v.wait_ge(S("y_turned"), 1)
                L(v.tensor_tensor(C.xt(i, 0, PT), C.xt(i, 0, PT), ps[:, 1, :], ALU.add))

            @block.scalar
            def _(a):
                a.wait_ge(S("down_ready"), 1)
                a.activation(y[:, :], ps[:, 0, :], ACT.Identity, bias=bq[:, 0:1], scale=su[:, 0:1]).then_inc(S("y_ready"), 1)

            @block.tensor
            def _(pe):
                for m in range(FT):
                    pe.wait_ge(S("hq_ready"), m + 1)
                    mm = pe.matmul(ps[:, 0, :], w2T[:, m * P:(m + 1) * P], hqT[:, m, :], start=m == 0, stop=m == FT - 1)
                mm.then_inc(S("down_ready"), 1)
                pe.wait_ge(S("y_ready"), 1)
                for t in range(PT):
                    mm = pe.transpose(ps[:, 1, t * P:(t + 1) * P], y[:, t * P:(t + 1) * P], C.ident)
                mm.then_inc(S("y_turned"), 1)


def wide_attention(C, k, ks, packed, maskd):
    nc, w, S, ps = C.nc, C.weights(k), C.sem, C.ps
    DK, M = 64, 8
    with ExitStack() as ctx:
        sb = lambda name, shape, dt=F32: ctx.enter_context(nc.sbuf_tensor(f"wide_{name}", shape, dt))
        xn = sb("xn", [P, PT, D])
        hT = sb("hT", [P, PAIR])
        cT = sb("cT", [P, PAIR])
        q = sb("q", [P, M, SEQ])
        kk = sb("k", [P, M, SEQ])
        V = sb("v", [P, 2, M * P])
        mask = sb("mask", [P, 1, 2, SEQ])
        sc = sb("sc", [P, 2, 2, SEQ])
        mx = sb("mx", [P, 2, 2])
        nm = sb("nm", [P, 2, 2])
        sums = sb("sums", [P, 2, 2])
        inv = sb("inv", [P, 2, 2])
        pr = sb("pr", [P, 2, 2, SEQ])
        diag = sb("diag", [P, 2, 2, P])
        prT = sb("prT", [P, 2, 2, SEQ])
        attT = sb("attT", [P, M, SEQ])
        start_sublayer(C, k, ks, packed)
        H = HEADS
        with nc.Fori(0, SEQS) as i, C.turn() as block:

            @block.sync
            def _(sp):
                sp.dma_start(mask[:, 0, :, :], maskd[:, bass.ds(i * 2 * SEQ, 2 * SEQ)]
                             .rearrange("p (t n) -> p t n", t=2)).then_inc(S("mask_loaded"), 16)

            @block.gpsimd
            def _(g):
                g.tensor_copy(cT[:, 0:SEQ], C.ctxT[:, bass.ds(i * SEQ, SEQ)]).then_inc(S("context_ready"), 1)

            @block.vector
            def _(v):
                L = Link(v, S("vector_step"))
                xs = [C.x[:, bass.ds(i * SEQ + t * D, D)] for t in range(2)]
                moments(v, L, C, xs)
                rsqrt(v, L, C, C.rstd[:, 0:2], C.mv[:, 0:2, 1], LN_EPS)
                for t in range(2):
                    v.tensor_scalar(xn[:, t, :], xs[t], C.mv[:, t, 0:1], C.rstd[:, t:t + 1],
                                    ALU.subtract, ALU.mult).then_inc(S("xn_ready"), 1)
                for n in range(4):
                    v.wait_ge(S("v_proj"), n + 1)
                    cols = slice((n % 2) * 512, (n % 2) * 512 + 512)
                    v.tensor_tensor(V[:, n // 2, cols], ps[:, 4 + n, :], w("bv")[:, cols], ALU.add)\
                     .then_inc(S("v_ready"), 1)
                v.wait_ge(S("mask_loaded"), 16)

                def masked(h):
                    v.wait_ge(S("scores_ready"), h + 1)
                    if h >= 2:
                        v.wait_ge(S("exp_done"), h - 1)
                    for qt in range(2):
                        L.tick(v.tensor_tensor_reduce(out=sc[:, h % 2, qt, :], in0=ps[:, h % 2, qt * SEQ:(qt + 1) * SEQ],
                                                      in1=mask[:, 0, qt, :], scale=1.0, scalar=-3.0e38, op0=ALU.add,
                                                      op1=ALU.max, accum_out=mx[:, h % 2, qt:qt + 1]))
                    L.settle()
                    v.tensor_scalar(nm[:, h % 2, :], mx[:, h % 2, :], -1.0, None, ALU.mult).then_inc(S("masked"), 1)

                def diagonal(h):
                    v.wait_ge(S("exp_done"), h + 1)
                    if h >= 2:
                        v.wait_ge(S("prT_ps"), h - 1)
                    L(v.reciprocal(inv[:, h % 2, :], sums[:, h % 2, :]))
                    L.tick(v.tensor_scalar(diag[:, h % 2, 0, :], C.ident, inv[:, h % 2, 0:1], None, ALU.mult))
                    v.tensor_scalar(diag[:, h % 2, 1, :], C.ident, inv[:, h % 2, 1:2], None, ALU.mult)\
                     .then_inc(S("diag_ready"), 1)

                def turned(h):
                    v.wait_ge(S("prT_ps"), h + 1)
                    if h >= 2:
                        v.wait_ge(S("pv_ready"), h - 1)
                    v.tensor_copy(prT[:, h % 2, :, :].rearrange("p t n -> p (t n)"), ps[:, 2 + h % 2, :])\
                     .then_inc(S("prT_ready"), 1)

                for h in range(H + 2):
                    if h < H:
                        masked(h)
                    if 1 <= h <= H:
                        diagonal(h - 1)
                    if h >= 2:
                        turned(h - 2)
                v.wait_ge(S("out_ready"), 1)
                xp = C.x[:, bass.ds(i * SEQ, SEQ)]
                L(v.tensor_tensor(xp, xp, ps[:, 6, 0:SEQ], ALU.add))
                x3 = xp.rearrange("p (t d) -> p t d", d=D)
                L(v.tensor_tensor(x3, x3, bcast(w("bo"), 1, [P, 2, D]), ALU.add))

            @block.scalar
            def _(a):
                a.wait_ge(S("hT_ps"), 1)
                a.activation(hT[:, 0:SEQ], ps[:, 0, 0:SEQ], ACT.Copy).then_inc(S("hT_ready"), 1)
                for m in range(M):
                    a.wait_ge(S("qk_proj"), m + 1)
                    a.activation(q[:, m, :], ps[:, m % 4, 0:SEQ], ACT.Identity, bias=w("bq")[:, m:m + 1])\
                     .then_inc(S("scalar_step"), 1)
                    a.activation(kk[:, m, :], ps[:, m % 4, SEQ:2 * SEQ], ACT.Identity, bias=w("bk")[:, m:m + 1])\
                     .then_inc(S("qk_copied"), 1)
                    a.wait_ge(S("scalar_step"), m + 1)
                    a.activation(q[:, m, :], q[:, m, :], ACT.Copy, scale=DK ** -0.5).then_inc(S("qk_ready"), 1)

                def exps(h):
                    a.wait_ge(S("masked"), h + 1)
                    if h >= 2:
                        a.wait_ge(S("diag_ready"), h - 1)
                        a.wait_ge(S("prT_ps"), h - 1)
                    for qt in range(2):
                        ins = a.activation(pr[:, h % 2, qt, :], sc[:, h % 2, qt, :], ACT.Exp, bias=nm[:, h % 2, qt:qt + 1],
                                           accum_out=sums[:, h % 2, qt:qt + 1])
                    ins.then_inc(S("exp_done"), 1)

                def att_copy(m):
                    a.wait_ge(S("pv_ready"), 2 * m + 2)
                    a.activation(attT[:, m, :], ps[:, 4 + m % 2, 0:SEQ], ACT.Copy).then_inc(S("attT_ready"), 1)

                for h in range(H):
                    exps(h)
                    if h >= 5 and h % 2:
                        att_copy((h - 5) // 2)
                for m in range((H - 5 + 1) // 2, M):
                    att_copy(m)

            @block.tensor
            def _(pe):
                for t in range(2):
                    pe.wait_ge(S("xn_ready"), t + 1)
                    mm = pe.transpose(ps[:, 0, t * P:(t + 1) * P], xn[:, t, :], C.ident)
                mm.then_inc(S("hT_ps"), 1)
                pe.wait_ge(S("context_ready"), 1)
                for n in range(4):
                    pe.matmul(ps[:, 4 + n, :], cT[:, (n // 2) * P:(n // 2 + 1) * P], w("wv")[:, (n % 2) * 512:(n % 2 + 1) * 512],
                              start=True, stop=True).then_inc(S("v_proj"), 1)
                pe.wait_ge(S("hT_ready"), 1)
                for m in range(M):
                    if m >= 4:
                        pe.wait_ge(S("qk_copied"), m - 3)
                    pe.matmul(ps[:, m % 4, 0:SEQ], w("wq")[:, m * P:(m + 1) * P], hT[:, 0:SEQ], start=True, stop=True)
                    pe.matmul(ps[:, m % 4, SEQ:2 * SEQ], w("wk")[:, m * P:(m + 1) * P], cT[:, 0:SEQ], start=True, stop=True)\
                      .then_inc(S("qk_proj"), 1)
                pe.wait_ge(S("qk_ready"), M)
                pe.wait_ge(S("v_ready"), 4)

                def scores(h):
                    if h >= 2:
                        pe.wait_ge(S("masked"), h - 1)
                    r = slice(DK * (h % 2), DK * (h % 2) + DK)
                    for qt in range(2):
                        mm = pe.matmul(ps[:, h % 2, qt * SEQ:(qt + 1) * SEQ], q[r, h // 2, qt * P:(qt + 1) * P],
                                       kk[r, h // 2, :], start=True, stop=True)
                    mm.then_inc(S("scores_ready"), 1)

                def turn(h):
                    pe.wait_ge(S("diag_ready"), h + 1)
                    if h >= 2:
                        pe.wait_ge(S("prT_ready"), h - 1)
                    for kt in range(2):
                        for qt in range(2):
                            mm = pe.matmul(ps[:, 2 + h % 2, kt * SEQ + qt * P:kt * SEQ + (qt + 1) * P],
                                           pr[:, h % 2, qt, kt * P:(kt + 1) * P], diag[:, h % 2, qt, :],
                                           start=True, stop=True)
                    mm.then_inc(S("prT_ps"), 1)

                def weigh(h):
                    pe.wait_ge(S("prT_ready"), h + 1)
                    m = h // 2
                    if m >= 2 and h % 2 == 0:
                        pe.wait_ge(S("attT_ready"), m - 1)
                    r = slice(DK * (h % 2), DK * (h % 2) + DK)
                    for kt in range(2):
                        mm = pe.matmul(ps[r, 4 + m % 2, 0:SEQ], V[:, kt, h * DK:(h + 1) * DK], prT[:, h % 2, kt, :],
                                       start=kt == 0, stop=kt == 1)
                    mm.then_inc(S("pv_ready"), 1)

                for h in range(H + 3):
                    if h < H:
                        scores(h)
                    if 2 <= h < H + 2:
                        turn(h - 2)
                    if h >= 3:
                        weigh(h - 3)
                pe.wait_ge(S("attT_ready"), M)
                for t in range(2):
                    for m in range(M):
                        mm = pe.matmul(ps[:, 6, t * P:(t + 1) * P], attT[:, m, t * P:(t + 1) * P],
                                       w("wo")[:, m * D:(m + 1) * D], start=m == 0, stop=m == M - 1)
                mm.then_inc(S("out_ready"), 1)


def decoder(nc, xd, ctxTd, boundary, maskd, packed, layout, out, ks):
    with ExitStack() as ctx:
        C = Core(nc, ctx, layout, ks)
        with C.turn() as block:
            @block.sync
            def _(sp):
                sp.dma_start(C.x[:, :].rearrange("p (t d) -> p t d", d=D),
                             xd.rearrange("(t p) d -> p t d", p=P)).then_inc(C.loaded, 16)
                sp.dma_start(C.const[:, :], packed["const"]).then_inc(C.loaded, 16)
                load_weights(C, sp, ks[0], packed)
                sp.dma_start(C.ctxT[:, :], ctxTd).then_inc(C.loaded, 16)

            @block.vector
            def _(v):
                v.wait_ge(C.loaded, 48)
                v.tensor_copy(C.identb[:, :], C.ident).then_inc(C.sem("vector_step"), 1)
        run = {
            0: lambda k: self_attention0(C, k, ks, packed),
            1: lambda k: attend8(C, k, ks, packed, cross=True),
            2: lambda k: sinkhorn_moe(C, k, ks, packed),
            3: lambda k: flow_attention(C, k, ks, packed),
            4: lambda k: attend8(C, k, ks, packed, cross=True, boundary=boundary),
            5: lambda k: bit_ffn(C, k, ks, packed),
            6: lambda k: relu_attention(C, k, ks, packed),
            7: lambda k: wide_attention(C, k, ks, packed, maskd),
            8: lambda k: top2_moe(C, k, ks, packed),
            9: lambda k: block_attention(C, k, ks, packed),
            10: lambda k: attend8(C, k, ks, packed, cross=True),
            11: lambda k: int8_ffn(C, k, ks, packed),
        }
        for k in ks:
            run[k](k)
        with nc.Block() as block:
            @block.sync
            def _(sp):
                sp.dma_start(out.rearrange("(t p) d -> p t d", p=P),
                             C.x[:, :].rearrange("p (t d) -> p t d", d=D)).then_inc(C.stored, 16)
                sp.wait_ge(C.stored, 16)


def self_attention0(C, k, ks, packed):
    with C.nc.sbuf_tensor("inner", [P, TILES * D], F32) as inner:
        attend8(C, k, ks, packed, cross=False, rope=True, causal=True, inner=inner)
        swiglu(C, k, inner)


KS = list(range(12))


def padded(wt, swap=False):
    wt = wt.reshape(wt.shape[0], GROUPS, 4, HD)
    if swap:
        wt = wt[..., [1, 0, 3, 2, 5, 4, 7, 6]]
    o = np.zeros((wt.shape[0], GROUPS, 4, 32), wt.dtype)
    o[..., :HD] = wt
    return o.reshape(wt.shape[0], GROUPS * P)


def padded_bias(b, aug):
    o = np.zeros((GROUPS, 4, 32), b.dtype)
    o[..., :HD] = b.reshape(GROUPS, 4, HD)
    o[..., AUG] = aug
    return np.ascontiguousarray(o.reshape(GROUPS, P).T)


def rows(b):
    return np.broadcast_to(b.reshape(1, -1), (P, b.size))


def tiles(wt):
    return np.ascontiguousarray(wt.reshape(-1, P, wt.shape[1]).transpose(1, 0, 2)).reshape(P, -1)


def columns(b):
    return np.ascontiguousarray(b.reshape(-1, P).T)


def constants():
    f = np.float32
    r = np.arange(P)
    head = r // HD
    pos = np.arange(SEQ, dtype=np.float32)
    kd = (np.arange(HD) // 2).astype(np.float32)
    ang = pos[:, None] / np.power(f(10000.0), f(2.0) * kd / f(HD))
    cos, sin = np.cos(ang).astype(f), np.sin(ang).astype(f)
    sin = sin * np.where(np.arange(HD) % 2 == 0, -1.0, 1.0).astype(f)

    def feature_major(tab):
        o = np.zeros((4, 32, SEQ), f)
        o[:, :HD, :] = tab.T
        return np.tile(o.reshape(P, SEQ), (1, 2))

    def token_major(tab):
        return np.tile(tab.reshape(2, P, 1, HD), (1, 1, HEADS, 1)).transpose(1, 0, 2, 3).reshape(P, 2 * D)

    aug = np.zeros((4, 32), f)
    aug[:, AUG] = 1.0
    return {
        "ident": np.eye(P, dtype=f), "ones": np.ones((P, P), f), "zeros": np.zeros((P, SEQ), f),
        "causalT": np.where(r[:, None] > r[None, :], NEG, 0.0).astype(f),
        "block": (head[:, None] == head[None, :]).astype(f),
        "heads": (head[:, None] == np.arange(HEADS)[None, :]).astype(f),
        "position": np.stack([r, r + P], 1).astype(f),
        "aug": aug.reshape(P, 1),
        "cosF": feature_major(cos), "sinF": feature_major(sin),
        "cosT": token_major(cos), "sinT": token_major(sin),
        "first": rows(np.arange(8, 0, -1).astype(f)),
    }


def pack(a):
    def attn(pre, wq, wk, wv, wo, bq, bk, bv, bo, transpose):
        t = (lambda m: a[pre + m].T) if transpose else (lambda m: a[pre + m])
        return {"wq": padded(t(wq)), "wk": padded(t(wk)), "wv": t(wv), "wo": t(wo),
                "bq": padded_bias(a[pre + bq], 0.0), "bk": padded_bias(a[pre + bk], 1.0),
                "bv": rows(a[pre + bv]), "bo": rows(a[pre + bo])}

    def experts(m):
        e, kk, n = m.shape
        return m.reshape(e, kk // P, P, n).transpose(2, 0, 1, 3).reshape(P, -1)

    def few(m):
        o = np.zeros((P, m.shape[1]), m.dtype)
        o[:m.shape[0]] = m
        return o

    parts = {
        "const": constants(),
        "L0_attn": {"wq": padded(a["L0_attn_wq"].T), "wq_swapped": padded(a["L0_attn_wq"].T, True),
                    "wk": padded(a["L0_attn_wk"].T), "wk_swapped": padded(a["L0_attn_wk"].T, True),
                    "wv": a["L0_attn_wv"].T, "wo": a["L0_attn_wo"].T,
                    "norm1": columns(a["L0_attn_norm1_w"]), "norm2": columns(a["L0_attn_norm2_w"]),
                    "w1": a["L0_attn_w1"].T, "w3": a["L0_attn_w3"].T, "w2": tiles(a["L0_attn_w2"].T)},
        "L0_xattn": attn("L0_xattn_", "Wq", "Wk", "Wv", "Wo", "bq", "bk", "bv", "bo", True),
        "L0_ffn": {"router": a["L0_ffn_router_w"].T, "router_b": rows(a["L0_ffn_router_b"]),
                   "temperature": rows(a["L0_ffn_temperature"]), "wg": experts(a["L0_ffn_wg"]),
                   "wp": experts(a["L0_ffn_wp"]), "wo": experts(a["L0_ffn_wo"])},
        "L1_attn": {"qkv": a["L1_attn_qkv_w"].T, "qkv_b": rows(a["L1_attn_qkv_b"]),
                    "proj": a["L1_attn_proj_w"].T, "proj_b": rows(a["L1_attn_proj_b"])},
        "L1_xattn": attn("L1_xattn_", "wq", "wk", "wv", "wo", "bq", "bk", "bv", "bo", True),
        "L1_ffn": {"gate": a["L1_ffn_w_gate"].T, "up": a["L1_ffn_w_up"].T, "down": tiles(a["L1_ffn_w_down"].T)},
        "L2_attn": {"qkv": a["L2_attn_Wqkv"].T, "qkv_b": rows(a["L2_attn_bqkv"]),
                    "gq": rows(a["L2_attn_gq"]), "gk": rows(a["L2_attn_gk"]), "gout": rows(a["L2_attn_gout"]),
                    "proj": a["L2_attn_Wout"].T, "proj_b": rows(a["L2_attn_bout"])},
        "L2_xattn": {"wq": a["L2_xattn_Wq"], "wk": a["L2_xattn_Wk"], "wv": a["L2_xattn_Wv"],
                     "wo": tiles(a["L2_xattn_Wo"]), "bq": columns(a["L2_xattn_bq"]), "bk": columns(a["L2_xattn_bk"]),
                     "bv": rows(a["L2_xattn_bv"]), "bo": rows(a["L2_xattn_bo"])},
        "L2_ffn": {"gate": a["L2_ffn_gate_w"], "gate_b": rows(a["L2_ffn_gate_b"]),
                   "w1": experts(a["L2_ffn_w1"]), "w2": experts(a["L2_ffn_w2"]), "wg": experts(a["L2_ffn_wg"]),
                   "w3": experts(a["L2_ffn_w3"]),
                   "b1": columns(a["L2_ffn_b1"].reshape(-1)), "b2": columns(a["L2_ffn_b2"].reshape(-1)),
                   "bg": columns(a["L2_ffn_bg"].reshape(-1)), "b3": few(a["L2_ffn_b3"])},
        "L3_attn": {"qkv": a["L3_attn_qkv_w"].T, "proj": a["L3_attn_proj_w"].T, "proj_b": rows(a["L3_attn_proj_b"])},
        "L3_xattn": attn("L3_xattn_", "Wq", "Wk", "Wv", "Wo", "bq", "bk", "bv", "bo", False),
        "L3_ffn": {"w1": tiles(a["L3_ffn_w1"]), "w2": a["L3_ffn_w2"],
                   "b1": columns(a["L3_ffn_b1"]), "b2": columns(a["L3_ffn_b2"])},
    }
    layout, packed = {}, {}
    for name, part in parts.items():
        at, layout[name] = 0, {}
        for key, m in part.items():
            layout[name][key] = (at, m.shape[1])
            at += m.shape[1]
        layout[name]["_width"] = at
        packed[name] = np.ascontiguousarray(np.concatenate(list(part.values()), axis=1))
    return layout, packed


def kernel(**inputs):
    import concourse.bacc as _bacc
    from concourse.bass_utils import run_bass_kernel_spmd as _run

    a = {n: np.asarray(m) for n, m in inputs.items()}
    layout, packed = pack(a)
    nc = _bacc.Bacc("TRN2", target_bir_lowering=False, num_devices=1)
    arrays = {
        "x": a["x"].reshape(SEQS * SEQ, D),
        "ctxT": np.ascontiguousarray(a["ctx_1024"].reshape(SEQS * SEQ, D).T),
        "boundary": a["mask_BxS_ik0"].reshape(1, SEQS * SEQ),
        "mask": np.ascontiguousarray(a["mask_Bx1xSxS2_ff0"].reshape(SEQS, 2, P, 2 * P).transpose(2, 0, 1, 3)
                                      .reshape(P, -1)),
    }
    for name in ["const"] + [SUBLAYERS[k] for k in KS]:
        arrays["packed_" + name] = packed[name]
    dram = {n: nc.dram_tensor("in_" + n, m.shape, mybir.dt.from_np(m.dtype), kind="ExternalInput").ap()
            for n, m in arrays.items()}
    out = nc.dram_tensor("out_0", (SEQS * SEQ, D), F32, kind="ExternalOutput").ap()
    decoder(nc, dram["x"], dram["ctxT"], dram["boundary"], dram["mask"],
            {n[7:]: ap for n, ap in dram.items() if n.startswith("packed_")}, layout, out, KS)
    r = _run(nc, [{"in_" + n: m for n, m in arrays.items()}], core_ids=[0])
    return r.results[0]["out_0"].reshape(SEQS, SEQ, D)
```

```python
from contextlib import ExitStack, contextmanager

import numpy as np

import concourse.bass as bass
from concourse import mybir

P = 128
SEQS, SEQ, D = 8, 256, 128
TILES = SEQS * SEQ // P
PT = 4
PAIR = PT * P
PAIRS = TILES // PT
HEADS, HD = 16, 8
GROUPS = 4
Q_PARTS, K_PARTS = (0, 0, 1, 1, 0, 2), (0, 1, 0, 1, 2, 0)
AUG = 8 * len(Q_PARTS)
NEG = -1.0e30
LN_EPS = 1e-5

ALU = mybir.AluOpType
ACT = mybir.ActivationFunctionType
AX = mybir.AxisListType
F32 = mybir.dt.float32
BF16 = mybir.dt.bfloat16
I32 = mybir.dt.int32

SUBLAYERS = ["L0_attn", "L0_xattn", "L0_ffn", "L1_attn", "L1_xattn", "L1_ffn",
             "L2_attn", "L2_xattn", "L2_ffn", "L3_attn", "L3_xattn", "L3_ffn"]


class Link:

    def __init__(self, eng, sem):
        self.eng, self.sem, self.n = eng, sem, 0

    def tick(self, ins):
        self.n += 1
        ins.then_inc(self.sem, 1)

    def settle(self):
        self.eng.wait_ge(self.sem, self.n)

    def __call__(self, ins):
        self.tick(ins)
        self.settle()


class Core:

    def __init__(self, nc, ctx, layout, ks):
        self.nc, self.layout, self.ks = nc, layout, ks
        sb = lambda name, shape, dt=F32: ctx.enter_context(nc.sbuf_tensor(name, shape, dt))
        self.x = sb("x", [P, TILES * D])
        self.ctxT = sb("ctxT", [P, TILES * P])
        self.const = sb("const", [P, layout["const"]["_width"]])
        self.identb = sb("identb", [P, P], BF16)
        widths = [[layout[SUBLAYERS[k]]["_width"] for k in ks[r::2]] or [1] for r in range(2)]
        self.regions = [sb(f"weights_{r}", [P, max(widths[r])]) for r in range(2)]
        self.stats = sb("stats", [P, PT, 6])
        self.mv = sb("mv", [P, PT, 2])
        self.rstd = sb("rstd", [P, PT])
        self.nwt = [sb("newton_a", [P, 64]), sb("newton_v", [P, 64])]
        self.ps = ctx.enter_context(nc.psum_tensor("ps", [P, 8, 512], F32))
        self.lay = sb("lay", [P, 2, 3, HEADS * 64], BF16)
        self.loaded = ctx.enter_context(nc.semaphore("loaded"))
        self.stored = ctx.enter_context(nc.semaphore("stored"))
        self.weights_loaded = [ctx.enter_context(nc.semaphore(f"weights_loaded_{n}")) for n in SUBLAYERS]
        self.sems, self.ctx = {}, ctx
        self.ident = self.c("ident")

    def c(self, name):
        o, n = self.layout["const"][name]
        return self.const[:, o:o + n]

    def psb(self, bank):
        return self.ps[:, bank, 0:256].bitcast(BF16)

    def sem(self, name):
        if name not in self.sems:
            self.sems[name] = self.ctx.enter_context(self.nc.semaphore(name))
        return self.sems[name]

    def region(self, k):
        return self.regions[self.ks.index(k) % 2]

    def weights(self, k):
        region, lay = self.region(k), self.layout[SUBLAYERS[k]]
        return lambda name: region[:, lay[name][0]:lay[name][0] + lay[name][1]]

    def xt(self, i, t, n=1):
        return self.x[:, bass.ds(i * PAIR + t * D, n * D)]

    @contextmanager
    def turn(self):
        with self.nc.Block() as block:
            yield block
        nums = [s.num for s in self.sems.values()]
        if nums:
            self.nc.sync.sem_clear(range(min(nums), max(nums) + 1))
            self.nc.all_engine_barrier()


def bcast(ap, axis, shape):
    return ap.unsqueeze(axis).to_broadcast(shape)


def load_weights(C, eng, k, packed):
    w = C.layout[SUBLAYERS[k]]["_width"]
    h = w // 2
    for a, b in ((0, h), (h, w)):
        eng.dma_start(C.region(k)[:, a:b], packed[SUBLAYERS[k]][:, a:b]).then_inc(C.weights_loaded[k], 16)


def start_sublayer(C, k, ks, packed, setup=None):
    nc = C.nc
    with C.turn() as block:
        @block.sync
        def _(sp):
            at = ks.index(k)
            if at + 1 < len(ks):
                load_weights(C, sp, ks[at + 1], packed)

        @block.vector
        def _(v):
            v.wait_ge(C.weights_loaded[k], 32)
            if setup:
                setup(v, Link(v, C.sem("vector_step")))


def rsqrt(v, L, C, out, var, eps):
    n = out.shape[1]
    a, vv = C.nwt[0][:, 0:n], C.nwt[1][:, 0:n]
    L(v.tensor_scalar(vv, var, eps, None, ALU.add))
    L(v.tensor_scalar(out.bitcast(I32), vv.bitcast(I32), -0.5, 1597463007.0, ALU.mult, ALU.add))
    for _ in range(3):
        L(v.scalar_tensor_tensor(a, out, -0.5, out, ALU.mult, ALU.mult))
        L(v.tensor_tensor(a, a, vv, ALU.mult))
        L(v.scalar_tensor_tensor(out, a, 1.5, out, ALU.add, ALU.mult))


def moments(v, L, C, tiles):
    for t, ap in enumerate(tiles):
        L.tick(v.bn_stats(C.stats[:, t, :], ap))
    L.settle()
    for t in range(len(tiles)):
        L.tick(v.bn_aggr(C.mv[:, t, :], C.stats[:, t, :]))
    L.settle()


def norm_pair(v, L, C, i, xn, ready):
    moments(v, L, C, [C.xt(i, t) for t in range(PT)])
    rsqrt(v, L, C, C.rstd[:, :], C.mv[:, :, 1], LN_EPS)
    for t in range(PT):
        v.tensor_scalar(xn[:, t, :], C.xt(i, t), C.mv[:, t, 0:1], C.rstd[:, t:t + 1],
                        ALU.subtract, ALU.mult).then_inc(ready, 1)


def turn_tiles(pe, C, bank, src, ready, done):
    for t in range(PT):
        pe.wait_ge(ready, t + 1)
        ins = pe.transpose(C.ps[:, bank, t * P:(t + 1) * P], src[:, t, :], C.ident)
    ins.then_inc(done, 1)


def attend8(C, k, ks, packed, *, cross, rope=False, causal=False, boundary=None, inner=None):
    nc, w = C.nc, C.weights(k)
    GP, SLOTS = HEADS // 2, HEADS
    RING = 4
    EARLY = (3, 5)
    with ExitStack() as ctx:
        sb = lambda name, shape, dt=F32: ctx.enter_context(nc.sbuf_tensor(f"{SUBLAYERS[k]}_{name}", shape, dt))
        xn = sb("xn", [P, PT, D])
        hn = sb("hn", [P, PT, D]) if rope else xn
        hT = sb("hT", [P, PAIR])
        kvT = sb("kvT", [P, PAIR]) if cross else hT
        full = sb("full", [P, 2, PAIR])
        parts = sb("parts", [P, 2, 3, PAIR], BF16)
        rest = sb("rest", [P, 2, PAIR])
        qs = sb("qs", [P, GP, 2, PAIR], BF16)
        kk = sb("ks", [P, GP, PAIR], BF16)
        V = sb("v", [P, PT, HEADS, 32])
        nmax = sb("nmax", [P, 2, 2, 2])
        maxs = sb("maxs", [P, 2, 2, P], BF16)
        probs = sb("probs", [P, RING, 2, 2, SEQ])
        pv = sb("pv", [P, 2, SEQ])
        sums = sb("sums", [P, 2, 4])
        att = sb("att", [P, PT, D])
        attT = sb("attT", [P, PAIR])
        rotc = sb("rotc", [P, 2, PAIR]) if rope else None
        maskT = None
        if causal:
            maskT = sb("maskT", [P, 1, P], BF16)
        if boundary is not None:
            maskT = sb("maskT", [P, 4, SEQ], BF16)
            bnd = sb("bnd", [P, PAIR], I32)
            bndf = sb("bndf", [P, PAIR])
            idx = sb("idx", [P, PAIR])
        masked = boundary is not None or causal
        ps = C.ps

        def setup(v, L):
            L.tick(v.memset(V[:, :, :, HD:HD + 1], 1.0))
            L.tick(v.memset(V[:, :, :, HD + 1:32], 0.0))
            L.tick(v.memset(maxs[:], 0.0))
            L.tick(v.memset(qs[:], 0.0))
            if causal:
                L.tick(v.tensor_copy(maskT[:, 0, :], C.c("causalT")))
            L.settle()

        start_sublayer(C, k, ks, packed, setup)
        scores_bank = lambda s: 2 * (s % 3)
        slots = [(s // GP, s % GP) for s in range(SLOTS)]
        half = [slice(64 * j, 64 * j + 64) for j in range(2)]
        S = C.sem
        with nc.Fori(0, PAIRS) as i, C.turn() as block:

            @block.sync
            def _(sp):
                if boundary is not None:
                    sp.dma_start(bnd[:, :], boundary[0:1, bass.ds(i * PAIR, PAIR)].to_broadcast([P, PAIR]))\
                      .then_inc(S("boundary_loaded"), 16)

            @block.gpsimd
            def _(g):
                if cross:
                    g.tensor_copy(kvT[:, :], C.ctxT[:, bass.ds(i * PAIR, PAIR)]).then_inc(S("context_ready"), 1)

            @block.vector
            def _(v):
                L = Link(v, S("vector_step"))
                if rope:
                    moments(v, L, C, [C.xt(i, t) for t in range(PT)])
                    rsqrt(v, L, C, C.rstd[:, :], C.mv[:, :, 1], LN_EPS)
                    for t in range(PT):
                        L.tick(v.tensor_scalar(xn[:, t, :], C.xt(i, t), C.mv[:, t, 0:1], C.rstd[:, t:t + 1],
                                               ALU.subtract, ALU.mult))
                    L.settle()
                    moments(v, L, C, [xn[:, t, :] for t in range(PT)])
                    L(v.tensor_tensor(C.mv[:, :, 0], C.mv[:, :, 0], C.mv[:, :, 0], ALU.mult))
                    L(v.tensor_tensor(C.mv[:, :, 1], C.mv[:, :, 1], C.mv[:, :, 0], ALU.add))
                    rsqrt(v, L, C, C.rstd[:, :], C.mv[:, :, 1], 1e-5)
                    for t in range(PT):
                        v.tensor_scalar(hn[:, t, :], xn[:, t, :], C.rstd[:, t:t + 1], None, ALU.mult)\
                         .then_inc(S("xn_ready"), 1)
                else:
                    norm_pair(v, L, C, i, xn, S("xn_ready"))
                for n in range(2):
                    if rope:
                        v.wait_ge(S("proj_ready"), n + 1)
                        L.tick(v.tensor_tensor(rotc[:, 0, :], ps[:, 3 * n, :], C.c("cosF"), ALU.mult))
                        L.tick(v.tensor_tensor(rotc[:, 1, :], ps[:, 3 * n + 1, :], C.c("sinF"), ALU.mult))
                        L.settle()
                        L(v.tensor_tensor(full[:, n, :], rotc[:, 0, :], rotc[:, 1, :], ALU.add))
                        L(v.tensor_copy(parts[:, n, 0, :], full[:, n, :]))
                    else:
                        v.wait_ge(S("first_part"), n + 1)
                    L(v.tensor_tensor(rest[:, n, :], full[:, n, :], parts[:, n, 0, :], ALU.subtract))
                    L(v.tensor_copy(parts[:, n, 1, :], rest[:, n, :]))
                    v.tensor_tensor(parts[:, n, 2, :], rest[:, n, :], parts[:, n, 1, :], ALU.subtract)\
                     .then_inc(S("parts_ready"), 1)
                v.wait_ge(S("v_proj"), 1)
                src = ps[:, 2, :].rearrange("p (t h d) -> p t h d", t=PT, d=HD)
                if rope:
                    v.tensor_copy(V[:, :, :, 0:HD], src).then_inc(S("v_ready"), 1)
                else:
                    bv = w("bv").rearrange("p (h d) -> p h d", d=HD)
                    v.tensor_tensor(V[:, :, :, 0:HD], src, bcast(bv, 1, [P, PT, HEADS, HD]), ALU.add)\
                     .then_inc(S("v_ready"), 1)
                if boundary is not None:
                    v.wait_ge(S("boundary_loaded"), 16)
                    L(v.tensor_copy(bndf[:, :], bnd[:, :]))
                    for b in range(2):
                        cols = slice(b * SEQ, (b + 1) * SEQ)
                        L.tick(v.tensor_tensor_scan(idx[:, cols], bndf[:, cols], C.c("zeros"), 0.0, ALU.add, ALU.add))
                    L.settle()
                    for b in range(2):
                        for kt in range(2):
                            v.tensor_scalar(maskT[:, 2 * b + kt, :], idx[:, b * SEQ:(b + 1) * SEQ],
                                            C.c("position")[:, kt:kt + 1], NEG, ALU.is_lt, ALU.mult)\
                             .then_inc(S("mask_ready"), 1)

                def maximum(s):
                    v.wait_ge(S("m_ready"), s + 1)
                    b0 = scores_bank(s)
                    nm = nmax[:, s % 2, :, :]
                    if causal:
                        L.tick(v.tensor_reduce(nm[:, :, 0], ps[:, b0:b0 + 2, 0:P], AX.X, ALU.max, negate=True))
                        v.tensor_reduce(nm[:, :, 1], ps[:, b0:b0 + 2, SEQ:2 * SEQ], AX.X, ALU.max, negate=True)\
                         .then_inc(S("m_used"), 1)
                        L.settle()
                    else:
                        v.tensor_reduce(nm, ps[:, b0:b0 + 2, :].rearrange("p j (t n) -> p j t n", t=2), AX.X, ALU.max,
                                        negate=True).then_inc(S("m_used"), 1)
                    v.wait_ge(S("m_used"), s + 1)
                    rows_ = maxs[:, s % 2, :, :].rearrange("p t (j r) -> p j t r", j=2)
                    L(v.tensor_copy(rows_[:, :, :, AUG], nm))
                    v.tensor_tensor(rows_[:, :, :, AUG + 1], nm, rows_[:, :, :, AUG], ALU.subtract)\
                     .then_inc(S("maxs_ready"), 1)

                def add_max(s):
                    b, gp = slots[s]
                    v.wait_ge(S("maxT_ready"), s + 1)
                    cols = slice(b * SEQ, (b + 1) * SEQ)
                    for j in range(2):
                        qh = qs[half[j], gp, j, cols]
                        ins = v.tensor_tensor(qh, qh, C.psb(6)[half[j], 0:SEQ], ALU.add)
                    ins.then_inc(S("max_in_q"), 1)

                def normalise(g):
                    v.wait_ge(S("pv_turned"), g + 1)
                    src = ps[:, 7, SEQ:2 * SEQ].rearrange("p (t j e) -> p t j e", t=2, e=32)
                    L(v.reciprocal(sums[:, :, :], src[:, :, :, HD]))
                    b, h0 = g // GROUPS, (g % GROUPS) * 4 * HD
                    dst = att[:, 2 * b:2 * b + 2, h0:h0 + 4 * HD].rearrange("p t (j d) -> p t j d", d=HD)
                    v.tensor_tensor(dst, src[:, :, :, 0:HD], bcast(sums[:, :, :], 3, [P, 2, 4, HD]), ALU.mult)\
                     .then_inc(S("normalised"), 1)

                for gp in range(GP):
                    v.wait_ge(S("k_laid"), gp + 1)
                    v.tensor_scalar(kk[:, gp, :], ps[:, 5 + gp % 2, :], C.c("aug"), None, ALU.add)\
                     .then_inc(S("k_ready"), 1)
                    if gp in EARLY:
                        maximum(EARLY.index(gp))
                for s in range(SLOTS + 5):
                    if s >= 6 and s % 2 == 0:
                        normalise((s - 6) // 2)
                    if len(EARLY) <= s < SLOTS:
                        maximum(s)
                    if 1 <= s <= SLOTS:
                        add_max(s - 1)
                v.wait_ge(S("out_ready"), 1)
                o, xs = ps[:, 1, :], C.xt(i, 0, PT)
                if inner is not None:
                    y = inner[:, bass.ds(i * PAIR, PAIR)]
                    L(v.tensor_tensor(y, xn[:, :, :].rearrange("p t d -> p (t d)"), o, ALU.add))
                    L(v.tensor_tensor(xs, xs, y, ALU.add))
                else:
                    x3 = xs.rearrange("p (t d) -> p t d", d=D)
                    L(v.tensor_tensor(xs, xs, o, ALU.add))
                    L(v.tensor_tensor(x3, x3, bcast(w("bo"), 1, [P, PT, D]), ALU.add))

            @block.scalar
            def _(a):
                a.wait_ge(S("hT_ps"), 1)
                if rope:
                    a.activation(hT[:, :], ps[:, 7, :], ACT.Copy, scale=w("norm1")).then_inc(S("hT_ready"), 1)
                else:
                    a.activation(hT[:, :], ps[:, 7, :], ACT.Copy).then_inc(S("hT_ready"), 1)
                    for n, bias in enumerate(("bq", "bk")):
                        a.wait_ge(S("proj_ready"), n + 1)
                        a.activation(full[:, n, :], ps[:, 3 * n, :], ACT.Identity, bias=w(bias))
                        a.activation(parts[:, n, 0, :], ps[:, 3 * n, :], ACT.Identity, bias=w(bias))\
                         .then_inc(S("first_part"), 1)
                for gp in range(GP):
                    a.wait_ge(S("q_laid"), gp + 1)
                    for j in range(2):
                        ins = a.activation(qs[half[j], gp, j, :], ps[half[j], (4, 7)[gp % 2], :], ACT.Copy)
                    ins.then_inc(S("q_ready"), 1)

                def exps(s):
                    a.wait_ge(S("p_ready"), s + 1)
                    if s >= RING:
                        a.wait_ge(S("pv_ready"), (s - RING) // 2 + 1)
                    b0 = scores_bank(s)
                    if causal:
                        a.activation(probs[:, s % RING, :, 0, :], ps[:, b0:b0 + 2, 0:SEQ], ACT.Exp, scale=HD ** -0.5)
                        a.activation(probs[:, s % RING, :, 1, P:SEQ], ps[:, b0:b0 + 2, SEQ + P:2 * SEQ], ACT.Exp,
                                     scale=HD ** -0.5).then_inc(S("probs_ready"), 1)
                    else:
                        a.activation(probs[:, s % RING, :, :, :].rearrange("p j t n -> p j (t n)"),
                                     ps[:, b0:b0 + 2, :], ACT.Exp, scale=HD ** -0.5).then_inc(S("probs_ready"), 1)

                def copy_pv(g):
                    a.wait_ge(S("pv_ready"), g + 1)
                    a.activation(pv[:, g % 2, :], ps[:, 7, 0:SEQ], ACT.Copy).then_inc(S("pv_copied"), 1)

                for s in range(SLOTS + 2):
                    if s >= 3 and s % 2:
                        copy_pv((s - 3) // 2)
                    if s < SLOTS:
                        exps(s)
                a.wait_ge(S("attT_ps"), 1)
                a.activation(attT[:, :], ps[:, 0, :], ACT.Copy).then_inc(S("attT_ready"), 1)

            @block.tensor
            def _(pe):
                turn_tiles(pe, C, 7, hn, S("xn_ready"), S("hT_ps"))
                pe.wait_ge(S("hT_ready"), 1)
                if cross:
                    pe.wait_ge(S("context_ready"), 1)
                for n, (wt, src) in enumerate((("wq", hT), ("wk", kvT))):
                    mm = pe.matmul(ps[:, 3 * n, :], w(wt), src[:, :], start=True, stop=True)
                    if rope:
                        mm = pe.matmul(ps[:, 3 * n + 1, :], w(wt + "_swapped"), src[:, :], start=True, stop=True)
                    mm.then_inc(S("proj_ready"), 1)
                for t in range(PT):
                    mm = pe.matmul(ps[:, 2, t * P:(t + 1) * P], kvT[:, t * P:(t + 1) * P], w("wv"),
                                   start=True, stop=True)
                mm.then_inc(S("v_proj"), 1)

                def max_scores(s):
                    b, gp = slots[s]
                    b0 = scores_bank(s)
                    if s >= 3:
                        pe.wait_ge(S("probs_ready"), s - 2)
                    for qt in range(2):
                        q0, c = b * SEQ + qt * P, qt * SEQ
                        nk = P if causal and qt == 0 else SEQ
                        if masked:
                            for j in range(2):
                                if causal:
                                    pe.matmul(ps[:, b0 + j, c + nk - P:c + nk], maskT[:, 0, :], C.identb[:, :],
                                              start=qt == 0, stop=False, skip_group_check=True)
                                else:
                                    for kt in range(2):
                                        pe.matmul(ps[:, b0 + j, c + kt * P:c + (kt + 1) * P],
                                                  maskT[:, 2 * b + kt, qt * P:(qt + 1) * P], C.identb[:, :],
                                                  start=qt == 0 and kt == 0, stop=False, skip_group_check=True)
                        for j in range(2):
                            for c0, c1 in ([(0, nk)] if not (causal and qt) else [(0, P), (P, SEQ)]):
                                mm = pe.matmul(ps[:, b0 + j, c + c0:c + c1], qs[:, gp, j, q0:q0 + P],
                                               kk[:, gp, b * SEQ + c0:b * SEQ + c1], start=not masked,
                                               stop=True, skip_group_check=masked)
                    mm.then_inc(S("m_ready"), 1)

                def turn_max(s):
                    pe.wait_ge(S("maxs_ready"), s + 1)
                    if s:
                        pe.wait_ge(S("max_in_q"), s)
                    for qt in range(2):
                        mm = pe.transpose(C.psb(6)[:, qt * P:(qt + 1) * P], maxs[:, s % 2, qt, :], C.identb[:, :])
                    mm.then_inc(S("maxT_ready"), 1)

                def prob_scores(s):
                    b, gp = slots[s]
                    b0 = scores_bank(s)
                    pe.wait_ge(S("max_in_q"), s + 1)
                    for kt in range(2):
                        k0, c = b * SEQ + kt * P, kt * SEQ
                        if masked:
                            for j in range(2):
                                if causal:
                                    pe.matmul(ps[:, b0 + j, c + kt * P:c + kt * P + P], C.identb[:, :], maskT[:, 0, :],
                                              start=kt == 0, stop=False, skip_group_check=True)
                                else:
                                    pe.matmul(ps[:, b0 + j, c:c + SEQ], C.identb[:, :], maskT[:, 2 * b + kt, :],
                                              start=kt == 0, stop=False, skip_group_check=True)
                        for j in range(2):
                            for c0, c1 in ([(0, SEQ)] if not causal else ([(0, P), (P, SEQ)] if kt == 0 else [(P, SEQ)])):
                                mm = pe.matmul(ps[:, b0 + j, c + c0:c + c1], kk[:, gp, k0:k0 + P],
                                               qs[:, gp, j, b * SEQ + c0:b * SEQ + c1],
                                               start=not masked, stop=True, skip_group_check=True)
                    mm.then_inc(S("p_ready"), 1)

                def weigh_values(g):
                    b = g // GROUPS
                    pe.wait_ge(S("probs_ready"), 2 * g + 2)
                    if g:
                        pe.wait_ge(S("pv_copied"), g)
                        pe.wait_ge(S("normalised"), g)
                    for kt in range(2):
                        q0 = P if causal and kt else 0
                        for j in range(4):
                            mm = pe.matmul(ps[32 * j:32 * j + 32, 7, q0:SEQ], V[:, 2 * b + kt, (g % GROUPS) * 4 + j, :],
                                           probs[:, (2 * g + j // 2) % RING, j % 2, kt, q0:SEQ],
                                           start=kt == 0, stop=kt == 1, skip_group_check=causal,
                                           tile_position=(0, 32 * j))
                    mm.then_inc(S("pv_ready"), 1)

                def turn_values(g):
                    pe.wait_ge(S("pv_copied"), g + 1)
                    for t in range(2):
                        mm = pe.transpose(ps[:, 7, SEQ + t * P:SEQ + (t + 1) * P], pv[:, g % 2, t * P:(t + 1) * P], C.ident)
                    mm.then_inc(S("pv_turned"), 1)

                pe.wait_ge(S("parts_ready"), 2)
                for gp in range(GP):
                    for n, (bank, ready, laid) in enumerate((((4, 7)[gp % 2], "q_ready", "q_laid"),
                                                             (5 + gp % 2, "k_ready", "k_laid"))):
                        if gp >= 2:
                            pe.wait_ge(S(ready), gp - 1)
                        for p in range(3):
                            mm = pe.matmul(ps[:, bank, :], C.lay[:, n, p, gp * P:(gp + 1) * P], parts[:, n, p, :],
                                           start=p == 0, stop=p == 2)
                        mm.then_inc(S(laid), 1)
                    if gp in EARLY:
                        if gp == EARLY[0]:
                            pe.wait_ge(S("v_ready"), 1)
                            if boundary is not None:
                                pe.wait_ge(S("mask_ready"), 4)
                        pe.wait_ge(S("q_ready"), EARLY.index(gp) + 1)
                        pe.wait_ge(S("k_ready"), EARLY.index(gp) + 1)
                        max_scores(EARLY.index(gp))
                pe.wait_ge(S("q_ready"), GP)
                pe.wait_ge(S("k_ready"), GP)
                for s in range(SLOTS + 4):
                    if 2 <= s < SLOTS + 2:
                        turn_max(s - 2)
                    if len(EARLY) <= s < SLOTS:
                        max_scores(s)
                    if 2 <= s < SLOTS + 2:
                        prob_scores(s - 2)
                    if s >= 5 and s % 2:
                        turn_values((s - 5) // 2)
                    if s >= 4 and s % 2 == 0:
                        weigh_values((s - 4) // 2)
                pe.wait_ge(S("normalised"), 2 * GROUPS)
                for t in range(PT):
                    mm = pe.transpose(ps[:, 0, t * P:(t + 1) * P], att[:, t, :], C.ident)
                mm.then_inc(S("attT_ps"), 1)
                pe.wait_ge(S("attT_ready"), 1)
                for t in range(PT):
                    mm = pe.matmul(ps[:, 1, t * P:(t + 1) * P], attT[:, t * P:(t + 1) * P], w("wo"),
                                   start=True, stop=True)
                mm.then_inc(S("out_ready"), 1)


def swiglu(C, k, y):
    nc, w, S, ps = C.nc, C.weights(k), C.sem, C.ps
    FT = 4
    with ExitStack() as ctx:
        sb = lambda name, shape, dt=F32: ctx.enter_context(nc.sbuf_tensor(f"swiglu_{name}", shape, dt))
        hn = sb("hn", [P, PT, D])
        hT = sb("hT", [P, PAIR])
        gate = sb("gate", [P, 2, PAIR])
        gated = sb("gated", [P, FT, PAIR])
        with nc.Fori(0, PAIRS) as i, C.turn() as block:

            @block.vector
            def _(v):
                L = Link(v, S("vector_step"))
                yt = [y[:, bass.ds(i * PAIR + t * D, D)] for t in range(PT)]
                moments(v, L, C, yt)
                L(v.tensor_tensor(C.mv[:, :, 0], C.mv[:, :, 0], C.mv[:, :, 0], ALU.mult))
                L(v.tensor_tensor(C.mv[:, :, 1], C.mv[:, :, 1], C.mv[:, :, 0], ALU.add))
                rsqrt(v, L, C, C.rstd[:, :], C.mv[:, :, 1], 1e-5)
                for t in range(PT):
                    v.tensor_scalar(hn[:, t, :], yt[t], C.rstd[:, t:t + 1], None, ALU.mult).then_inc(S("xn_ready"), 1)
                for m in range(FT):
                    v.wait_ge(S("gate_ready"), m + 1)
                    v.tensor_tensor(gated[:, m, :], gate[:, m % 2, :], ps[:, 3 + m % 2, :], ALU.mult)\
                     .then_inc(S("gated_ready"), 1)
                v.wait_ge(S("down_ready"), 1)
                L(v.tensor_tensor(C.xt(i, 0, PT), C.xt(i, 0, PT), ps[:, 5, :], ALU.add))

            @block.scalar
            def _(a):
                a.wait_ge(S("hT_ps"), 1)
                a.activation(hT[:, :], ps[:, 0, :], ACT.Copy, scale=w("norm2")).then_inc(S("hT_ready"), 1)
                for m in range(FT):
                    a.wait_ge(S("up_ready"), m + 1)
                    if m >= 2:
                        a.wait_ge(S("gated_ready"), m - 1)
                    a.activation(gate[:, m % 2, :], ps[:, 1 + m % 2, :], ACT.Silu).then_inc(S("gate_ready"), 1)

            @block.tensor
            def _(pe):
                turn_tiles(pe, C, 0, hn, S("xn_ready"), S("hT_ps"))
                pe.wait_ge(S("hT_ready"), 1)
                for m in range(FT):
                    if m >= 2:
                        pe.wait_ge(S("gated_ready"), m - 1)
                    pe.matmul(ps[:, 1 + m % 2, :], w("w1")[:, m * P:(m + 1) * P], hT[:, :], start=True, stop=True)
                    pe.matmul(ps[:, 3 + m % 2, :], w("w3")[:, m * P:(m + 1) * P], hT[:, :], start=True, stop=True)\
                      .then_inc(S("up_ready"), 1)
                pe.wait_ge(S("gated_ready"), FT)
                for t in range(PT):
                    for m in range(FT):
                        mm = pe.matmul(ps[:, 5, t * P:(t + 1) * P], gated[:, m, t * P:(t + 1) * P],
                                       w("w2")[:, m * D:(m + 1) * D], start=m == 0, stop=m == FT - 1)
                mm.then_inc(S("down_ready"), 1)


def choose_two(v, L, C, g, sel, top, n, tmp):
    m, c, cm = tmp
    first = bcast(C.c("first"), 1, [P, n, 8])
    for s in range(2):
        src = g if s == 0 else m
        L(v.tensor_reduce(top[:, s, :], src, AX.X, ALU.max))
        L(v.tensor_tensor(c, src, bcast(top[:, s, :], 2, [P, n, 8]), ALU.is_equal))
        L(v.tensor_tensor(c, c, first, ALU.mult))
        L(v.tensor_reduce(cm, c, AX.X, ALU.max))
        L(v.tensor_tensor(sel[:, s, :, :], c, bcast(cm, 2, [P, n, 8]), ALU.is_equal))
        if s == 0:
            L(v.scalar_tensor_tensor(m, sel[:, 0, :, :], -3.0e38, g, ALU.mult, ALU.add))


def sinkhorn_moe(C, k, ks, packed):
    nc, w, S, ps = C.nc, C.weights(k), C.sem, C.ps
    E, FT, ROUNDS = 8, 2, 3
    with ExitStack() as ctx:
        sb = lambda name, shape, dt=F32: ctx.enter_context(nc.sbuf_tensor(f"moe0_{name}", shape, dt))
        xn = sb("xn", [P, PT, D])
        hT = sb("hT", [P, PAIR])
        la = sb("la", [P, TILES, E])
        ex = sb("ex", [P, TILES, E])
        st = sb("st", [P, 4, TILES])
        packed_la = sb("packed_la", [P, 2, SEQS * E])
        laT = sb("laT", [SEQS * E, 2 * P])
        exT = sb("exT", [SEQS * E, 2 * P])
        stT = sb("stT", [SEQS * E, 4])
        sel = sb("sel", [P, 2, TILES, E])
        top = sb("top", [P, 2, TILES])
        cw = sb("cw", [P, TILES, E])
        cwp = sb("cwp", [P, PT, E])
        g_sb = sb("g_sb", [P, 2, FT, PAIR])
        h_sb = sb("h_sb", [P, 2, FT, PAIR])
        acc = sb("acc", [P, PAIR])
        tmp = (sb("tm", [P, TILES, E]), sb("tc", [P, TILES, E]), sb("tcm", [P, TILES]))
        itemp = sb("itemp", [P, 1])

        def setup(v, L):
            L(v.tensor_scalar(itemp[:, :], w("temperature"), 0.1, None, ALU.max))
            L(v.reciprocal(itemp[:, :], itemp[:, :]))

        start_sublayer(C, k, ks, packed, setup)

        with nc.Fori(0, PAIRS) as i, C.turn() as block:

            @block.vector
            def _(v):
                L = Link(v, S("vector_step"))
                norm_pair(v, L, C, i, xn, S("xn_ready"))
                v.wait_ge(S("logits_ready"), 1)
                lg = la[:, bass.ds(i * PT, PT), :]
                L(v.tensor_tensor(lg, ps[:, 1, 0:PT * E].rearrange("p (t e) -> p t e", e=E),
                                  bcast(w("router_b"), 1, [P, PT, E]), ALU.add))
                L(v.tensor_scalar(lg, lg, itemp[:, 0:1], None, ALU.mult))

            @block.scalar
            def _(a):
                a.wait_ge(S("hT_ps"), 1)
                a.activation(hT[:, :], ps[:, 0, :], ACT.Copy).then_inc(S("hT_ready"), 1)

            @block.tensor
            def _(pe):
                turn_tiles(pe, C, 0, xn, S("xn_ready"), S("hT_ps"))
                pe.wait_ge(S("hT_ready"), 1)
                for t in range(PT):
                    mm = pe.matmul(ps[:, 1, t * E:(t + 1) * E], hT[:, t * P:(t + 1) * P], w("router"),
                                   start=True, stop=True)
                mm.then_inc(S("logits_ready"), 1)

        with C.turn() as block:

            @block.vector
            def _(v):
                L = Link(v, S("vector_step"))
                mx, sm = st[:, 0, :], st[:, 1, :]
                back = ps[:, 2, 0:2 * SEQS * E].rearrange("p (t b e) -> p b t e", t=2, e=E)
                la4 = la[:, :, :].rearrange("p (b t) e -> p b t e", t=2)
                for r in range(ROUNDS):
                    if r:
                        v.wait_ge(S("turned_back"), r)
                        L(v.tensor_copy(la4, back))
                    L(v.tensor_reduce(mx, la[:, :, :], AX.X, ALU.max))
                    v.tensor_tensor(la[:, :, :], la[:, :, :], bcast(mx, 2, [P, TILES, E]), ALU.subtract)\
                     .then_inc(S("shifted"), 1)
                    v.wait_ge(S("expd"), r + 1)
                    v.tensor_reduce(sm, ex[:, :, :], AX.X, ALU.add).then_inc(S("summed"), 1)
                    v.wait_ge(S("logd"), r + 1)
                    v.tensor_tensor(packed_la[:, :, :].rearrange("p t (b e) -> p b t e", e=E), la4,
                                    bcast(st[:, 3, :].rearrange("p (b t) -> p b t", t=2), 3, [P, SEQS, 2, E]),
                                    ALU.subtract).then_inc(S("rows_done"), 1)
                    v.wait_ge(S("turned"), r + 1)
                    L(v.tensor_copy(laT[:, :], ps[0:SEQS * E, 3, 0:2 * P]))
                    v.tensor_reduce(stT[:, 0:1], laT[:, :], AX.X, ALU.max, negate=True).then_inc(S("max_done"), 1)
                    v.wait_ge(S("lse_done"), r + 1)
                    v.wait_ge(S("max_done"), r + 1)
                    L(v.tensor_tensor(stT[:, 3:4], stT[:, 0:1], stT[:, 2:3], ALU.subtract))
                    v.tensor_scalar(laT[:, :], laT[:, :], stT[:, 3:4], None, ALU.add).then_inc(S("cols_done"), 1)
                v.wait_ge(S("gates"), 1)
                L(v.tensor_reduce(sm, ex[:, :, :], AX.X, ALU.add))
                L(v.tensor_scalar(sm, sm, 1e-8, None, ALU.add))
                L(v.reciprocal(sm, sm))
                L(v.tensor_tensor(ex[:, :, :], ex[:, :, :], bcast(sm, 2, [P, TILES, E]), ALU.mult))
                choose_two(v, L, C, ex[:, :, :], sel, top, TILES, (tmp[0][:, :, :], tmp[1][:, :, :], tmp[2][:, :]))
                L(v.tensor_tensor(sm, top[:, 0, :], top[:, 1, :], ALU.add))
                L(v.tensor_scalar(sm, sm, 1e-8, None, ALU.add))
                L(v.reciprocal(sm, sm))
                L(v.tensor_tensor(cw[:, :, :], sel[:, 0, :, :], sel[:, 1, :, :], ALU.add))
                L(v.tensor_tensor(cw[:, :, :], cw[:, :, :], ex[:, :, :], ALU.mult))
                L(v.tensor_tensor(cw[:, :, :], cw[:, :, :], bcast(sm, 2, [P, TILES, E]), ALU.mult))

            @block.scalar
            def _(a):
                for r in range(ROUNDS):
                    a.wait_ge(S("shifted"), r + 1)
                    a.activation(ex[:, :, :], la[:, :, :], ACT.Exp).then_inc(S("expd"), 1)
                    a.wait_ge(S("summed"), r + 1)
                    a.activation(st[:, 3, :], st[:, 1, :], ACT.Ln).then_inc(S("logd"), 1)
                    a.wait_ge(S("max_done"), r + 1)
                    a.activation(exT[:, :], laT[:, :], ACT.Exp, bias=stT[:, 0:1],
                                 accum_out=stT[:, 1:2]).then_inc(S("scalar_step"), 1)
                    a.wait_ge(S("scalar_step"), r + 1)
                    a.activation(stT[:, 2:3], stT[:, 1:2], ACT.Ln).then_inc(S("lse_done"), 1)
                a.wait_ge(S("turned_back"), ROUNDS)
                a.activation(ex[:, :, :].rearrange("p (b t) e -> p b t e", t=2),
                             ps[:, 2, 0:2 * SEQS * E].rearrange("p (t b e) -> p b t e", t=2, e=E),
                             ACT.Exp).then_inc(S("gates"), 1)

            @block.tensor
            def _(pe):
                n = SEQS * E
                for r in range(ROUNDS):
                    pe.wait_ge(S("rows_done"), r + 1)
                    for tt in range(2):
                        mm = pe.transpose(ps[0:n, 3, tt * P:(tt + 1) * P], packed_la[:, tt, :], C.ident)
                    mm.then_inc(S("turned"), 1)
                    pe.wait_ge(S("cols_done"), r + 1)
                    for tt in range(2):
                        mm = pe.transpose(ps[:, 2, tt * n:(tt + 1) * n], laT[:, tt * P:(tt + 1) * P],
                                          C.ident[0:n, 0:n])
                    mm.then_inc(S("turned_back"), 1)

        with nc.Fori(0, PAIRS) as i, C.turn() as block:

            @block.vector
            def _(v):
                L = Link(v, S("vector_step"))
                L.tick(v.tensor_copy(cwp[:, :, :], cw[:, bass.ds(i * PT, PT), :]))
                norm_pair(v, L, C, i, xn, S("xn_ready"))
                L.settle()
                accs = [acc[:, t * P:(t + 1) * P] for t in range(PT)]

                def down(e):
                    v.wait_ge(S("down_ready"), e + 1)
                    for t in range(PT):
                        ins = v.scalar_tensor_tensor(accs[t], ps[:, 5 + e % 2, t * P:(t + 1) * P], cwp[:, t, e:e + 1],
                                                     xn[:, t, :] if e == 0 else accs[t], ALU.mult, ALU.add)
                        L.tick(ins) if t < PT - 1 else ins.then_inc(S("combined"), 1)
                    v.wait_ge(S("combined"), e + 1)

                v.wait_ge(S("xn_ready"), PT)
                for e in range(E):
                    for f in range(FT):
                        v.wait_ge(S("g_ready"), FT * e + f + 1)
                        if e >= 2 and f == 0:
                            v.wait_ge(S("down_ready"), e - 1)
                        v.tensor_tensor(h_sb[:, e % 2, f, :], g_sb[:, e % 2, f, :], ps[:, 3 + f, :], ALU.mult)\
                         .then_inc(S("h_ready"), 1)
                    if e:
                        down(e - 1)
                down(E - 1)
                L(v.tensor_tensor(C.xt(i, 0, PT), C.xt(i, 0, PT), acc[:, :], ALU.add))

            @block.scalar
            def _(a):
                a.wait_ge(S("hT_ps"), 1)
                a.activation(hT[:, :], ps[:, 0, :], ACT.Copy).then_inc(S("hT_ready"), 1)
                for e in range(E):
                    for f in range(FT):
                        a.wait_ge(S("up_ready"), FT * e + f + 1)
                        if e >= 2:
                            a.wait_ge(S("h_ready"), FT * (e - 2) + f + 1)
                        a.activation(g_sb[:, e % 2, f, :], ps[:, 1 + f, :], ACT.Relu).then_inc(S("g_ready"), 1)

            @block.tensor
            def _(pe):
                turn_tiles(pe, C, 0, xn, S("xn_ready"), S("hT_ps"))
                pe.wait_ge(S("hT_ready"), 1)

                def down(e):
                    pe.wait_ge(S("h_ready"), FT * (e + 1))
                    if e >= 2:
                        pe.wait_ge(S("combined"), e - 1)
                    for t in range(PT):
                        for f in range(FT):
                            mm = pe.matmul(ps[:, 5 + e % 2, t * P:(t + 1) * P], h_sb[:, e % 2, f, t * P:(t + 1) * P],
                                           w("wo")[:, (e * FT + f) * D:(e * FT + f + 1) * D],
                                           start=f == 0, stop=f == FT - 1)
                    mm.then_inc(S("down_ready"), 1)

                for e in range(E):
                    for f in range(FT):
                        if e:
                            pe.wait_ge(S("h_ready"), FT * (e - 1) + f + 1)
                        col = slice((e * FT + f) * P, (e * FT + f + 1) * P)
                        pe.matmul(ps[:, 1 + f, :], w("wg")[:, col], hT[:, :], start=True, stop=True)
                        pe.matmul(ps[:, 3 + f, :], w("wp")[:, col], hT[:, :], start=True, stop=True)\
                          .then_inc(S("up_ready"), 1)
                    if e:
                        down(e - 1)
                down(E - 1)


def top2_moe(C, k, ks, packed):
    nc, w, S, ps = C.nc, C.weights(k), C.sem, C.ps
    E, FT = 8, 2
    with ExitStack() as ctx:
        sb = lambda name, shape, dt=F32: ctx.enter_context(nc.sbuf_tensor(f"moe2_{name}", shape, dt))
        xn = sb("xn", [P, PT, D])
        hT = sb("hT", [P, PAIR])
        lg = sb("lg", [P, PT, E])
        sel = sb("sel", [P, 2, PT, E])
        top = sb("top", [P, 2, PT])
        pr = sb("pr", [P, 2, PT])
        cw = sb("cw", [P, PT, E])
        cwT = sb("cwT", [E, PAIR])
        one = sb("one", [P, PT])
        a_sb = sb("a_sb", [P, 2, PAIR])
        z_sb = sb("z_sb", [P, FT, PAIR])
        s_sb = sb("s_sb", [P, 2, FT, PAIR])
        acc = sb("acc", [P, PAIR])
        tmp = (sb("tm", [P, PT, E]), sb("tc", [P, PT, E]), sb("tcm", [P, PT]))
        start_sublayer(C, k, ks, packed)
        with nc.Fori(0, PAIRS) as i, C.turn() as block:

            @block.vector
            def _(v):
                L = Link(v, S("vector_step"))
                norm_pair(v, L, C, i, xn, S("xn_ready"))
                v.wait_ge(S("logits_ready"), 1)
                L(v.tensor_tensor(lg[:, :, :], ps[:, 7, 0:PT * E].rearrange("p (t e) -> p t e", e=E),
                                  bcast(w("gate_b"), 1, [P, PT, E]), ALU.add))
                choose_two(v, L, C, lg[:, :, :], sel, top, PT, (tmp[0][:, :, :], tmp[1][:, :, :], tmp[2][:, :]))
                v.tensor_tensor(pr[:, 1, :], top[:, 1, :], top[:, 0, :], ALU.subtract).then_inc(S("gap_ready"), 1)
                v.wait_ge(S("gap_exp"), 1)
                L(v.tensor_scalar(one[:, :], pr[:, 0, :], 1.0, None, ALU.add))
                L(v.reciprocal(one[:, :], one[:, :]))
                L(v.tensor_tensor(pr[:, 1, :], pr[:, 0, :], one[:, :], ALU.mult))
                L(v.tensor_tensor(cw[:, :, :], sel[:, 0, :, :], bcast(one[:, :], 2, [P, PT, E]), ALU.mult))
                L(v.tensor_tensor(tmp[0][:, :, :], sel[:, 1, :, :], bcast(pr[:, 1, :], 2, [P, PT, E]), ALU.mult))
                v.tensor_tensor(cw[:, :, :], cw[:, :, :], tmp[0][:, :, :], ALU.add).then_inc(S("weights_ready"), 1)
                v.wait_ge(S("weights_ready"), 1)
                v.wait_ge(S("cwT_ps"), 1)
                v.tensor_copy(cwT[:, :], ps[0:E, 7, :]).then_inc(S("cwT_ready"), 1)
                v.wait_ge(S("bias_ready"), 1)
                v.tensor_copy(acc[:, :], ps[:, 7, :]).then_inc(S("acc_ready"), 1)
                v.wait_ge(S("acc_ready"), 1)
                accs = [acc[:, t * P:(t + 1) * P] for t in range(PT)]

                def down(e):
                    v.wait_ge(S("down_ready"), e + 1)
                    for t in range(PT):
                        ins = v.scalar_tensor_tensor(accs[t], ps[:, 7, t * P:(t + 1) * P], cw[:, t, e:e + 1],
                                                     accs[t], ALU.mult, ALU.add)
                        L.tick(ins) if t < PT - 1 else ins.then_inc(S("combined"), 1)
                    v.wait_ge(S("combined"), e + 1)

                for e in range(E):
                    for f in range(FT):
                        v.wait_ge(S("a_ready"), FT * e + f + 1)
                        if e:
                            v.wait_ge(S("mid_ready"), FT * e)
                        v.scalar_tensor_tensor(z_sb[:, f, :], ps[:, 3 + f, :], w("b2")[:, e * FT + f:e * FT + f + 1],
                                               a_sb[:, f, :], ALU.add, ALU.mult).then_inc(S("z_ready"), 1)
                    if e:
                        down(e - 1)
                down(E - 1)
                L(v.tensor_tensor(C.xt(i, 0, PT), C.xt(i, 0, PT), acc[:, :], ALU.add))

            @block.scalar
            def _(a):
                a.wait_ge(S("hT_ps"), 1)
                a.activation(hT[:, :], ps[:, 0, :], ACT.Copy).then_inc(S("hT_ready"), 1)
                a.wait_ge(S("gap_ready"), 1)
                a.activation(pr[:, 0, :], pr[:, 1, :], ACT.Exp).then_inc(S("gap_exp"), 1)
                for e in range(E):
                    for f in range(FT):
                        a.wait_ge(S("up_ready"), FT * e + f + 1)
                        if e:
                            a.wait_ge(S("z_ready"), FT * (e - 1) + f + 1)
                        a.activation(a_sb[:, f, :], ps[:, 1 + f, :], ACT.Identity,
                                     bias=w("b1")[:, e * FT + f:e * FT + f + 1]).then_inc(S("a_ready"), 1)
                    for f in range(FT):
                        a.wait_ge(S("mid_ready"), FT * e + f + 1)
                        if e >= 2:
                            a.wait_ge(S("down_ready"), e - 1)
                        a.activation(s_sb[:, e % 2, f, :], ps[:, 5 + f, :], ACT.Silu,
                                     bias=w("bg")[:, e * FT + f:e * FT + f + 1]).then_inc(S("s_ready"), 1)

            @block.tensor
            def _(pe):
                turn_tiles(pe, C, 0, xn, S("xn_ready"), S("hT_ps"))
                pe.wait_ge(S("hT_ready"), 1)
                for t in range(PT):
                    mm = pe.matmul(ps[:, 7, t * E:(t + 1) * E], hT[:, t * P:(t + 1) * P], w("gate"),
                                   start=True, stop=True)
                mm.then_inc(S("logits_ready"), 1)

                def up(e):
                    for f in range(FT):
                        if e:
                            pe.wait_ge(S("z_ready"), FT * (e - 1) + f + 1)
                        col = slice((e * FT + f) * P, (e * FT + f + 1) * P)
                        pe.matmul(ps[:, 1 + f, :], w("w1")[:, col], hT[:, :], start=True, stop=True)
                        pe.matmul(ps[:, 3 + f, :], w("w2")[:, col], hT[:, :], start=True, stop=True)\
                          .then_inc(S("up_ready"), 1)

                def mid(e):
                    pe.wait_ge(S("z_ready"), FT * (e + 1))
                    for m in range(FT):
                        if e:
                            pe.wait_ge(S("s_ready"), FT * (e - 1) + m + 1)
                        for f in range(FT):
                            c0 = (e * FT + f) * FT * P + m * P
                            mm = pe.matmul(ps[:, 5 + m, :], w("wg")[:, c0:c0 + P], z_sb[:, f, :],
                                           start=f == 0, stop=f == FT - 1)
                        mm.then_inc(S("mid_ready"), 1)

                def down(e):
                    pe.wait_ge(S("s_ready"), FT * (e + 1))
                    if e:
                        pe.wait_ge(S("combined"), e)
                    else:
                        pe.wait_ge(S("acc_ready"), 1)
                    for t in range(PT):
                        for f in range(FT):
                            mm = pe.matmul(ps[:, 7, t * P:(t + 1) * P], s_sb[:, e % 2, f, t * P:(t + 1) * P],
                                           w("w3")[:, (e * FT + f) * D:(e * FT + f + 1) * D],
                                           start=f == 0, stop=f == FT - 1)
                    mm.then_inc(S("down_ready"), 1)

                up(0)
                pe.wait_ge(S("weights_ready"), 1)
                for t in range(PT):
                    mm = pe.transpose(ps[0:E, 7, t * P:(t + 1) * P], cw[:, t, :], C.ident)
                mm.then_inc(S("cwT_ps"), 1)
                pe.wait_ge(S("cwT_ready"), 1)
                for t in range(PT):
                    mm = pe.matmul(ps[:, 7, t * P:(t + 1) * P], cwT[:, t * P:(t + 1) * P], w("b3")[0:E, :],
                                   start=True, stop=True)
                mm.then_inc(S("bias_ready"), 1)
                for e in range(E):
                    mid(e)
                    if e + 1 < E:
                        up(e + 1)
                    down(e)


def heads4(ap):
    return ap.rearrange("p t (h d) -> p t h d", d=HD)


def project_tokens(pe, C, first_bank, hT, wt, n, done):
    for t in range(PT):
        pe.matmul(C.ps[:, first_bank + t, 0:n], hT[:, t * P:(t + 1) * P], wt, start=True, stop=True)\
          .then_inc(done, 1)


def flow_attention(C, k, ks, packed):
    nc, w, S, ps = C.nc, C.weights(k), C.sem, C.ps
    EPS = 1e-6
    with ExitStack() as ctx:
        sb = lambda name, shape, dt=F32: ctx.enter_context(nc.sbuf_tensor(f"flow_{name}", shape, dt))
        xn = sb("xn", [P, PT, D])
        hT = sb("hT", [P, PAIR])
        pre = sb("pre", [P, PT, 3 * D])
        qk = sb("qk", [P, PT, 2 * D])
        qke = sb("qke", [P, PT, 2 * D])
        tot = sb("tot", [P, 2, 2 * D])
        prod = sb("prod", [P, PT, 2 * D])
        flow = sb("flow", [P, PT, 2 * HEADS])
        scaled = sb("scaled", [P, PT, 2 * D])
        cons = sb("cons", [P, PT, 2 * HEADS])
        comp = sb("comp", [P, PT, HEADS])
        csum = sb("csum", [P, 2, HEADS])
        alloc = sb("alloc", [P, PT, HEADS])
        vc = sb("vc", [P, PT, D])
        qT = sb("qT", [P, PAIR])
        kv = sb("kv", [P, 2, D])
        att = sb("att", [P, PT, D])
        attT = sb("attT", [P, PAIR])
        start_sublayer(C, k, ks, packed)
        by2 = lambda ap: ap.rearrange("p (b t) n -> p b t n", t=2)
        with nc.Fori(0, PAIRS) as i, C.turn() as block:

            @block.vector
            def _(v):
                L = Link(v, S("vector_step"))
                norm_pair(v, L, C, i, xn, S("xn_ready"))
                for t in range(PT):
                    v.wait_ge(S("qkv_ready"), t + 1)
                    v.tensor_tensor(pre[:, t, :], ps[:, t, 0:3 * D], w("qkv_b"), ALU.add).then_inc(S("biased"), 1)
                v.wait_ge(S("biased"), PT)
                v.wait_ge(S("sigmoid"), 1)
                L(v.tensor_scalar(qke[:, :, :], qk[:, :, :], EPS, None, ALU.add))

                def against_totals(n, out):
                    v.wait_ge(S("totals"), n)
                    L(v.tensor_scalar(tot[:, :, :], ps[:, 4:6, 0:2 * D], EPS, None, ALU.add))
                    for b in range(2):
                        for s in range(2):
                            L.tick(v.tensor_tensor(prod[:, 2 * b:2 * b + 2, s * D:(s + 1) * D],
                                                   qke[:, 2 * b:2 * b + 2, s * D:(s + 1) * D],
                                                   bcast(tot[:, b, (1 - s) * D:(2 - s) * D], 1, [P, 2, D]), ALU.mult))
                    L.settle()
                    L(v.tensor_reduce(out, prod[:, :, :].rearrange("p t (h d) -> p t h d", d=HD), AX.X, ALU.add))

                against_totals(1, flow[:, :, :])
                L(v.reciprocal(flow[:, :, :], flow[:, :, :]))
                v.tensor_tensor(heads4(scaled[:, :, :]), heads4(qk[:, :, :]),
                                bcast(flow[:, :, :], 3, [P, PT, 2 * HEADS, HD]), ALU.mult).then_inc(S("scaled_ready"), 1)
                v.wait_ge(S("scaled_ready"), 1)
                against_totals(2, cons[:, :, :])
                L(v.tensor_scalar(cons[:, :, :], cons[:, :, :], EPS, None, ALU.add))
                v.tensor_scalar(cons[:, :, HEADS:2 * HEADS], cons[:, :, HEADS:2 * HEADS], -1.0, 1.0,
                                ALU.max, ALU.min).then_inc(S("conserved"), 1)
                v.wait_ge(S("comp_sum"), 1)
                L(v.reciprocal(csum[:, :, :], ps[:, 6, 0:2 * HEADS].rearrange("p (b h) -> p b h", b=2)))
                L(v.tensor_scalar(csum[:, :, :], csum[:, :, :], float(SEQ), None, ALU.mult))
                for b in range(2):
                    L.tick(v.tensor_tensor(comp[:, 2 * b:2 * b + 2, :], comp[:, 2 * b:2 * b + 2, :],
                                           bcast(csum[:, b, :], 1, [P, 2, HEADS]), ALU.mult))
                L.settle()
                v.tensor_tensor(heads4(vc[:, :, :]), heads4(pre[:, :, 2 * D:3 * D]),
                                bcast(comp[:, :, :], 3, [P, PT, HEADS, HD]), ALU.mult).then_inc(S("vc_ready"), 1)
                for b in range(2):
                    v.wait_ge(S("kv_ps"), b + 1)
                    v.tensor_tensor(kv[:, b, :], ps[:, 2 + b, 0:D], C.c("block"), ALU.mult).then_inc(S("kv_ready"), 1)
                v.wait_ge(S("att_ps"), 1)
                v.wait_ge(S("alloc_ready"), 1)
                v.tensor_tensor(heads4(att[:, :, :]), heads4(ps[:, 4, :].rearrange("p (t d) -> p t d", d=D)),
                                bcast(alloc[:, :, :], 3, [P, PT, HEADS, HD]), ALU.mult).then_inc(S("att_ready"), 1)
                add_projection(v, L, C, i, w, S, 6)

            @block.scalar
            def _(a):
                a.wait_ge(S("hT_ps"), 1)
                a.activation(hT[:, :], ps[:, 7, :], ACT.Copy).then_inc(S("hT_ready"), 1)
                a.wait_ge(S("biased"), PT)
                a.activation(qk[:, :, :], pre[:, :, 0:2 * D], ACT.Sigmoid).then_inc(S("sigmoid"), 1)
                a.wait_ge(S("conserved"), 1)
                a.activation(alloc[:, :, :], cons[:, :, 0:HEADS], ACT.Sigmoid).then_inc(S("alloc_ready"), 1)
                a.activation(comp[:, :, :], cons[:, :, HEADS:2 * HEADS], ACT.Exp).then_inc(S("comp_ready"), 1)
                a.wait_ge(S("qT_ps"), 1)
                a.activation(qT[:, :], ps[:, 7, :], ACT.Copy).then_inc(S("qT_ready"), 1)
                a.wait_ge(S("attT_ps"), 1)
                a.activation(attT[:, :], ps[:, 5, :], ACT.Copy).then_inc(S("attT_ready"), 1)

            @block.tensor
            def _(pe):
                ones = C.c("ones")
                turn_tiles(pe, C, 7, xn, S("xn_ready"), S("hT_ps"))
                pe.wait_ge(S("hT_ready"), 1)
                project_tokens(pe, C, 0, hT, w("qkv"), 3 * D, S("qkv_ready"))

                def totals(src):
                    for b in range(2):
                        for t in range(2):
                            mm = pe.matmul(ps[:, 4 + b, 0:2 * D], ones, src[:, 2 * b + t, :], start=t == 0, stop=t == 1)
                    mm.then_inc(S("totals"), 1)

                pe.wait_ge(S("sigmoid"), 1)
                totals(qk)
                pe.wait_ge(S("scaled_ready"), 1)
                totals(scaled)
                for t in range(PT):
                    mm = pe.transpose(ps[:, 7, t * P:(t + 1) * P], scaled[:, t, 0:D], C.ident)
                mm.then_inc(S("qT_ps"), 1)
                pe.wait_ge(S("comp_ready"), 1)
                for b in range(2):
                    for t in range(2):
                        mm = pe.matmul(ps[:, 6, b * HEADS:(b + 1) * HEADS], ones, comp[:, 2 * b + t, :],
                                       start=t == 0, stop=t == 1)
                mm.then_inc(S("comp_sum"), 1)
                pe.wait_ge(S("vc_ready"), 1)
                for b in range(2):
                    for t in range(2):
                        mm = pe.matmul(ps[:, 2 + b, 0:D], qk[:, 2 * b + t, D:2 * D], vc[:, 2 * b + t, :],
                                       start=t == 0, stop=t == 1)
                    mm.then_inc(S("kv_ps"), 1)
                pe.wait_ge(S("qT_ready"), 1)
                pe.wait_ge(S("kv_ready"), 2)
                for t in range(PT):
                    mm = pe.matmul(ps[:, 4, t * P:(t + 1) * P], qT[:, t * P:(t + 1) * P], kv[:, t // 2, :],
                                   start=True, stop=True)
                mm.then_inc(S("att_ps"), 1)
                turn_and_project(pe, C, w, S, att, attT, 5, 6)


def turn_and_project(pe, C, w, S, att, attT, turn_bank, out_bank):
    pe.wait_ge(S("att_ready"), 1)
    for t in range(PT):
        mm = pe.transpose(C.ps[:, turn_bank, t * P:(t + 1) * P], att[:, t, :], C.ident)
    mm.then_inc(S("attT_ps"), 1)
    pe.wait_ge(S("attT_ready"), 1)
    for t in range(PT):
        mm = pe.matmul(C.ps[:, out_bank, t * P:(t + 1) * P], attT[:, t * P:(t + 1) * P], w("proj"),
                       start=True, stop=True)
    mm.then_inc(S("out_ready"), 1)


def add_projection(v, L, C, i, w, S, bank):
    v.wait_ge(S("out_ready"), 1)
    xs = C.xt(i, 0, PT)
    L(v.tensor_tensor(xs, xs, C.ps[:, bank, :], ALU.add))
    L(v.tensor_tensor(xs.rearrange("p (t d) -> p t d", d=D), xs.rearrange("p (t d) -> p t d", d=D),
                      bcast(w("proj_b"), 1, [P, PT, D]), ALU.add))


def relu_attention(C, k, ks, packed):
    nc, w, S, ps = C.nc, C.weights(k), C.sem, C.ps
    RMS_EPS, LIN_EPS = 1.1920929e-07, 1e-6
    N = D + HEADS
    with ExitStack() as ctx:
        sb = lambda name, shape, dt=F32: ctx.enter_context(nc.sbuf_tensor(f"lin_{name}", shape, dt))
        xn = sb("xn", [P, PT, D])
        hT = sb("hT", [P, PAIR])
        pre = sb("pre", [P, PT, 3 * D + 1])
        qk = sb("qk", [P, 2, PT, D])
        rot = sb("rot", [P, 2, PT, D])
        qT = sb("qT", [P, PAIR])
        kv = sb("kv", [P, 2, N])
        den = sb("den", [P, PT, HEADS])
        att = sb("att", [P, PT, D])
        attT = sb("attT", [P, PAIR])
        o = sb("o", [P, PT, D])

        def setup(v, L):
            L(v.memset(pre[:, :, 3 * D:3 * D + 1], 1.0))

        start_sublayer(C, k, ks, packed, setup)
        pairs = lambda ap: ap.rearrange("p t (c two) -> p t c two", two=2)

        def mean_square(v, L):
            L(v.tensor_tensor(C.mv[:, :, 0], C.mv[:, :, 0], C.mv[:, :, 0], ALU.mult))
            L(v.tensor_tensor(C.mv[:, :, 1], C.mv[:, :, 1], C.mv[:, :, 0], ALU.add))

        with nc.Fori(0, PAIRS) as i, C.turn() as block:

            @block.vector
            def _(v):
                L = Link(v, S("vector_step"))
                norm_pair(v, L, C, i, xn, S("xn_ready"))
                for t in range(PT):
                    v.wait_ge(S("qkv_ready"), t + 1)
                    L.tick(v.tensor_tensor(pre[:, t, 0:3 * D], ps[:, t, 0:3 * D], w("qkv_b"), ALU.add))
                L.settle()
                for s, gain in enumerate(("gq", "gk")):
                    moments(v, L, C, [pre[:, t, s * D:(s + 1) * D] for t in range(PT)])
                    mean_square(v, L)
                    rsqrt(v, L, C, C.rstd[:, :], C.mv[:, :, 1], RMS_EPS)
                    for t in range(PT):
                        L.tick(v.scalar_tensor_tensor(qk[:, s, t, :], pre[:, t, s * D:(s + 1) * D],
                                                      C.rstd[:, t:t + 1], w(gain), ALU.mult, ALU.mult))
                    L.settle()
                    cosT = C.c("cosT").rearrange("p (t d) -> p t d", t=2)
                    sinT = pairs(C.c("sinT").rearrange("p (t d) -> p t d", t=2))
                    for b in range(2):
                        tl = slice(2 * b, 2 * b + 2)
                        a2, r2 = pairs(qk[:, s, tl, :]), pairs(rot[:, s, tl, :])
                        for e in range(2):
                            L.tick(v.tensor_tensor(r2[:, :, :, e], a2[:, :, :, 1 - e], sinT[:, :, :, e], ALU.mult))
                    L.settle()
                    for b in range(2):
                        tl = slice(2 * b, 2 * b + 2)
                        L.tick(v.tensor_tensor(qk[:, s, tl, :], qk[:, s, tl, :], cosT, ALU.mult))
                    L.settle()
                    L(v.tensor_tensor(qk[:, s, :, :], qk[:, s, :, :], rot[:, s, :, :], ALU.add))
                    v.tensor_scalar(qk[:, s, :, :], qk[:, s, :, :], 0.0, None, ALU.max).then_inc(S("qk_ready"), 1)
                for b in range(2):
                    v.wait_ge(S("kv_ps"), b + 1)
                    L.tick(v.tensor_tensor(kv[:, b, 0:D], ps[:, 4 + b, 0:D], C.c("block"), ALU.mult))
                    v.tensor_scalar(kv[:, b, D:N], C.c("heads"), ps[:, 4 + b, D:D + 1], None, ALU.mult)\
                     .then_inc(S("kv_ready"), 1)
                for h in range(2):
                    v.wait_ge(S("att_ps"), h + 1)
                    src = ps[:, 6 + h, 0:2 * N].rearrange("p (t n) -> p t n", n=N)
                    tl = slice(2 * h, 2 * h + 2)
                    L(v.tensor_scalar(den[:, tl, :], src[:, :, D:N], LIN_EPS, None, ALU.add))
                    L(v.reciprocal(den[:, tl, :], den[:, tl, :]))
                    ins = v.tensor_tensor(heads4(att[:, tl, :]), heads4(src[:, :, 0:D]),
                                          bcast(den[:, tl, :], 3, [P, 2, HEADS, HD]), ALU.mult)
                    ins.then_inc(S("att_ready" if h else "att_half"), 1)
                v.wait_ge(S("out_ready"), 1)
                L(v.tensor_tensor(o[:, :, :], ps[:, 1, :].rearrange("p (t d) -> p t d", d=D),
                                  bcast(w("proj_b"), 1, [P, PT, D]), ALU.add))
                moments(v, L, C, [o[:, t, :] for t in range(PT)])
                mean_square(v, L)
                rsqrt(v, L, C, C.rstd[:, :], C.mv[:, :, 1], RMS_EPS)
                for t in range(PT):
                    L.tick(v.scalar_tensor_tensor(o[:, t, :], o[:, t, :], C.rstd[:, t:t + 1], w("gout"),
                                                  ALU.mult, ALU.mult))
                L.settle()
                xs = C.xt(i, 0, PT)
                L(v.tensor_tensor(xs, xs, o[:, :, :].rearrange("p t d -> p (t d)"), ALU.add))

            @block.scalar
            def _(a):
                a.wait_ge(S("hT_ps"), 1)
                a.activation(hT[:, :], ps[:, 7, :], ACT.Copy).then_inc(S("hT_ready"), 1)
                a.wait_ge(S("qT_ps"), 1)
                a.activation(qT[:, :], ps[:, 7, :], ACT.Copy).then_inc(S("qT_ready"), 1)
                a.wait_ge(S("attT_ps"), 1)
                a.activation(attT[:, :], ps[:, 0, :], ACT.Copy).then_inc(S("attT_ready"), 1)

            @block.tensor
            def _(pe):
                turn_tiles(pe, C, 7, xn, S("xn_ready"), S("hT_ps"))
                pe.wait_ge(S("hT_ready"), 1)
                project_tokens(pe, C, 0, hT, w("qkv"), 3 * D, S("qkv_ready"))
                pe.wait_ge(S("qk_ready"), 1)
                for t in range(PT):
                    mm = pe.transpose(ps[:, 7, t * P:(t + 1) * P], qk[:, 0, t, :], C.ident)
                mm.then_inc(S("qT_ps"), 1)
                pe.wait_ge(S("qk_ready"), 2)
                for b in range(2):
                    for t in range(2):
                        mm = pe.matmul(ps[:, 4 + b, 0:D + 1], qk[:, 1, 2 * b + t, :], pre[:, 2 * b + t, 2 * D:3 * D + 1],
                                       start=t == 0, stop=t == 1)
                    mm.then_inc(S("kv_ps"), 1)
                pe.wait_ge(S("qT_ready"), 1)
                for t in range(PT):
                    pe.wait_ge(S("kv_ready"), t // 2 + 1)
                    mm = pe.matmul(ps[:, 6 + t // 2, (t % 2) * N:(t % 2 + 1) * N], qT[:, t * P:(t + 1) * P],
                                   kv[:, t // 2, :], start=True, stop=True)
                    if t % 2:
                        mm.then_inc(S("att_ps"), 1)
                turn_and_project(pe, C, w, S, att, attT, 0, 1)


def block_attention(C, k, ks, packed):
    nc, w, S, ps = C.nc, C.weights(k), C.sem, C.ps
    EPS, B = 1e-3, 64
    N = D + HEADS
    with ExitStack() as ctx:
        sb = lambda name, shape, dt=F32: ctx.enter_context(nc.sbuf_tensor(f"blocks_{name}", shape, dt))
        xn = sb("xn", [P, PT, D])
        hT = sb("hT", [P, PAIR])
        qx = sb("qx", [P, PT, D])
        kx = sb("kx", [P, PT, D])
        vv = sb("vv", [P, PT, D + 1])
        mx = sb("mx", [P, PT, HEADS])
        qT = sb("qT", [P, PAIR])
        kv = sb("kv", [P, 2, 3, N])
        den = sb("den", [P, PT, HEADS])
        att = sb("att", [P, PT, D])
        attT = sb("attT", [P, PAIR])

        def setup(v, L):
            L(v.memset(vv[:, :, D:D + 1], 1.0))

        start_sublayer(C, k, ks, packed, setup)
        with nc.Fori(0, PAIRS) as i, C.turn() as block:

            @block.vector
            def _(v):
                L = Link(v, S("vector_step"))
                norm_pair(v, L, C, i, xn, S("xn_ready"))
                bc = lambda ap: bcast(ap, 3, [P, PT, HEADS, HD])
                v.wait_ge(S("qkv_ready"), PT)
                for t in range(PT):
                    L.tick(v.tensor_reduce(mx[:, t, :], ps[:, t, 0:D].rearrange("p (h d) -> p h d", d=HD), AX.X, ALU.max))
                    L.tick(v.tensor_copy(vv[:, t, 0:D], ps[:, t, 2 * D:3 * D]))
                L.settle()
                for t in range(PT):
                    L.tick(v.tensor_tensor(qx[:, t, :].rearrange("p (h d) -> p h d", d=HD),
                                           ps[:, t, 0:D].rearrange("p (h d) -> p h d", d=HD),
                                           bcast(mx[:, t, :], 2, [P, HEADS, HD]), ALU.subtract))
                L.settle()
                v.tensor_copy(kx[:, :, :], ps[:, 0:PT, D:2 * D]).then_inc(S("logits_ready"), 1)
                v.wait_ge(S("exp_ready"), 1)
                L(v.tensor_reduce(mx[:, :, :], heads4(qx[:, :, :]), AX.X, ALU.add))
                L(v.reciprocal(mx[:, :, :], mx[:, :, :]))
                L(v.tensor_scalar(mx[:, :, :], mx[:, :, :], HD ** -0.5, None, ALU.mult))
                v.tensor_tensor(heads4(qx[:, :, :]), heads4(qx[:, :, :]), bc(mx[:, :, :]), ALU.mult)\
                 .then_inc(S("q_ready"), 1)
                for b in range(2):
                    v.wait_ge(S("kv_ps"), b + 1)
                    for u in range(3):
                        src = ps[:, 4 + b, u * (D + 1):(u + 1) * (D + 1)]
                        L.tick(v.tensor_tensor(kv[:, b, u, 0:D], src[:, 0:D], C.c("block"), ALU.mult))
                        ins = v.tensor_scalar(kv[:, b, u, D:N], C.c("heads"), src[:, D:D + 1], None, ALU.mult)
                        L.tick(ins) if u < 2 else ins.then_inc(S("kv_ready"), 1)
                for b in range(2):
                    L.tick(v.memset(att[0:B, 2 * b, :], 0.0))
                L.settle()
                for b in range(2):
                    v.wait_ge(S("att_ps"), b + 1)
                    for t, p0 in ((0, B), (1, 0)):
                        src = ps[p0:P, 6 + b, t * N:(t + 1) * N]
                        L(v.tensor_scalar(den[p0:P, 2 * b + t, :], src[:, D:N], EPS, None, ALU.max))
                        L(v.reciprocal(den[p0:P, 2 * b + t, :], den[p0:P, 2 * b + t, :]))
                        ins = v.tensor_tensor(att[p0:P, 2 * b + t, :].rearrange("p (h d) -> p h d", d=HD),
                                              src[:, 0:D].rearrange("p (h d) -> p h d", d=HD),
                                              bcast(den[p0:P, 2 * b + t, :], 2, [P - p0, HEADS, HD]), ALU.mult)
                        L.tick(ins) if (b, t) != (1, 1) else ins.then_inc(S("att_ready"), 1)
                L.settle()
                add_projection(v, L, C, i, w, S, 1)

            @block.scalar
            def _(a):
                a.wait_ge(S("hT_ps"), 1)
                a.activation(hT[:, :], ps[:, 7, :], ACT.Copy).then_inc(S("hT_ready"), 1)
                a.wait_ge(S("logits_ready"), 1)
                a.activation(qx[:, :, :], qx[:, :, :], ACT.Exp)
                a.activation(kx[:, :, :], kx[:, :, :], ACT.Exp).then_inc(S("exp_ready"), 1)
                a.wait_ge(S("qT_ps"), 1)
                a.activation(qT[:, :], ps[:, 7, :], ACT.Copy).then_inc(S("qT_ready"), 1)
                a.wait_ge(S("attT_ps"), 1)
                a.activation(attT[:, :], ps[:, 0, :], ACT.Copy).then_inc(S("attT_ready"), 1)

            @block.tensor
            def _(pe):
                turn_tiles(pe, C, 7, xn, S("xn_ready"), S("hT_ps"))
                pe.wait_ge(S("hT_ready"), 1)
                project_tokens(pe, C, 0, hT, w("qkv"), 3 * D, S("qkv_ready"))
                pe.wait_ge(S("exp_ready"), 1)
                for b in range(2):
                    for u, parts in enumerate(([(0, B)], [(0, P)], [(0, P), (1, B)])):
                        for n, (t, rows_) in enumerate(parts):
                            mm = pe.matmul(ps[:, 4 + b, u * (D + 1):(u + 1) * (D + 1)], kx[0:rows_, 2 * b + t, :],
                                           vv[0:rows_, 2 * b + t, :], start=n == 0, stop=n == len(parts) - 1)
                    mm.then_inc(S("kv_ps"), 1)
                pe.wait_ge(S("q_ready"), 1)
                for t in range(PT):
                    mm = pe.transpose(ps[:, 7, t * P:(t + 1) * P], qx[:, t, :], C.ident)
                mm.then_inc(S("qT_ps"), 1)
                pe.wait_ge(S("qT_ready"), 1)
                for b in range(2):
                    pe.wait_ge(S("kv_ready"), b + 1)
                    for u in range(1, 4):
                        t, p0 = u // 2, (u % 2) * B
                        mm = pe.matmul(ps[p0:p0 + B, 6 + b, t * N:(t + 1) * N],
                                       qT[:, 2 * b * P + u * B:2 * b * P + (u + 1) * B], kv[:, b, u - 1, :],
                                       start=True, stop=True)
                    mm.then_inc(S("att_ps"), 1)
                turn_and_project(pe, C, w, S, att, attT, 0, 1)


ROUND = 1.5 * 2.0 ** 23


def bit_ffn(C, k, ks, packed):
    nc, w, S, ps = C.nc, C.weights(k), C.sem, C.ps
    F, FT = 4 * D, 4
    with ExitStack() as ctx:
        sb = lambda name, shape, dt=F32: ctx.enter_context(nc.sbuf_tensor(f"bit_{name}", shape, dt))
        wq = {n: sb("q_" + n, [P, F], BF16) for n in ("gate", "up", "down")}
        wabs = sb("wabs", [P, 4])
        wscale = sb("wscale", [P, 4])
        winv = sb("winv", [P, 4])
        wt = sb("wt", [P, F])
        xn = sb("xn", [P, PT, D])
        amax = sb("amax", [P, PT])
        asc = sb("asc", [P, PT])
        gsc = sb("gsc", [P, PT])
        usc = sb("usc", [P, PT])
        dsc = sb("dsc", [P, PT])
        hmax = sb("hmax", [P, PT])
        hsc = sb("hsc", [P, PT])
        xr = sb("xr", [P, PT, D])
        xq = sb("xq", [P, PT, D], BF16)
        xqT = sb("xqT", [P, PAIR], BF16)
        gate = sb("gate", [P, 2, F])
        h = sb("h", [P, 2, F])
        hr = sb("hr", [P, 2, F])
        hq = sb("hq", [P, 2, F], BF16)
        hqT = sb("hqT", [P, 2, F], BF16)
        psb = lambda bank: ps[:, bank, 0:F // 2].bitcast(BF16)
        start_sublayer(C, k, ks, packed)
        names = ("gate", "up", "down")
        with C.turn() as block:

            @block.vector
            def _(v):
                L = Link(v, S("vector_step"))
                L(v.memset(wabs[:, 3:4], 0.0))
                for n, name in enumerate(names):
                    L.tick(v.tensor_reduce(wabs[:, n:n + 1], w(name), AX.X, ALU.add, apply_absolute_value=True))
                L.settle()
                v.tensor_copy(wscale[:, :], wabs[:, :]).then_inc(S("row_sums"), 1)
                v.wait_ge(S("sums"), 1)
                L(v.tensor_scalar(wscale[:, :], ps[:, 0, 0:4], 1.0 / (F * D), 1e-5, ALU.mult, ALU.max))
                L(v.reciprocal(winv[:, :], wscale[:, :]))
                for n, name in enumerate(names):
                    L(v.tensor_scalar(wt[:, :], w(name), winv[:, n:n + 1], ROUND, ALU.mult, ALU.add))
                    L(v.tensor_scalar(wt[:, :], wt[:, :], -ROUND, None, ALU.add))
                    L(v.tensor_scalar(wq[name][:, :], wt[:, :], -1.0, 1.0, ALU.max, ALU.min))

            @block.tensor
            def _(pe):
                pe.wait_ge(S("row_sums"), 1)
                pe.matmul(ps[:, 0, 0:4], C.c("ones"), wscale[:, :], start=True, stop=True).then_inc(S("sums"), 1)

        with nc.Fori(0, PAIRS) as i, C.turn() as block:

            @block.vector
            def _(v):
                L = Link(v, S("vector_step"))
                norm_pair(v, L, C, i, xn, S("xn_ready"))
                v.wait_ge(S("xn_ready"), PT)
                L(v.tensor_reduce(amax[:, :], xn[:, :, :], AX.X, ALU.max, apply_absolute_value=True))
                L(v.tensor_scalar(amax[:, :], amax[:, :], 1e-5, None, ALU.max))
                L(v.reciprocal(asc[:, :], amax[:, :]))
                L(v.tensor_scalar(asc[:, :], asc[:, :], 127.0, None, ALU.mult))
                for t in range(PT):
                    L.tick(v.tensor_scalar(xr[:, t, :], xn[:, t, :], asc[:, t:t + 1], ROUND, ALU.mult, ALU.add))
                L.settle()
                L(v.tensor_scalar(xr[:, :, :], xr[:, :, :], -ROUND, None, ALU.add))
                v.tensor_scalar(xq[:, :, :], xr[:, :, :], -128.0, 127.0, ALU.max, ALU.min).then_inc(S("xq_ready"), 1)
                L(v.tensor_scalar(amax[:, :], amax[:, :], 1.0 / 127.0, None, ALU.mult))
                L(v.tensor_scalar(usc[:, :], amax[:, :], wscale[:, 1:2], None, ALU.mult))
                v.tensor_scalar(gsc[:, :], amax[:, :], wscale[:, 0:1], None, ALU.mult).then_inc(S("scales_ready"), 1)
                for t in range(PT):
                    hb, rb = h[:, t % 2, :], hr[:, t % 2, :]
                    v.wait_ge(S("gate_ready"), t + 1)
                    L(v.scalar_tensor_tensor(hb, ps[:, 3 + t % 2, :], usc[:, t:t + 1], gate[:, t % 2, :], ALU.mult, ALU.mult))
                    L(v.tensor_reduce(hmax[:, t:t + 1], hb, AX.X, ALU.max, apply_absolute_value=True))
                    L(v.tensor_scalar(hmax[:, t:t + 1], hmax[:, t:t + 1], 1e-5, None, ALU.max))
                    L(v.reciprocal(hsc[:, t:t + 1], hmax[:, t:t + 1]))
                    L(v.tensor_scalar(hsc[:, t:t + 1], hsc[:, t:t + 1], 127.0, None, ALU.mult))
                    L(v.tensor_scalar(rb, hb, hsc[:, t:t + 1], ROUND, ALU.mult, ALU.add))
                    L(v.tensor_scalar(rb, rb, -ROUND, None, ALU.add))
                    if t >= 2:
                        v.wait_ge(S("hqT_ps"), t - 1)
                    v.tensor_scalar(hq[:, t % 2, :], rb, -128.0, 127.0, ALU.max, ALU.min).then_inc(S("hq_ready"), 1)
                L(v.tensor_scalar(dsc[:, :], hmax[:, :], 1.0 / 127.0, wscale[:, 2:3], ALU.mult, ALU.mult))
                v.wait_ge(S("down_ready"), PT)
                for t in range(PT):
                    xs = C.xt(i, t)
                    L.tick(v.scalar_tensor_tensor(xs, ps[:, 7, t * P:(t + 1) * P], dsc[:, t:t + 1], xs, ALU.mult, ALU.add))
                L.settle()

            def turned(a, t):
                a.wait_ge(S("hqT_ps"), t + 1)
                if t >= 2:
                    a.wait_ge(S("down_ready"), t - 1)
                a.activation(hqT[:, t % 2, :], psb(5 + t % 2), ACT.Copy).then_inc(S("hqT_ready"), 1)

            @block.scalar
            def _(a):
                a.wait_ge(S("xqT_ps"), 1)
                a.activation(xqT[:, :], psb(0), ACT.Copy).then_inc(S("xqT_ready"), 1)
                a.wait_ge(S("scales_ready"), 1)
                for t in range(PT):
                    a.wait_ge(S("up_ready"), t + 1)
                    if t >= 2:
                        a.wait_ge(S("hq_ready"), t - 1)
                    a.activation(gate[:, t % 2, :], ps[:, 1 + t % 2, :], ACT.Silu, scale=gsc[:, t:t + 1])\
                     .then_inc(S("gate_ready"), 1)
                    if t >= 1:
                        turned(a, t - 1)
                turned(a, PT - 1)

            @block.tensor
            def _(pe):
                pe.wait_ge(S("xq_ready"), 1)
                for t in range(PT):
                    mm = pe.transpose(psb(0)[:, t * P:(t + 1) * P], xq[:, t, :], C.identb[:, :])
                mm.then_inc(S("xqT_ps"), 1)
                pe.wait_ge(S("xqT_ready"), 1)

                def up(t):
                    if t >= 2:
                        pe.wait_ge(S("hq_ready"), t - 1)
                    pe.matmul(ps[:, 1 + t % 2, :], xqT[:, t * P:(t + 1) * P], wq["gate"][:, :], start=True, stop=True)
                    pe.matmul(ps[:, 3 + t % 2, :], xqT[:, t * P:(t + 1) * P], wq["up"][:, :], start=True, stop=True)\
                      .then_inc(S("up_ready"), 1)

                up(0)
                for t in range(PT):
                    if t + 1 < PT:
                        up(t + 1)
                    pe.wait_ge(S("hq_ready"), t + 1)
                    if t >= 2:
                        pe.wait_ge(S("hqT_ready"), t - 1)
                    for m in range(FT):
                        mm = pe.transpose(psb(5 + t % 2)[:, m * P:(m + 1) * P], hq[:, t % 2, m * P:(m + 1) * P], C.identb[:, :])
                    mm.then_inc(S("hqT_ps"), 1)
                    pe.wait_ge(S("hqT_ready"), t + 1)
                    for m in range(FT):
                        mm = pe.matmul(ps[:, 7, t * P:(t + 1) * P], hqT[:, t % 2, m * P:(m + 1) * P],
                                       wq["down"][:, m * D:(m + 1) * D], start=m == 0, stop=m == FT - 1)
                    mm.then_inc(S("down_ready"), 1)


def int8_ffn(C, k, ks, packed):
    nc, w, S, ps = C.nc, C.weights(k), C.sem, C.ps
    F, FT, EPS = 4 * D, 4, 1e-8
    with ExitStack() as ctx:
        sb = lambda name, shape, dt=F32: ctx.enter_context(nc.sbuf_tensor(f"int8_{name}", shape, dt))
        wr = sb("wr", [P, F])
        w1b = sb("w1b", [P, F], BF16)
        w2b = sb("w2b", [P, F], BF16)
        w1T = sb("w1T", [P, F], BF16)
        w2T = sb("w2T", [P, F], BF16)
        ws = sb("ws", [P, 2 * FT])
        wi = sb("wi", [P, 2 * FT])
        xn = sb("xn", [P, PT, D])
        xT = sb("xT", [P, TILES * P])
        xqT = sb("xqT", [P, PAIR], BF16)
        rnd = sb("rnd", [P, PAIR])
        hT = sb("hT", [P, FT, TILES * P])
        hmaxs = sb("hmaxs", [P, TILES])
        hqT = sb("hqT", [P, FT, PAIR], BF16)
        rnd2 = sb("rnd2", [P, FT, PAIR])
        m1 = sb("m1", [P, 1])
        mall = sb("mall", [P, 1])
        s1 = sb("s1", [P, 1])
        s1i = sb("s1i", [P, 1])
        su = sb("su", [P, FT])
        sui = sb("sui", [P, FT])
        bq = sb("bq", [P, FT])
        y = sb("y", [P, PAIR])
        psb = lambda bank: ps[:, bank, 0:F // 2].bitcast(BF16)

        def setup(v, L):
            L(v.memset(hmaxs[:, :], 0.0))
            for n in range(FT):
                L.tick(v.tensor_reduce(ws[:, n:n + 1], w("w1")[:, n * P:(n + 1) * P], AX.X, ALU.max, apply_absolute_value=True))
            L.tick(v.tensor_reduce(ws[:, FT:FT + 1], w("w2"), AX.X, ALU.max, apply_absolute_value=True))
            L.settle()
            n5 = FT + 1
            L(v.tensor_scalar(ws[:, 0:n5], ws[:, 0:n5], EPS, 1.0 / 127.0, ALU.max, ALU.mult))
            L(v.reciprocal(wi[:, 0:n5], ws[:, 0:n5]))
            for n in range(FT):
                L.tick(v.tensor_scalar(wr[:, n * P:(n + 1) * P], w("w1")[:, n * P:(n + 1) * P], wi[:, n:n + 1], ROUND,
                                       ALU.mult, ALU.add))
            L.settle()
            L(v.tensor_scalar(wr[:, :], wr[:, :], -ROUND, None, ALU.add))
            L(v.tensor_scalar(w1b[:, :], wr[:, :], -128.0, 127.0, ALU.max, ALU.min))
            L(v.tensor_scalar(wr[:, :], w("w2"), wi[:, FT:FT + 1], ROUND, ALU.mult, ALU.add))
            L(v.tensor_scalar(wr[:, :], wr[:, :], -ROUND, None, ALU.add))
            L(v.tensor_scalar(w2b[:, :], wr[:, :], -128.0, 127.0, ALU.max, ALU.min))

        def scale_and_bias(v, L, wcols, bias, n):
            L(v.tensor_scalar(s1[:, :], mall[:, :], EPS, 1.0 / 255.0, ALU.max, ALU.mult))
            L(v.reciprocal(s1i[:, :], s1[:, :]))
            L(v.tensor_scalar(su[:, 0:n], wcols, s1[:, 0:1], None, ALU.mult))
            L(v.reciprocal(sui[:, 0:n], su[:, 0:n]))
            L(v.tensor_tensor(bq[:, 0:n], bias, sui[:, 0:n], ALU.mult))
            L(v.tensor_scalar(bq[:, 0:n], bq[:, 0:n], ROUND, None, ALU.add))
            L(v.tensor_scalar(bq[:, 0:n], bq[:, 0:n], -ROUND, None, ALU.add))
            L(v.tensor_tensor(bq[:, 0:n], bq[:, 0:n], su[:, 0:n], ALU.mult))

        start_sublayer(C, k, ks, packed, setup)

        with C.turn() as block:

            @block.tensor
            def _(pe):
                for bank, src in ((0, w1b), (1, w2b)):
                    for n in range(FT):
                        mm = pe.transpose(psb(bank)[:, n * P:(n + 1) * P], src[:, n * P:(n + 1) * P], C.identb[:, :])
                    mm.then_inc(S("weights_turned"), 1)

            @block.scalar
            def _(a):
                for bank, dst in ((0, w1T), (1, w2T)):
                    a.wait_ge(S("weights_turned"), bank + 1)
                    a.activation(dst[:, :], psb(bank), ACT.Copy).then_inc(S("weights_copied"), 1)

        with nc.Fori(0, PAIRS) as i, C.turn() as block:

            @block.vector
            def _(v):
                norm_pair(v, Link(v, S("vector_step")), C, i, xn, S("xn_ready"))

            @block.scalar
            def _(a):
                a.wait_ge(S("hT_ps"), 1)
                a.activation(xT[:, bass.ds(i * PAIR, PAIR)], ps[:, 0, :], ACT.Copy).then_inc(S("hT_ready"), 1)

            @block.tensor
            def _(pe):
                turn_tiles(pe, C, 0, xn, S("xn_ready"), S("hT_ps"))

        def whole_max(block, src, wcols, bias, n):
            @block.vector
            def _(v):
                L = Link(v, S("vector_step"))
                v.tensor_reduce(m1[:, :], src, AX.X, ALU.max).then_inc(S("row_max"), 1)
                v.wait_ge(S("all_max"), 1)
                scale_and_bias(v, L, wcols, bias, n)

            @block.gpsimd
            def _(g):
                g.wait_ge(S("row_max"), 1)
                g.partition_all_reduce(mall[:, :], m1[:, :], P, bass.bass_isa.ReduceOp.max).then_inc(S("all_max"), 1)

        with C.turn() as block:
            whole_max(block, xT[:, :], ws[:, 0:FT], w("b1"), FT)

        with nc.Fori(0, PAIRS) as i, C.turn() as block:

            @block.vector
            def _(v):
                L = Link(v, S("vector_step"))
                L(v.tensor_scalar(rnd[:, :], xT[:, bass.ds(i * PAIR, PAIR)], s1i[:, 0:1], ROUND, ALU.mult, ALU.add))
                L(v.tensor_scalar(rnd[:, :], rnd[:, :], -ROUND, None, ALU.add))
                v.tensor_scalar(xqT[:, :], rnd[:, :], 0.0, 255.0, ALU.max, ALU.min).then_inc(S("xq_ready"), 1)
                for m in range(FT):
                    v.wait_ge(S("h_ready"), m + 1)
                    L.tick(v.tensor_reduce(hmaxs[:, bass.ds(i * FT + m, 1)],
                                           hT[:, m, bass.ds(i * PAIR, PAIR)], AX.X, ALU.max))
                L.settle()

            @block.scalar
            def _(a):
                for m in range(FT):
                    a.wait_ge(S("up_ready"), m + 1)
                    a.activation(hT[:, m, bass.ds(i * PAIR, PAIR)], ps[:, m, :], ACT.Relu, bias=bq[:, m:m + 1],
                                 scale=su[:, m:m + 1]).then_inc(S("h_ready"), 1)

            @block.tensor
            def _(pe):
                pe.wait_ge(S("xq_ready"), 1)
                for m in range(FT):
                    pe.matmul(ps[:, m, :], w1T[:, m * P:(m + 1) * P], xqT[:, :], start=True, stop=True)\
                      .then_inc(S("up_ready"), 1)

        with C.turn() as block:
            whole_max(block, hmaxs[:, :], ws[:, FT:FT + 1], w("b2"), 1)

        with nc.Fori(0, PAIRS) as i, C.turn() as block:

            @block.vector
            def _(v):
                L = Link(v, S("vector_step"))
                for m in range(FT):
                    L.tick(v.tensor_scalar(rnd2[:, m, :], hT[:, m, bass.ds(i * PAIR, PAIR)], s1i[:, 0:1], ROUND,
                                           ALU.mult, ALU.add))
                L.settle()
                for m in range(FT):
                    L.tick(v.tensor_scalar(rnd2[:, m, :], rnd2[:, m, :], -ROUND, None, ALU.add))
                L.settle()
                for m in range(FT):
                    v.tensor_scalar(hqT[:, m, :], rnd2[:, m, :], 0.0, 255.0, ALU.max, ALU.min).then_inc(S("hq_ready"), 1)
                v.wait_ge(S("y_turned"), 1)
                L(v.tensor_tensor(C.xt(i, 0, PT), C.xt(i, 0, PT), ps[:, 1, :], ALU.add))

            @block.scalar
            def _(a):
                a.wait_ge(S("down_ready"), 1)
                a.activation(y[:, :], ps[:, 0, :], ACT.Identity, bias=bq[:, 0:1], scale=su[:, 0:1]).then_inc(S("y_ready"), 1)

            @block.tensor
            def _(pe):
                for m in range(FT):
                    pe.wait_ge(S("hq_ready"), m + 1)
                    mm = pe.matmul(ps[:, 0, :], w2T[:, m * P:(m + 1) * P], hqT[:, m, :], start=m == 0, stop=m == FT - 1)
                mm.then_inc(S("down_ready"), 1)
                pe.wait_ge(S("y_ready"), 1)
                for t in range(PT):
                    mm = pe.transpose(ps[:, 1, t * P:(t + 1) * P], y[:, t * P:(t + 1) * P], C.ident)
                mm.then_inc(S("y_turned"), 1)


def wide_attention(C, k, ks, packed, maskd):
    nc, w, S, ps = C.nc, C.weights(k), C.sem, C.ps
    DK, M = 64, 8
    with ExitStack() as ctx:
        sb = lambda name, shape, dt=F32: ctx.enter_context(nc.sbuf_tensor(f"wide_{name}", shape, dt))
        xn = sb("xn", [P, PT, D])
        hT = sb("hT", [P, PAIR])
        cT = sb("cT", [P, PAIR])
        q = sb("q", [P, M, 2, SEQ])
        bq = sb("bq", [P, M])
        kk = sb("k", [P, M, SEQ])
        V = sb("v", [P, 2, M * P])
        mask = sb("mask", [P, 1, 2, SEQ])
        sc = sb("sc", [P, 2, 2, SEQ])
        mx = sb("mx", [P, 2, 2])
        nm = sb("nm", [P, 2, 2])
        sums = sb("sums", [P, 2, 2])
        inv = sb("inv", [P, 2, 2])
        pr = sb("pr", [P, 2, 2, SEQ])
        prT = sb("prT", [P, 4, 2, SEQ])
        attT = sb("attT", [P, M, SEQ])

        def setup(v, L):
            L.tick(v.memset(q[:], 0.0))
            L.tick(v.tensor_scalar(bq[:, :], w("bq"), DK ** -0.5, None, ALU.mult))
            L.settle()

        start_sublayer(C, k, ks, packed, setup)
        H = HEADS
        half = [slice(DK * j, DK * j + DK) for j in range(2)]
        with nc.Fori(0, SEQS) as i, C.turn() as block:

            @block.sync
            def _(sp):
                sp.dma_start(mask[:, 0, :, :], maskd[:, bass.ds(i * 2 * SEQ, 2 * SEQ)]
                             .rearrange("p (t n) -> p t n", t=2)).then_inc(S("mask_loaded"), 16)

            @block.gpsimd
            def _(g):
                g.tensor_copy(cT[:, 0:SEQ], C.ctxT[:, bass.ds(i * SEQ, SEQ)]).then_inc(S("context_ready"), 1)

            @block.vector
            def _(v):
                L = Link(v, S("vector_step"))
                xs = [C.x[:, bass.ds(i * SEQ + t * D, D)] for t in range(2)]
                moments(v, L, C, xs)
                rsqrt(v, L, C, C.rstd[:, 0:2], C.mv[:, 0:2, 1], LN_EPS)
                for t in range(2):
                    v.tensor_scalar(xn[:, t, :], xs[t], C.mv[:, t, 0:1], C.rstd[:, t:t + 1],
                                    ALU.subtract, ALU.mult).then_inc(S("xn_ready"), 1)
                for n in range(4):
                    v.wait_ge(S("v_proj"), n + 1)
                    cols = slice((n % 2) * 512, (n % 2) * 512 + 512)
                    v.tensor_tensor(V[:, n // 2, cols], ps[:, 4 + n, :], w("bv")[:, cols], ALU.add)\
                     .then_inc(S("v_ready"), 1)
                v.wait_ge(S("mask_loaded"), 16)

                def masked(h):
                    v.wait_ge(S("scores_ready"), h + 1)
                    if h >= 2:
                        v.wait_ge(S("exp_done"), h - 1)
                    for qt in range(2):
                        L.tick(v.tensor_tensor_reduce(out=sc[:, h % 2, qt, :], in0=ps[:, h % 2, qt * SEQ:(qt + 1) * SEQ],
                                                      in1=mask[:, 0, qt, :], scale=1.0, scalar=-3.0e38, op0=ALU.add,
                                                      op1=ALU.max, accum_out=mx[:, h % 2, qt:qt + 1]))
                    L.settle()
                    v.tensor_scalar(nm[:, h % 2, :], mx[:, h % 2, :], -1.0, None, ALU.mult).then_inc(S("masked"), 1)

                def normalise(h):
                    v.wait_ge(S("exp_done"), h + 1)
                    L(v.reciprocal(inv[:, h % 2, :], sums[:, h % 2, :]))
                    for qt in range(2):
                        ins = v.tensor_scalar(pr[:, h % 2, qt, :], pr[:, h % 2, qt, :], inv[:, h % 2, qt:qt + 1], None,
                                              ALU.mult)
                    ins.then_inc(S("normalised"), 1)

                def turned(h):
                    v.wait_ge(S("prT_ps"), h + 1)
                    if h >= 4:
                        v.wait_ge(S("pv_ready"), (h - 4) // 2 + 1)
                    v.tensor_copy(prT[:, h % 4, :, :].rearrange("p t n -> p (t n)"), ps[:, 2 + h % 2, :])\
                     .then_inc(S("prT_ready"), 1)

                for h in range(H + 2):
                    if h < H:
                        masked(h)
                    if 1 <= h <= H:
                        normalise(h - 1)
                    if h >= 2:
                        turned(h - 2)
                v.wait_ge(S("out_ready"), 1)
                xp = C.x[:, bass.ds(i * SEQ, SEQ)]
                L(v.tensor_tensor(xp, xp, ps[:, 6, 0:SEQ], ALU.add))
                x3 = xp.rearrange("p (t d) -> p t d", d=D)
                L(v.tensor_tensor(x3, x3, bcast(w("bo"), 1, [P, 2, D]), ALU.add))

            @block.scalar
            def _(a):
                a.wait_ge(S("hT_ps"), 1)
                a.activation(hT[:, 0:SEQ], ps[:, 0, 0:SEQ], ACT.Copy).then_inc(S("hT_ready"), 1)
                for m in range(M):
                    a.wait_ge(S("qk_proj"), m + 1)
                    for j in range(2):
                        a.activation(q[half[j], m, j, :], ps[half[j], m % 4, 0:SEQ], ACT.Identity,
                                     bias=bq[half[j], m:m + 1], scale=DK ** -0.5)
                    a.activation(kk[:, m, :], ps[:, m % 4, SEQ:2 * SEQ], ACT.Identity, bias=w("bk")[:, m:m + 1])\
                     .then_inc(S("qk_copied"), 1)

                def exps(h):
                    a.wait_ge(S("masked"), h + 1)
                    if h >= 2:
                        a.wait_ge(S("normalised"), h - 1)
                        a.wait_ge(S("prT_ps"), h - 1)
                    for qt in range(2):
                        ins = a.activation(pr[:, h % 2, qt, :], sc[:, h % 2, qt, :], ACT.Exp, bias=nm[:, h % 2, qt:qt + 1],
                                           accum_out=sums[:, h % 2, qt:qt + 1])
                    ins.then_inc(S("exp_done"), 1)

                def att_copy(m):
                    a.wait_ge(S("pv_ready"), m + 1)
                    a.activation(attT[:, m, :], ps[:, 4 + m % 2, 0:SEQ], ACT.Copy).then_inc(S("attT_ready"), 1)

                for h in range(H):
                    exps(h)
                    if h >= 7 and h % 2:
                        att_copy((h - 7) // 2)
                for m in range((H - 7 + 1) // 2, M):
                    att_copy(m)

            @block.tensor
            def _(pe):
                for t in range(2):
                    pe.wait_ge(S("xn_ready"), t + 1)
                    mm = pe.transpose(ps[:, 0, t * P:(t + 1) * P], xn[:, t, :], C.ident)
                mm.then_inc(S("hT_ps"), 1)
                pe.wait_ge(S("context_ready"), 1)
                for n in range(4):
                    pe.matmul(ps[:, 4 + n, :], cT[:, (n // 2) * P:(n // 2 + 1) * P], w("wv")[:, (n % 2) * 512:(n % 2 + 1) * 512],
                              start=True, stop=True).then_inc(S("v_proj"), 1)
                pe.wait_ge(S("hT_ready"), 1)
                for m in range(M):
                    if m >= 4:
                        pe.wait_ge(S("qk_copied"), m - 3)
                    pe.matmul(ps[:, m % 4, 0:SEQ], w("wq")[:, m * P:(m + 1) * P], hT[:, 0:SEQ], start=True, stop=True)
                    pe.matmul(ps[:, m % 4, SEQ:2 * SEQ], w("wk")[:, m * P:(m + 1) * P], cT[:, 0:SEQ], start=True, stop=True)\
                      .then_inc(S("qk_proj"), 1)
                pe.wait_ge(S("qk_copied"), M)
                pe.wait_ge(S("v_ready"), 4)

                def scores(h):
                    if h >= 2:
                        pe.wait_ge(S("masked"), h - 1)
                    for qt in range(2):
                        mm = pe.matmul(ps[:, h % 2, qt * SEQ:(qt + 1) * SEQ], q[:, h // 2, h % 2, qt * P:(qt + 1) * P],
                                       kk[:, h // 2, :], start=True, stop=True)
                    mm.then_inc(S("scores_ready"), 1)

                def turn(h):
                    pe.wait_ge(S("normalised"), h + 1)
                    if h >= 2:
                        pe.wait_ge(S("prT_ready"), h - 1)
                    for kt in range(2):
                        for qt in range(2):
                            mm = pe.transpose(ps[:, 2 + h % 2, kt * SEQ + qt * P:kt * SEQ + (qt + 1) * P],
                                              pr[:, h % 2, qt, kt * P:(kt + 1) * P], C.ident)
                    mm.then_inc(S("prT_ps"), 1)

                def weigh(m):
                    pe.wait_ge(S("prT_ready"), 2 * m + 2)
                    if m >= 2:
                        pe.wait_ge(S("attT_ready"), m - 1)
                    for kt in range(2):
                        for j in range(2):
                            mm = pe.matmul(ps[half[j], 4 + m % 2, 0:SEQ], V[:, kt, (2 * m + j) * DK:(2 * m + j + 1) * DK],
                                           prT[:, (2 * m + j) % 4, kt, :], start=kt == 0, stop=kt == 1)
                    mm.then_inc(S("pv_ready"), 1)

                for h in range(H + 4):
                    if h < H:
                        scores(h)
                    if 2 <= h < H + 2:
                        turn(h - 2)
                    if h >= 4 and h % 2 == 0:
                        weigh((h - 4) // 2)
                pe.wait_ge(S("attT_ready"), M)
                for t in range(2):
                    for m in range(M):
                        mm = pe.matmul(ps[:, 6, t * P:(t + 1) * P], attT[:, m, t * P:(t + 1) * P],
                                       w("wo")[:, m * D:(m + 1) * D], start=m == 0, stop=m == M - 1)
                mm.then_inc(S("out_ready"), 1)


def decoder(nc, xd, ctxTd, boundary, maskd, packed, layout, out, ks):
    with ExitStack() as ctx:
        C = Core(nc, ctx, layout, ks)
        with C.turn() as block:
            @block.sync
            def _(sp):
                sp.dma_start(C.x[:, :].rearrange("p (t d) -> p t d", d=D),
                             xd.rearrange("(t p) d -> p t d", p=P)).then_inc(C.loaded, 16)
                sp.dma_start(C.const[:, :], packed["const"]).then_inc(C.loaded, 16)
                load_weights(C, sp, ks[0], packed)
                sp.dma_start(C.ctxT[:, :], ctxTd).then_inc(C.loaded, 16)

            @block.vector
            def _(v):
                v.wait_ge(C.loaded, 48)
                L = Link(v, C.sem("vector_step"))
                L.tick(v.tensor_copy(C.identb[:, :], C.ident))
                L(v.memset(C.lay[:, :, :, :], 0.0))
                for n, order in enumerate((Q_PARTS, K_PARTS)):
                    for slot, part in enumerate(order):
                        dst = C.lay[:, n, part, :].rearrange("p (h r) -> p h r", r=64)[:, :, HD * slot:HD * (slot + 1)]
                        L.tick(v.tensor_copy(dst, C.ident.rearrange("p (h d) -> p h d", d=HD)))
                L.settle()
        run = {
            0: lambda k: self_attention0(C, k, ks, packed),
            1: lambda k: attend8(C, k, ks, packed, cross=True),
            2: lambda k: sinkhorn_moe(C, k, ks, packed),
            3: lambda k: flow_attention(C, k, ks, packed),
            4: lambda k: attend8(C, k, ks, packed, cross=True, boundary=boundary),
            5: lambda k: bit_ffn(C, k, ks, packed),
            6: lambda k: relu_attention(C, k, ks, packed),
            7: lambda k: wide_attention(C, k, ks, packed, maskd),
            8: lambda k: top2_moe(C, k, ks, packed),
            9: lambda k: block_attention(C, k, ks, packed),
            10: lambda k: attend8(C, k, ks, packed, cross=True),
            11: lambda k: int8_ffn(C, k, ks, packed),
        }
        for k in ks:
            run[k](k)
        with nc.Block() as block:
            @block.sync
            def _(sp):
                sp.dma_start(out.rearrange("(t p) d -> p t d", p=P),
                             C.x[:, :].rearrange("p (t d) -> p t d", d=D)).then_inc(C.stored, 16)
                sp.wait_ge(C.stored, 16)


def self_attention0(C, k, ks, packed):
    with C.nc.sbuf_tensor("inner", [P, TILES * D], F32) as inner:
        attend8(C, k, ks, packed, cross=False, rope=True, causal=True, inner=inner)
        swiglu(C, k, inner)


KS = list(range(12))


def swapped(wt):
    return np.ascontiguousarray(wt.reshape(wt.shape[0], -1, 2)[:, :, ::-1]).reshape(wt.shape)


def rows(b):
    return np.broadcast_to(b.reshape(1, -1), (P, b.size))


def tiles(wt):
    return np.ascontiguousarray(wt.reshape(-1, P, wt.shape[1]).transpose(1, 0, 2)).reshape(P, -1)


def columns(b):
    return np.ascontiguousarray(b.reshape(-1, P).T)


def constants():
    f = np.float32
    r = np.arange(P)
    head = r // HD
    pos = np.arange(SEQ, dtype=np.float32)
    kd = (np.arange(HD) // 2).astype(np.float32)
    ang = pos[:, None] / np.power(f(10000.0), f(2.0) * kd / f(HD))
    cos, sin = np.cos(ang).astype(f), np.sin(ang).astype(f)
    sin = sin * np.where(np.arange(HD) % 2 == 0, -1.0, 1.0).astype(f)

    def feature_major(tab):
        return np.tile(tab.T, (HEADS, 2))

    def token_major(tab):
        return np.tile(tab.reshape(2, P, 1, HD), (1, 1, HEADS, 1)).transpose(1, 0, 2, 3).reshape(P, 2 * D)

    aug = np.zeros((2, 64), f)
    aug[:, AUG:AUG + 2] = 1.0
    return {
        "ident": np.eye(P, dtype=f), "ones": np.ones((P, P), f), "zeros": np.zeros((P, SEQ), f),
        "causalT": np.where(r[:, None] > r[None, :], NEG, 0.0).astype(f),
        "block": (head[:, None] == head[None, :]).astype(f),
        "heads": (head[:, None] == np.arange(HEADS)[None, :]).astype(f),
        "position": np.stack([r, r + P], 1).astype(f),
        "aug": aug.reshape(P, 1),
        "cosF": feature_major(cos), "sinF": feature_major(sin),
        "cosT": token_major(cos), "sinT": token_major(sin),
        "first": rows(np.arange(8, 0, -1).astype(f)),
    }


def pack(a):
    def attn(pre, wq, wk, wv, wo, bq, bk, bv, bo, transpose):
        t = (lambda m: a[pre + m].T) if transpose else (lambda m: a[pre + m])
        return {"wq": t(wq), "wk": t(wk), "wv": t(wv), "wo": t(wo),
                "bq": columns(a[pre + bq]), "bk": columns(a[pre + bk]),
                "bv": rows(a[pre + bv]), "bo": rows(a[pre + bo])}

    def experts(m):
        e, kk, n = m.shape
        return m.reshape(e, kk // P, P, n).transpose(2, 0, 1, 3).reshape(P, -1)

    def few(m):
        o = np.zeros((P, m.shape[1]), m.dtype)
        o[:m.shape[0]] = m
        return o

    parts = {
        "const": constants(),
        "L0_attn": {"wq": a["L0_attn_wq"].T, "wq_swapped": swapped(a["L0_attn_wq"].T),
                    "wk": a["L0_attn_wk"].T, "wk_swapped": swapped(a["L0_attn_wk"].T),
                    "wv": a["L0_attn_wv"].T, "wo": a["L0_attn_wo"].T,
                    "norm1": columns(a["L0_attn_norm1_w"]), "norm2": columns(a["L0_attn_norm2_w"]),
                    "w1": a["L0_attn_w1"].T, "w3": a["L0_attn_w3"].T, "w2": tiles(a["L0_attn_w2"].T)},
        "L0_xattn": attn("L0_xattn_", "Wq", "Wk", "Wv", "Wo", "bq", "bk", "bv", "bo", True),
        "L0_ffn": {"router": a["L0_ffn_router_w"].T, "router_b": rows(a["L0_ffn_router_b"]),
                   "temperature": rows(a["L0_ffn_temperature"]), "wg": experts(a["L0_ffn_wg"]),
                   "wp": experts(a["L0_ffn_wp"]), "wo": experts(a["L0_ffn_wo"])},
        "L1_attn": {"qkv": a["L1_attn_qkv_w"].T, "qkv_b": rows(a["L1_attn_qkv_b"]),
                    "proj": a["L1_attn_proj_w"].T, "proj_b": rows(a["L1_attn_proj_b"])},
        "L1_xattn": attn("L1_xattn_", "wq", "wk", "wv", "wo", "bq", "bk", "bv", "bo", True),
        "L1_ffn": {"gate": a["L1_ffn_w_gate"].T, "up": a["L1_ffn_w_up"].T, "down": tiles(a["L1_ffn_w_down"].T)},
        "L2_attn": {"qkv": a["L2_attn_Wqkv"].T, "qkv_b": rows(a["L2_attn_bqkv"]),
                    "gq": rows(a["L2_attn_gq"]), "gk": rows(a["L2_attn_gk"]), "gout": rows(a["L2_attn_gout"]),
                    "proj": a["L2_attn_Wout"].T, "proj_b": rows(a["L2_attn_bout"])},
        "L2_xattn": {"wq": a["L2_xattn_Wq"], "wk": a["L2_xattn_Wk"], "wv": a["L2_xattn_Wv"],
                     "wo": tiles(a["L2_xattn_Wo"]), "bq": columns(a["L2_xattn_bq"]), "bk": columns(a["L2_xattn_bk"]),
                     "bv": rows(a["L2_xattn_bv"]), "bo": rows(a["L2_xattn_bo"])},
        "L2_ffn": {"gate": a["L2_ffn_gate_w"], "gate_b": rows(a["L2_ffn_gate_b"]),
                   "w1": experts(a["L2_ffn_w1"]), "w2": experts(a["L2_ffn_w2"]), "wg": experts(a["L2_ffn_wg"]),
                   "w3": experts(a["L2_ffn_w3"]),
                   "b1": columns(a["L2_ffn_b1"].reshape(-1)), "b2": columns(a["L2_ffn_b2"].reshape(-1)),
                   "bg": columns(a["L2_ffn_bg"].reshape(-1)), "b3": few(a["L2_ffn_b3"])},
        "L3_attn": {"qkv": a["L3_attn_qkv_w"].T, "proj": a["L3_attn_proj_w"].T, "proj_b": rows(a["L3_attn_proj_b"])},
        "L3_xattn": attn("L3_xattn_", "Wq", "Wk", "Wv", "Wo", "bq", "bk", "bv", "bo", False),
        "L3_ffn": {"w1": tiles(a["L3_ffn_w1"]), "w2": a["L3_ffn_w2"],
                   "b1": columns(a["L3_ffn_b1"]), "b2": columns(a["L3_ffn_b2"])},
    }
    layout, packed = {}, {}
    for name, part in parts.items():
        at, layout[name] = 0, {}
        for key, m in part.items():
            layout[name][key] = (at, m.shape[1])
            at += m.shape[1]
        layout[name]["_width"] = at
        packed[name] = np.ascontiguousarray(np.concatenate(list(part.values()), axis=1))
    return layout, packed


def kernel(**inputs):
    import concourse.bacc as _bacc
    from concourse.bass_utils import run_bass_kernel_spmd as _run

    a = {n: np.asarray(m) for n, m in inputs.items()}
    layout, packed = pack(a)
    nc = _bacc.Bacc("TRN2", target_bir_lowering=False, num_devices=1)
    arrays = {
        "x": a["x"].reshape(SEQS * SEQ, D),
        "ctxT": np.ascontiguousarray(a["ctx_1024"].reshape(SEQS * SEQ, D).T),
        "boundary": a["mask_BxS_ik0"].reshape(1, SEQS * SEQ),
        "mask": np.ascontiguousarray(a["mask_Bx1xSxS2_ff0"].reshape(SEQS, 2, P, 2 * P).transpose(2, 0, 1, 3)
                                      .reshape(P, -1)),
    }
    for name in ["const"] + [SUBLAYERS[k] for k in KS]:
        arrays["packed_" + name] = packed[name]
    dram = {n: nc.dram_tensor("in_" + n, m.shape, mybir.dt.from_np(m.dtype), kind="ExternalInput").ap()
            for n, m in arrays.items()}
    out = nc.dram_tensor("out_0", (SEQS * SEQ, D), F32, kind="ExternalOutput").ap()
    decoder(nc, dram["x"], dram["ctxT"], dram["boundary"], dram["mask"],
            {n[7:]: ap for n, ap in dram.items() if n.startswith("packed_")}, layout, out, KS)
    r = _run(nc, [{"in_" + n: m for n, m in arrays.items()}], core_ids=[0])
    return r.results[0]["out_0"].reshape(SEQS, SEQ, D)
```
